# Optimizing a Trainium2 kernel written in Bass

```python
import numpy as np
import jax
import jax.numpy as jnp

def _softmax(x, axis=-1):
    return jax.nn.softmax(x, axis=axis)

def _gelu(x):
    return jax.nn.gelu(x, approximate=True)

def _silu(x):
    return jax.nn.silu(x)

def _sigmoid(x):
    return jax.nn.sigmoid(x)

def _layernorm(x, axis=-1, eps=1e-05):
    m = jnp.mean(x, axis=axis, keepdims=True)
    v = jnp.var(x, axis=axis, keepdims=True)
    return (x - m) / jnp.sqrt(v + eps)

def _scatter_add(tgt, idx, src, axis=0):
    return tgt.at[idx].add(src)

def _segment_sum(src, seg, n):
    return jax.ops.segment_sum(src, seg, n)
kernel_name = 'mk_perceiver_d1_seqx_r4_843d24'

def setup_inputs(seed: int=0):
    np.random.seed(seed)
    _w = jnp.asarray

    def _rec_inputs():
        import jax
        import jax.numpy as jnp
        _rk = jax.random.key(seed)
        x = -0.0002928 + 1 * jax.random.normal(jax.random.fold_in(_rk, 1), (32, 64, 256), jnp.float32)
        _lenS = 64 - jax.random.randint(jax.random.fold_in(_rk, 7), (32,), 0, max(1, 64 // 4) + 1, jnp.int32)
        _lenS2 = 1601 - jax.random.randint(jax.random.fold_in(_rk, 8), (32,), 0, max(1, 1601 // 4) + 1, jnp.int32)
        _ctx_768P = jax.random.normal(jax.random.fold_in(_rk, 11), (32, 16, 192), jnp.float32)
        _ctx_768c = jax.random.dirichlet(jax.random.fold_in(_rk, 511), 0.3 * jnp.ones((16,), jnp.float32), (32, 1601))
        _ctx_768t = jnp.einsum('bsk,bkd->bsd', _ctx_768c, _ctx_768P)
        _ctx_768t = _ctx_768t * jax.lax.rsqrt(jnp.mean(jnp.square(_ctx_768t)) + 1e-12) * 0.953939
        ctx_768 = 2.09791e-05 + 1.00001 * (_ctx_768t + 0.3 * jax.random.normal(jax.random.fold_in(_rk, 611), (32, 1601, 192), jnp.float32))
        return (x, ctx_768)
    x, ctx_768 = _rec_inputs()

    def _L0_xattn_setup():
        import jax, jax.numpy as jnp
        import numpy as np
        B, LQ, LKV = (2, 512, 512)
        C, CTX, H, DK = (256, 192, 16, 64)
        SCALE = DK ** (-0.5)
        key = jax.random.key(seed)
        kx, ky, kq, kkv, kp, kb = jax.random.split(key, 6)
        return {'x': jax.random.normal(kx, (B, LQ, C), dtype=jnp.float32), 'y': jax.random.normal(ky, (B, LKV, CTX), dtype=jnp.float32), 'Wq': jax.random.normal(kq, (C, H * DK), dtype=jnp.float32) * C ** (-0.5), 'Wkv': jax.random.normal(kkv, (CTX, 2 * H * DK), dtype=jnp.float32) * CTX ** (-0.5), 'Wproj': jax.random.normal(kp, (H * DK, C), dtype=jnp.float32) * (H * DK) ** (-0.5), 'bproj': jax.random.normal(kb, (C,), dtype=jnp.float32) * 0.01}
    _L0_xattn_all = _L0_xattn_setup()
    _L0_xattn_in = {k: v for k, v in _L0_xattn_all.items() if k in ('Wq', 'Wkv', 'Wproj', 'bproj')}
    del _L0_xattn_all

    def _L0_attn_setup():
        import jax, jax.numpy as jnp
        import numpy as np
        D_MODEL = 256
        D_STATE = 16
        D_CONV = 4
        EXPAND = 2
        D_INNER = EXPAND * D_MODEL
        DT_MIN, DT_MAX = (0.001, 0.1)
        BATCH, SEQ = (4, 512)

        def _silu(v):
            return v * jax.nn.sigmoid(v)
        key = jax.random.key(seed)
        ks = jax.random.split(key, 5)
        x = jax.random.normal(ks[0], (BATCH, SEQ, D_MODEL), jnp.float32)
        W_in = jax.random.normal(ks[1], (2 * D_INNER, D_MODEL), jnp.float32) / np.sqrt(D_MODEL)
        conv_w = jax.random.normal(ks[2], (D_INNER, D_CONV), jnp.float32) / np.sqrt(D_CONV)
        conv_b = jnp.zeros((D_INNER,), jnp.float32)
        W_xproj = jax.random.normal(ks[3], (2 * D_STATE + 1, D_INNER), jnp.float32) / np.sqrt(D_INNER)
        A_log = jnp.log(jnp.arange(1, D_STATE + 1, dtype=jnp.float32))
        D_param = jnp.ones((D_INNER,), jnp.float32)
        W_out = jax.random.normal(ks[4], (D_MODEL, D_INNER), jnp.float32) / np.sqrt(D_INNER)
        return dict(x=x, W_in=W_in, conv_w=conv_w, conv_b=conv_b, W_xproj=W_xproj, A_log=A_log, D_param=D_param, W_out=W_out)
    _L0_attn_all = _L0_attn_setup()
    _L0_attn_in = {k: v for k, v in _L0_attn_all.items() if k in ('W_in', 'conv_w', 'conv_b', 'W_xproj', 'A_log', 'D_param', 'W_out')}
    del _L0_attn_all

    def _L0_ffn_setup():
        import jax, jax.numpy as jnp
        import numpy as np
        H = 256
        DFF = 1024
        E = 8
        B = 8
        S = 128
        INIT_LAMBDA = 0.2
        key = jax.random.key(seed)
        ks = jax.random.split(key, 9)
        hidden_states = jax.random.normal(ks[0], (S, B, H), dtype=jnp.float32)
        gW1 = 0.01 * jax.random.normal(ks[1], (H, H), dtype=jnp.float32)
        gb1 = jnp.zeros((H,), dtype=jnp.float32)
        gW2 = 0.01 * jax.random.normal(ks[2], (E, H), dtype=jnp.float32)
        gb2 = jnp.full((E,), INIT_LAMBDA, dtype=jnp.float32)
        sc1 = 1.0 / np.sqrt(H)
        sc2 = 1.0 / np.sqrt(DFF)
        eW1 = sc1 * jax.random.normal(ks[3], (E, DFF, H), dtype=jnp.float32)
        eb1 = sc1 * jax.random.normal(ks[4], (E, DFF), dtype=jnp.float32)
        eW2 = sc2 * jax.random.normal(ks[5], (E, H, DFF), dtype=jnp.float32)
        eb2 = sc2 * jax.random.normal(ks[6], (E, H), dtype=jnp.float32)
        return {'hidden_states': hidden_states, 'gW1': gW1, 'gb1': gb1, 'gW2': gW2, 'gb2': gb2, 'eW1': eW1, 'eb1': eb1, 'eW2': eW2, 'eb2': eb2}
    _L0_ffn_all = _L0_ffn_setup()
    _L0_ffn_in = {k: v for k, v in _L0_ffn_all.items() if k in ('gW1', 'gb1', 'gW2', 'gb2', 'eW1', 'eb1', 'eW2', 'eb2')}
    del _L0_ffn_all
    return {'x': x, 'ctx_768': ctx_768, 'L0_xattn_Wq': _L0_xattn_in['Wq'], 'L0_xattn_Wkv': _L0_xattn_in['Wkv'], 'L0_xattn_Wproj': _L0_xattn_in['Wproj'], 'L0_xattn_bproj': _L0_xattn_in['bproj'], 'L0_attn_W_in': _L0_attn_in['W_in'], 'L0_attn_conv_w': _L0_attn_in['conv_w'], 'L0_attn_conv_b': _L0_attn_in['conv_b'], 'L0_attn_W_xproj': _L0_attn_in['W_xproj'], 'L0_attn_A_log': _L0_attn_in['A_log'], 'L0_attn_D_param': _L0_attn_in['D_param'], 'L0_attn_W_out': _L0_attn_in['W_out'], 'L0_ffn_gW1': _L0_ffn_in['gW1'], 'L0_ffn_gb1': _L0_ffn_in['gb1'], 'L0_ffn_gW2': _L0_ffn_in['gW2'], 'L0_ffn_gb2': _L0_ffn_in['gb2'], 'L0_ffn_eW1': _L0_ffn_in['eW1'], 'L0_ffn_eb1': _L0_ffn_in['eb1'], 'L0_ffn_eW2': _L0_ffn_in['eW2'], 'L0_ffn_eb2': _L0_ffn_in['eb2']}

def reference(x, ctx_768, L0_xattn_Wq, L0_xattn_Wkv, L0_xattn_Wproj, L0_xattn_bproj, L0_attn_W_in, L0_attn_conv_w, L0_attn_conv_b, L0_attn_W_xproj, L0_attn_A_log, L0_attn_D_param, L0_attn_W_out, L0_ffn_gW1, L0_ffn_gb1, L0_ffn_gW2, L0_ffn_gb2, L0_ffn_eW1, L0_ffn_eb1, L0_ffn_eW2, L0_ffn_eb2):
    import jax
    import jax.numpy as jnp

    def _L0_xattn_ref(x, y, Wq, Wkv, Wproj, bproj):
        import jax, jax.numpy as jnp
        import numpy as np
        B, LQ, LKV = (2, 512, 512)
        C, CTX, H, DK = (256, 192, 16, 64)
        SCALE = DK ** (-0.5)
        b, lq, _ = x.shape
        lkv = y.shape[1]
        q = (x @ Wq).reshape(b, lq, H, DK).transpose(0, 2, 1, 3)
        kv = (y @ Wkv).reshape(b, lkv, 2, H, DK).transpose(2, 0, 3, 1, 4)
        k, v = (kv[0], kv[1])
        atten = jax.nn.softmax(jnp.einsum('bhid,bhjd->bhij', q, k) * SCALE, axis=-1)
        res = jnp.einsum('bhij,bhjd->bhid', atten, v)
        res = res.transpose(0, 2, 1, 3).reshape(b, lq, H * DK)
        out = res @ Wproj + bproj
        return out

    def _L0_attn_ref(x, W_in, conv_w, conv_b, W_xproj, A_log, D_param, W_out):
        import jax, jax.numpy as jnp
        import numpy as np
        D_MODEL = 256
        D_STATE = 16
        D_CONV = 4
        EXPAND = 2
        D_INNER = EXPAND * D_MODEL
        DT_MIN, DT_MAX = (0.001, 0.1)
        BATCH, SEQ = (4, 512)

        def _silu(v):
            return v * jax.nn.sigmoid(v)
        b, l, d = x.shape
        xz = x @ W_in.T
        x_proj, z = jnp.split(xz, 2, axis=-1)
        xp = jnp.pad(x_proj, ((0, 0), (D_CONV - 1, 0), (0, 0)))
        x_conv = conv_b + sum((xp[:, k:k + l, :] * conv_w[:, k] for k in range(D_CONV)))
        x_conv = _silu(x_conv)
        x_dbl = x_conv @ W_xproj.T
        Bmat = x_dbl[..., :D_STATE]
        Cmat = x_dbl[..., D_STATE:2 * D_STATE]
        dt = jnp.clip(jax.nn.softplus(x_dbl[..., -1]), DT_MIN, DT_MAX)
        A = -jnp.exp(A_log)

        def step(h, inp):
            x_t, dt_t, B_t, C_t = inp
            dt_A = jnp.clip(dt_t[:, None] * A, -20.0, 0.0)
            A_bar = jnp.exp(dt_A)[:, None, :]
            B_bar = jnp.clip(dt_t[:, None] * B_t, -10.0, 10.0)[:, None, :]
            h = jnp.clip(A_bar * h + B_bar * x_t[:, :, None], -100.0, 100.0)
            y_t = jnp.einsum('bds,bs->bd', h, C_t)
            return (h, y_t)
        h0 = jnp.zeros((b, D_INNER, D_STATE), x.dtype)
        xs = (jnp.swapaxes(x_conv, 0, 1), jnp.swapaxes(dt, 0, 1), jnp.swapaxes(Bmat, 0, 1), jnp.swapaxes(Cmat, 0, 1))
        _, ys = jax.lax.scan(step, h0, xs)
        y = jnp.swapaxes(ys, 0, 1)
        y = y * _silu(z) + x_conv * D_param
        return y @ W_out.T

    def _L0_ffn_ref(hidden_states, gW1, gb1, gW2, gb2, eW1, eb1, eW2, eb2):
        import jax, jax.numpy as jnp
        import numpy as np
        H = 256
        DFF = 1024
        E = 8
        B = 8
        S = 128
        INIT_LAMBDA = 0.2
        x = jnp.transpose(hidden_states, (1, 0, 2))
        h = jax.nn.relu(jnp.einsum('bsh,oh->bso', x, gW1) + gb1)
        gate = jnp.einsum('bsh,eh->bse', h, gW2) + gb2
        g = gate.mean(axis=1)
        W1 = jnp.einsum('be,eoi->boi', g, eW1)
        b1 = g @ eb1
        W2 = jnp.einsum('be,eoi->boi', g, eW2)
        b2 = g @ eb2
        y = jax.nn.relu(jnp.einsum('bsi,boi->bso', x, W1) + b1[:, None, :])
        y = jnp.einsum('bsi,boi->bso', y, W2) + b2[:, None, :]
        return jnp.transpose(y, (1, 0, 2))
    x = x + _L0_xattn_ref(_layernorm(x, axis=-1), ctx_768, L0_xattn_Wq, L0_xattn_Wkv, L0_xattn_Wproj, L0_xattn_bproj)
    x = x + _L0_attn_ref(_layernorm(x, axis=-1), L0_attn_W_in, L0_attn_conv_w, L0_attn_conv_b, L0_attn_W_xproj, L0_attn_A_log, L0_attn_D_param, L0_attn_W_out)
    x = x + _L0_ffn_ref(_layernorm(x, axis=-1), L0_ffn_gW1, L0_ffn_gb1, L0_ffn_gW2, L0_ffn_gb2, L0_ffn_eW1, L0_ffn_eb1, L0_ffn_eW2, L0_ffn_eb2)
    return x

_drawn_inputs = setup_inputs


def setup_inputs(seed=0):
    import zlib

    import numpy as np

    out = dict(_drawn_inputs(seed))
    spreads = {'L0_attn_conv_b': (0.0, 0.1),
     'L0_attn_D_param': (1.0, 0.2),
     'L0_ffn_gb1': (0.0, 0.8),
     'L0_ffn_gb2': (0.20000000298023224, 0.2)}
    factors = {'L0_xattn_bproj': 5.882,
     'L0_ffn_gW1': 8.0,
     'L0_ffn_gW2': 3.131,
     'L0_ffn_eb1': 5.7,
     'L0_ffn_eb2': 4.317}
    for name, (base, spread) in spreads.items():
        noise = np.random.default_rng([zlib.crc32(name.encode()), seed]).standard_normal(out[name].shape)
        drawn = base * np.exp(spread * noise) if base else spread * noise
        out[name] = jnp.asarray(drawn.astype(out[name].dtype))
    for name, factor in factors.items():
        out[name] = (out[name] * factor).astype(out[name].dtype)
    return out
```

```python
from contextlib import ExitStack

import numpy as np
import concourse.bass as bass
from concourse import mybir

F32 = mybir.dt.float32
F16 = mybir.dt.float16
ALU = mybir.AluOpType
ACT = mybir.ActivationFunctionType
AX_X = mybir.AxisListType.X

P = 128
B, T, C = 32, 64, 256
J, CTX = 1601, 192
H, DK = 16, 64
HP = H // 2
PAIR_TOK = 2 * T
NPAIR = B // 2
JT = J // P
JR = J - JT * P
JN = JT + 1
C1 = CTX - P
SCALE = DK ** -0.5
EPS = 1e-5

DI, DS, DC = 512, 16, 4
KD = DI // P
XD = 2 * DS + 1
E, DFF = 8, 1024
FT = DFF // P


def bank(psum, i, n=512):
    return psum[:, 512 * i:512 * i + n]


class LayerNorm:

    def __init__(self, nc, ctx, tag, X, ident, psum, xT, nhalf):
        def sb(name, shape):
            return ctx.enter_context(nc.sbuf_tensor(f"{tag}_{name}", shape, F32))

        def sem(name):
            return ctx.enter_context(nc.semaphore(f"{tag}_{name}"))

        self.X, self.ident, self.psum, self.xT, self.nhalf = X, ident, psum, xT, nhalf
        self.stats = sb("stats", [P, NPAIR, 6])
        self.diff = sb("diff", [P, NPAIR])
        self.var = sb("var", [P, NPAIR])
        self.mean = sb("mean", [P, NPAIR])
        self.rstd = sb("rstd", [P, NPAIR])
        self.xn = sb("xn", [P, NPAIR, C])
        self.stats_done = sem("stats_done")
        self.var_done = sem("var_done")
        self.rstd_done = sem("rstd_done")
        self.centred = sem("centred")
        self.normed = sem("normed")
        self.turned = sem("turned")
        self.kept = sem("kept")

    def vector(self, dve):
        st = self.stats
        with dve.Fori(0, NPAIR) as n:
            dve.bn_stats(st[:, bass.ds(n, 1), :].rearrange("p a s -> p (a s)"),
                         self.X[:, bass.ds(n, 1), :].rearrange("p a c -> p (a c)")).then_inc(self.stats_done, 1)
        dve.wait_ge(self.stats_done, NPAIR)
        dve.tensor_tensor(self.diff[:, :], st[:, :, 1], st[:, :, 4], ALU.subtract).then_inc(self.stats_done, 1)
        dve.tensor_tensor(self.mean[:, :], st[:, :, 1], st[:, :, 4], ALU.add).then_inc(self.stats_done, 1)
        dve.tensor_tensor(self.var[:, :], st[:, :, 2], st[:, :, 5], ALU.add).then_inc(self.stats_done, 1)
        dve.wait_ge(self.stats_done, NPAIR + 1)
        dve.scalar_tensor_tensor(self.rstd[:, :], self.diff[:, :], 0.25, self.diff[:, :], ALU.mult,
                                 ALU.mult).then_inc(self.stats_done, 1)
        dve.wait_ge(self.stats_done, NPAIR + 4)
        dve.tensor_scalar(self.mean[:, :], self.mean[:, :], 0.5, None, ALU.mult).then_inc(self.stats_done, 1)
        dve.scalar_tensor_tensor(self.diff[:, :], self.var[:, :], 1.0 / C, self.rstd[:, :], ALU.mult,
                                 ALU.add).then_inc(self.stats_done, 1)
        dve.wait_ge(self.stats_done, NPAIR + 6)
        dve.tensor_scalar(self.var[:, :], self.diff[:, :], EPS, None, ALU.add).then_inc(self.var_done, 1)
        dve.tensor_tensor(self.xn[:, :, :], self.X[:, :, :],
                          self.mean[:, :][:, :, None].to_broadcast([P, NPAIR, C]),
                          ALU.subtract).then_inc(self.centred, 1)
        dve.wait_ge(self.centred, 1)
        dve.wait_ge(self.rstd_done, 1)
        dve.tensor_tensor(self.xn[:, :, :], self.xn[:, :, :],
                          self.rstd[:, :][:, :, None].to_broadcast([P, NPAIR, C]),
                          ALU.mult).then_inc(self.normed, 1)

    def gpsimd(self, pool):
        pool.wait_ge(self.var_done, 1)
        pool.tensor_tensor(self.rstd[:, :], self.var[:, :], self.nhalf[:, :], ALU.pow).then_inc(self.rstd_done, 1)

    def tensor(self, pe):
        pe.wait_ge(self.normed, 1)
        for g in range(NPAIR // 2):
            if g >= 2:
                pe.wait_ge(self.kept, g - 1)
            for n in range(2):
                for k in range(2):
                    ins = pe.transpose(bank(self.psum, g % 2)[:, (2 * n + k) * P:(2 * n + k + 1) * P],
                                       self.xn[:, 2 * g + n, k * P:(k + 1) * P], self.ident[:, :])
            ins.then_inc(self.turned, 1)

    def scalar(self, act):
        for g in range(NPAIR // 2):
            act.wait_ge(self.turned, g + 1)
            act.activation(self.xT[:, :, 2 * g * P:(2 * g + 2) * P].rearrange("p k (n t) -> p k n t", n=2),
                           bank(self.psum, g % 2).rearrange("p (n k t) -> p k n t", n=2, k=2),
                           ACT.Copy).then_inc(self.kept, 1)


def build(nc, a, out):
    with ExitStack() as top:
        def sem(name):
            return top.enter_context(nc.semaphore(name))

        def tensor_in(ctx):
            def sb(name, shape, dt=F32):
                return ctx.enter_context(nc.sbuf_tensor(name, shape, dt))
            return sb

        sb = tensor_in(top)
        psum = top.enter_context(nc.psum_tensor("psum", [P, 8 * 512], F32))
        X = sb("X", [P, NPAIR, C])
        ident = sb("ident", [P, P])
        nhalf = sb("nhalf", [P, NPAIR])
        xT = sb("xT", [P, 2, B * T + 2 * PAIR_TOK])

        attention(nc, a, sem, tensor_in, psum, X, ident, nhalf, xT)
        state_space(nc, a, sem, tensor_in, psum, X, ident, nhalf, xT)
        experts(nc, a, out, sem, tensor_in, psum, X, ident, nhalf, xT)


def attention(nc, a, sem, tensor_in, psum, X, ident, nhalf, xT):
    with ExitStack() as ctx:
        sb = tensor_in(ctx)
        Wq = sb("Wq", [P, 2, H * DK])
        WkS = sb("WkS", [P, HP, 2, 2 * P])
        Wvp = sb("Wvp", [P, 3 * HP, C])

        with ExitStack() as cs:
            sbs = tensor_in(cs)
            WvS = sbs("WvS", [P, HP, 3, P])
            Wpr = sbs("Wpr", [P, HP, C])
            bpr = sbs("bpr", [P, C])
            x_in, w_in = sem("x_in"), sem("w_in")
            half_set, wvp_done, wvp_kept, bias_in, wrap = (
                sem("half_set"), sem("wvp_done"), sem("wvp_kept"), sem("bias_in"), sem("wrap"))
            ln = LayerNorm(nc, cs, "ln1", X, ident, psum, xT, nhalf)
            block = cs.enter_context(nc.Block())

            @block.sync
            def _(sp):
                sp.dma_start(X[:, :, :], a["x"].rearrange("(n p) c -> p n c", p=P)).then_inc(x_in, 16)
                sp.dma_start(ident[:, :], a["ident"]).then_inc(x_in, 16)
                sp.dma_start(bpr[:, :], a["bproj"].partition_broadcast(P)).then_inc(bias_in, 16)
                sp.dma_start(WvS[:, :, :, :], a["WvS"]).then_inc(w_in, 16)
                sp.dma_start(Wpr[:, :, :], a["Wproj"].rearrange("(g p) n -> p g n", p=P)).then_inc(w_in, 16)
                sp.dma_start(Wq[:, :, :], a["Wq"].rearrange("(k p) n -> p k n", p=P)).then_inc(w_in, 16)
                sp.dma_start(WkS[:, :, :, :], a["WkS"]).then_inc(w_in, 16)
                sp.wait_ge(w_in, 64)

            @block.vector
            def _(dve):
                dve.memset(nhalf[:, :], -0.5).then_inc(half_set, 1)
                dve.wait_ge(x_in, 32)
                ln.vector(dve)
                dve.wait_ge(bias_in, 16)
                dve.wait_ge(ln.normed, 1)
                dve.tensor_tensor(X[:, :, :], X[:, :, :], bpr[:, :][:, None, :].to_broadcast([P, NPAIR, C]), ALU.add)

            @block.gpsimd
            def _(pool):
                pool.wait_ge(half_set, 1)
                ln.gpsimd(pool)
                pool.wait_ge(ln.kept, 1)
                pool.tensor_copy(xT[:, :, B * T:B * T + PAIR_TOK], xT[:, :, 0:PAIR_TOK]).then_inc(wrap, 1)

            @block.tensor
            def _(pe):
                pe.wait_ge(x_in, 32)
                ln.tensor(pe)
                pe.wait_ge(w_in, 64)
                for g in range(HP):
                    for s in range(3):
                        n = 3 * g + s
                        if n >= 2:
                            pe.wait_ge(wvp_kept, n - 1)
                        pe.matmul(bank(psum, 2 + n % 2, C), WvS[:, g, s, :], Wpr[:, g, :],
                                  start=True, stop=True).then_inc(wvp_done, 1)

            @block.scalar
            def _(act):
                ln.scalar(act)
                for g in range(HP):
                    for s in range(3):
                        n = 3 * g + s
                        act.wait_ge(wvp_done, n + 1)
                        act.activation(Wvp[:, 2 * g + s if s < 2 else H + g, :], bank(psum, 2 + n % 2, C),
                                       ACT.Copy).then_inc(wvp_kept, 1)

        qT = sb("qT", [P, HP, PAIR_TOK])
        Q = [sb(f"Q{i}", [P, 4, 2, H * T], F16) for i in range(2)]
        yN = [sb(f"yN{i}", [P, JN, 2 * CTX], F16) for i in range(2)]
        yT = [sb(f"yT{i}", [P, 3, J], F16) for i in range(2)]
        stage = [sb(f"stage{i}", [P, J]) for i in range(2)]
        prob = sb("prob", [P, J])
        pT = [sb(f"pT{i}", [P, JN, P], F16) for i in range(2)]
        On = sb("On", [P, 2 * P])
        Olo = sb("Olo", [P, CTX])
        OT = sb("OT", [P, 3 * HP, PAIR_TOK])
        mx = sb("mx", [P, 4])
        nb = sb("nb", [P, 2])
        den = sb("den", [P, 2])
        rden = sb("rden", [P, 2])
        psS = psum[:, 0:2048]
        psT = [bank(psum, 4), bank(psum, 5)]
        psO = bank(psum, 6)
        psM = bank(psum, 7)
        psP = psum[:, 1536:1536 + C]

        loaded = [sem("loaded0"), sem("loaded1")]
        stage_free = [sem("stage0_free"), sem("stage1_free")]
        hi_cut = sem("hi_cut")
        ctx_ready = sem("ctx_ready")
        scored = sem("scored")
        maxed = sem("maxed")
        biased = sem("biased")
        expd = sem("expd")
        recip = sem("recip")
        turned = sem("turned")
        hi_kept = sem("hi_kept")
        lo_kept = sem("lo_kept")
        summed = sem("summed")
        olo_kept = sem("olo_kept")
        normed = sem("normed")
        o_turned = sem("o_turned")
        o_kept = sem("o_kept")
        q_done = sem("q_done")
        q_kept = sem("q_kept")
        qk_done = sem("qk_done")
        qk_hi = sem("qk_hi")
        qk_lo = sem("qk_lo")
        projected = sem("projected")
        x_added = sem("x_added")
        AHEAD, LO_AHEAD, CTX_AHEAD = 16, 4, 2
        GROUPS = [(0, 4), (4, 8), (8, 12), (12, 13)]
        block = ctx.enter_context(nc.Block())

        def per_pair(i, u, n, k):
            return i * (2 * n) + (u * n + k)

        @block.sync
        def _(sp):
            with sp.Fori(0, NPAIR // 2) as i:
                for u in range(2):
                    for b in range(2):
                        be = i * 4 + (2 * u + b)
                        n = 2 * (2 * u + b)
                        yt = a["ctxT"][bass.ds(be, 1)].rearrange("a c j -> (a c) j")
                        yn = a["ctxN"][bass.ds(be, 1)].rearrange("a p m c -> (a p) m c")
                        yr = a["ctxR"][bass.ds(be, 1)].rearrange("a p c -> (a p) c")
                        half = 7 * CTX
                        sp.wait_ge(stage_free[0], i * 8 + (n + 1))
                        sp.dma_start(stage[0][:, :], yt[0:P, :]).then_inc(loaded[0], 16)
                        sp.wait_ge(ctx_ready, i * 8 + (n + CTX_AHEAD))
                        sp.dma_start(stage[1][0:C1, :], yt[P:CTX, :]).then_inc(loaded[1], 16)
                        sp.dma_start(stage[1][C1:P, :], yt[P:CTX, :]).then_inc(loaded[1], 16)
                        sp.wait_ge(stage_free[0], i * 8 + (n + 2))
                        sp.dma_start(stage[0][:, 0:half].rearrange("p (m c) -> p m c", c=CTX),
                                     yn[:, 0:7, :]).then_inc(loaded[0], 16)
                        sp.wait_ge(stage_free[1], i * 4 + (n // 2 + 1))
                        sp.dma_start(stage[1][:, 0:5 * CTX].rearrange("p (m c) -> p m c", c=CTX),
                                     yn[:, 7:12, :]).then_inc(loaded[1], 16)
                        sp.dma_start(stage[1][0:JR, 5 * CTX:6 * CTX], yr).then_inc(loaded[1], 16)

        @block.gpsimd
        def _(pool):
            pool.sem_inc(stage_free[0], 1)
            pool.sem_inc(ctx_ready, CTX_AHEAD)
            with pool.Fori(0, NPAIR // 2) as i:
                for u in range(2):
                    for b in range(2):
                        n = 2 * u + b
                        s0, s1, N_, T_ = stage[0], stage[1], yN[b], yT[b]
                        pool.wait_ge(normed, i * 32 + (AHEAD + (n - 1) * HP))
                        pool.wait_ge(loaded[0], i * 128 + (32 * n + 16))
                        pool.nop(nofuse=True)
                        pool.tensor_copy(T_[:, 0, :], s0[:, :]).then_inc(hi_cut, 1)
                        pool.wait_ge(hi_cut, i * 20 + (5 * n + 1))
                        pool.tensor_tensor(T_[:, 2, :], s0[:, :], T_[:, 0, :], ALU.subtract)\
                            .then_inc(stage_free[0], 1)
                        pool.wait_ge(loaded[1], i * 256 + (64 * n + 32))
                        pool.nop(nofuse=True)
                        pool.tensor_copy(T_[:, 1, :], s1[:, :]).then_inc(hi_cut, 1)
                        pool.wait_ge(hi_cut, i * 20 + (5 * n + 2))
                        pool.tensor_tensor(T_[0:C1, 1, :], s1[0:C1, :], T_[0:C1, 1, :], ALU.subtract)\
                            .then_inc(stage_free[1], 1)
                        v0 = s0[:, 0:7 * CTX].rearrange("p (m c) -> p m c", c=CTX)
                        pool.wait_ge(loaded[0], i * 128 + (32 * n + 32))
                        pool.nop(nofuse=True)
                        pool.tensor_copy(N_[:, 0:7, 0:CTX], v0).then_inc(hi_cut, 1)
                        pool.wait_ge(hi_cut, i * 20 + (5 * n + 3))
                        pool.tensor_tensor(N_[:, 0:7, CTX:], v0, N_[:, 0:7, 0:CTX], ALU.subtract)\
                            .then_inc(stage_free[0], 1)
                        v1 = s1[:, 0:5 * CTX].rearrange("p (m c) -> p m c", c=CTX)
                        vr = s1[0:JR, 5 * CTX:6 * CTX]
                        pool.wait_ge(loaded[1], i * 256 + (64 * n + 64))
                        pool.nop(nofuse=True)
                        pool.tensor_copy(N_[:, 7:12, 0:CTX], v1).then_inc(hi_cut, 1)
                        pool.tensor_copy(N_[0:JR, 12, 0:CTX], vr).then_inc(hi_cut, 1)
                        pool.wait_ge(hi_cut, i * 20 + (5 * n + 5))
                        pool.tensor_tensor(N_[:, 7:12, CTX:], v1, N_[:, 7:12, 0:CTX], ALU.subtract)\
                            .then_inc(ctx_ready, 1)
                        pool.tensor_tensor(N_[0:JR, 12, CTX:], vr, N_[0:JR, 12, 0:CTX], ALU.subtract)\
                            .then_inc(ctx_ready, 1)

        @block.tensor
        def _(pe):
            def q_half(pair, half, misc_free):
                misc_free()
                for g in range(4):
                    for k in range(2):
                        ins = pe.matmul(psM[:, g * P:(g + 1) * P],
                                        Wq[:, k, (4 * half + g) * P:(4 * half + g + 1) * P],
                                        xT[:, k, bass.ds(pair * PAIR_TOK, PAIR_TOK)]
                                        if not isinstance(pair, int) else
                                        xT[:, k, pair * PAIR_TOK:(pair + 1) * PAIR_TOK],
                                        start=(k == 0), stop=(k == 1))
                ins.then_inc(q_done, 1)

            def qk_group(g, misc_free):
                misc_free()
                for c in range(2):
                    for h2 in range(2):
                        ins = pe.matmul(psM[:, (2 * c + h2) * P:(2 * c + h2 + 1) * P],
                                        WkS[:, g, h2, c * P:(c + 1) * P], qT[:, g, :], start=True, stop=True)
                ins.then_inc(qk_done, 1)

            def wait_for(s, v):
                return lambda: pe.wait_ge(s, v)

            q_half(0, 0, lambda: None)
            q_half(0, 1, wait_for(q_kept, 1))
            pe.wait_ge(q_kept, 2)
            for g in range(HP):
                qk_group(g, wait_for(qk_lo, g) if g else (lambda: None))

            with pe.Fori(0, NPAIR // 2) as i:
                for u in range(2):
                    nxt = i * 2 + (u + 1)

                    def at(n, k, u=u, i=i):
                        return per_pair(i, u, n, k)

                    def score(t, chunks, u=u, at=at):
                        b, tt = divmod(t, HP)
                        if 0 in chunks:
                            if tt == 0:
                                pe.wait_ge(ctx_ready, at(4, 2 * b + 2) + CTX_AHEAD)
                            if t == 0:
                                pe.wait_ge(qk_lo, at(8, 8))
                            if t > 0:
                                pe.wait_ge(expd, at(16, t))
                        for c in chunks:
                            lo, hi = 512 * c, min(J, 512 * (c + 1))
                            if t == 0 and c == 3:
                                pe.wait_ge(x_added, at(1, 1))
                            for n, (q, y) in enumerate([(0, 0), (1, 1), (0, 2), (2, 0), (3, 1)]):
                                ins = pe.matmul(psS[:, lo:hi], Q[u][:, q, b, tt * P:(tt + 1) * P],
                                                yT[b][:, y, lo:hi], start=(n == 0), stop=(n == 4))
                            if c in (1, 3):
                                ins.then_inc(scored, 1)

                    def turn(t, g, at=at):
                        if g == 0:
                            pe.wait_ge(expd, at(16, t + 1))
                        pe.wait_ge(lo_kept, at(64, 4 * t + g - 1) + LO_AHEAD)
                        lo, hi = GROUPS[g]
                        for n in range(lo, hi):
                            w = P if n < JT else JR
                            ins = pe.transpose(psT[g % 2][0:w, (n - lo) * P:(n - lo + 1) * P],
                                               prob[:, n * P:n * P + w], ident[:, :])
                        ins.then_inc(turned, 1)

                    def gather(t, at=at):
                        b = t // HP
                        pe.wait_ge(normed, at(16, t) + AHEAD)
                        for n in range(JN):
                            k = P if n < JT else JR
                            if n % 4 == 0:
                                pe.wait_ge(lo_kept, at(64, 4 * t + n // 4 + 1) + LO_AHEAD)
                            pe.matmul(psO[:, 0:2 * CTX], pT[0][0:k, n, :], yN[b][0:k, n, :],
                                      start=(n == 0), stop=False)
                            ins = pe.matmul(psO[:, 0:CTX], pT[1][0:k, n, :], yN[b][0:k, n, 0:CTX],
                                            start=False, stop=(n == JN - 1))
                        ins.then_inc(summed, 1)

                    def turn_o(t, misc_free, at=at):
                        pe.wait_ge(normed, at(16, t + 1) + AHEAD)
                        misc_free()
                        for k in range(2):
                            ins = pe.transpose(psM[:, k * P:(k + 1) * P], On[:, k * P:(k + 1) * P], ident[:, :])
                        ins.then_inc(o_turned, 1)

                    def project(chunks, first=False, last=False):
                        for n, k in enumerate(chunks):
                            ins = pe.matmul(psP, OT[:, k, :], Wvp[:, k, :],
                                            start=(first and n == 0), stop=(last and n == len(chunks) - 1))
                        if last:
                            ins.then_inc(projected, 1)

                    def o_free(t, at=at):
                        return wait_for(o_kept, at(16, t) + AHEAD)

                    def qk_free(n, at=at):
                        return wait_for(qk_lo, at(8, n) + 8)

                    def q_free(n, at=at):
                        return wait_for(q_kept, at(2, n) + 2)

                    score(0, [0, 1, 2, 3])
                    q_half(nxt, 0, o_free(0))
                    for t in range(1, 16):
                        turn(t - 1, 0)
                        turn(t - 1, 1)
                        score(t, [0])
                        turn(t - 1, 2)
                        score(t, [1])
                        turn(t - 1, 3)
                        score(t, [2, 3])
                        if t >= 2:
                            turn_o(t - 2, q_free(2) if t == 2 else qk_free(t - 2) if t <= 9 else o_free(t - 2))
                        gather(t - 1)
                        if t == 1:
                            q_half(nxt, 1, q_free(1))
                        elif t <= 8:
                            qk_group(t - 2, o_free(t - 1))
                    for g in range(4):
                        turn(15, g)
                    qk_group(7, o_free(14))
                    gather(15)
                    turn_o(14, qk_free(8))
                    pe.wait_ge(o_kept, at(16, 15) + AHEAD)
                    pe.wait_ge(expd, at(16, 16))
                    project(range(0, 12), first=True)
                    turn_o(15, lambda: None)
                    project([12, 13] + list(range(16, 23)))
                    pe.wait_ge(o_kept, at(16, 16) + AHEAD)
                    project([14, 15, 23], last=True)

        @block.scalar
        def _(act):
            act.sem_inc(o_kept, AHEAD)

            def q_copy(half, v):
                act.wait_ge(q_done, v)
                act.activation(qT[:, 4 * half:4 * half + 4, :], psM.rearrange("p (g t) -> p g t", g=4),
                               ACT.Copy).then_inc(q_kept, 1)

            def qk_high(g, dst, v):
                act.wait_ge(qk_done, v)
                for c in range(2):
                    ins = act.activation(dst[:, c, :, 2 * g * T:(2 * g + 2) * T].rearrange("p b (h t) -> p h b t", h=2),
                                         psM[:, 2 * c * P:(2 * c + 2) * P].rearrange("p (h b t) -> p h b t", h=2, b=2),
                                         ACT.Copy)
                ins.then_inc(qk_hi, 1)

            q_copy(0, 1)
            q_copy(1, 2)
            for g in range(HP):
                qk_high(g, Q[0], g + 1)

            with act.Fori(0, NPAIR // 2) as i:
                for u in range(2):
                    def at(n, k, u=u, i=i):
                        return per_pair(i, u, n, k)

                    def exponentials(t, at=at):
                        act.wait_ge(biased, at(16, t + 1))
                        act.activation(prob[:, :], psS[:, 0:J], ACT.Exp, bias=nb[:, t % 2:t % 2 + 1], scale=SCALE,
                                       accum_out=den[:, t % 2:t % 2 + 1]).then_inc(expd, 1)

                    def high(t, at=at):
                        for g, (lo, hi) in enumerate(GROUPS):
                            act.wait_ge(turned, at(64, 4 * t + g + 1))
                            w = P if g < 3 else JR
                            act.activation(pT[0][0:w, lo:hi, :],
                                           psT[g % 2][0:w, 0:(hi - lo) * P].rearrange("p (n h) -> p n h", h=P),
                                           ACT.Copy).then_inc(hi_kept, 1)

                    def sum_low(t, at=at):
                        act.wait_ge(summed, at(16, t + 1))
                        act.wait_ge(recip, at(16, t + 1))
                        act.activation(Olo[:, :], psO[:, CTX:2 * CTX], ACT.Copy,
                                       scale=rden[:, t % 2:t % 2 + 1]).then_inc(olo_kept, 1)

                    def o_copy(t, at=at):
                        b, tt = divmod(t, HP)
                        act.wait_ge(o_turned, at(16, t + 1))
                        if t == 0:
                            act.wait_ge(x_added, at(1, 1))
                        tok = slice(b * T, (b + 1) * T)
                        act.activation(OT[:, 2 * tt:2 * tt + 2, tok], psM[:, 0:P].rearrange("p (h t) -> p h t", h=2),
                                       ACT.Copy)
                        act.activation(OT[0:C1, H + tt, tok], psM[0:C1, P:P + T], ACT.Copy)
                        act.activation(OT[C1:P, H + tt, tok], psM[C1:P, P + T:2 * P], ACT.Copy).then_inc(o_kept, 1)

                    exponentials(0)
                    q_copy(0, at(2, 1) + 2)
                    for t in range(1, 16):
                        high(t - 1)
                        if t >= 2:
                            o_copy(t - 2)
                        exponentials(t)
                        sum_low(t - 1)
                        if t == 1:
                            q_copy(1, at(2, 2) + 2)
                        elif t <= 8:
                            qk_high(t - 2, Q[1 - u], at(8, t - 1) + 8)
                    high(15)
                    qk_high(7, Q[1 - u], at(8, 8) + 8)
                    sum_low(15)
                    o_copy(14)
                    o_copy(15)

        @block.vector
        def _(dve):
            dve.sem_inc(normed, AHEAD)
            dve.sem_inc(x_added, 1)
            dve.sem_inc(lo_kept, LO_AHEAD)

            def qk_low(g, dst, v):
                dve.wait_ge(qk_hi, v)
                for c in range(2):
                    hi, lo = (dst[:, s, :, 2 * g * T:(2 * g + 2) * T].rearrange("p b (h t) -> p h b t", h=2)
                              for s in (c, 2 + c))
                    ins = dve.tensor_tensor(lo, psM[:, 2 * c * P:(2 * c + 2) * P].rearrange("p (h b t) -> p h b t", h=2, b=2),
                                            hi, ALU.subtract)
                ins.then_inc(qk_lo, 1)

            for g in range(HP):
                qk_low(g, Q[0], g + 1)

            with dve.Fori(0, NPAIR // 2) as i:
                for u in range(2):
                    pair = i * 2 + u

                    def at(n, k, u=u, i=i):
                        return per_pair(i, u, n, k)

                    def maximum(t, at=at):
                        for n, (lo, hi) in enumerate([(0, 1024), (1024, J)]):
                            dve.wait_ge(scored, at(32, 2 * t + n + 1))
                            dve.tensor_reduce(mx[:, 2 * (t % 2) + n:2 * (t % 2) + n + 1], psS[:, lo:hi], AX_X,
                                              ALU.max).then_inc(maxed, 1)
                        dve.wait_ge(maxed, at(32, 2 * t + 2))
                        m = 2 * (t % 2)
                        dve.tensor_scalar(nb[:, t % 2:t % 2 + 1], mx[:, m:m + 1], mx[:, m + 1:m + 2], -SCALE,
                                          ALU.max, ALU.mult).then_inc(biased, 1)

                    def low(t, at=at):
                        for g, (lo, hi) in enumerate(GROUPS):
                            dve.wait_ge(hi_kept, at(64, 4 * t + g + 1))
                            w = P if g < 3 else JR
                            dve.tensor_tensor(pT[1][0:w, lo:hi, :],
                                              psT[g % 2][0:w, 0:(hi - lo) * P].rearrange("p (n h) -> p n h", h=P),
                                              pT[0][0:w, lo:hi, :], ALU.subtract).then_inc(lo_kept, 1)

                    def reciprocal(t, at=at):
                        dve.wait_ge(expd, at(16, t + 1))
                        dve.reciprocal(rden[:, t % 2:t % 2 + 1], den[:, t % 2:t % 2 + 1]).then_inc(recip, 1)

                    def normalise(t, at=at):
                        dve.wait_ge(olo_kept, at(16, t + 1))
                        if t == 15:
                            dve.wait_ge(o_turned, at(16, 15))
                        r = rden[:, t % 2:t % 2 + 1]
                        dve.scalar_tensor_tensor(On[:, 0:CTX], psO[:, 0:CTX], r, Olo[:, :], ALU.mult, ALU.add)
                        dve.scalar_tensor_tensor(On[:, CTX:2 * P], psO[:, P:CTX], r, Olo[:, P:CTX], ALU.mult,
                                                 ALU.add).then_inc(normed, 1)

                    maximum(0)
                    reciprocal(0)
                    for t in range(1, 16):
                        low(t - 1)
                        maximum(t)
                        reciprocal(t)
                        normalise(t - 1)
                        if 2 <= t <= 8:
                            qk_low(t - 2, Q[1 - u], at(8, t - 1) + 8)
                    low(15)
                    qk_low(7, Q[1 - u], at(8, 8) + 8)
                    normalise(15)
                    dve.wait_ge(projected, at(1, 1))
                    xp = X[:, bass.ds(pair, 1), :].rearrange("p a c -> p (a c)")
                    dve.tensor_tensor(xp, psP, xp, ALU.add).then_inc(x_added, 1)


def norm_phase(nc, tag, sem, tensor_in, psum, X, ident, nhalf, xT):
    with ExitStack() as ctx:
        ln = LayerNorm(nc, ctx, tag, X, ident, psum, xT, nhalf)
        block = ctx.enter_context(nc.Block())

        @block.vector
        def _(dve):
            ln.vector(dve)

        @block.gpsimd
        def _(pool):
            ln.gpsimd(pool)
            pool.wait_ge(ln.kept, 1)
            pool.tensor_copy(xT[:, :, B * T:], xT[:, :, 0:2 * PAIR_TOK]).then_inc(ln.centred, 1)

        @block.tensor
        def _(pe):
            ln.tensor(pe)

        @block.scalar
        def _(act):
            ln.scalar(act)


def state_space(nc, a, sem, tensor_in, psum, X, ident, nhalf, xT):
    norm_phase(nc, "ln2", sem, tensor_in, psum, X, ident, nhalf, xT)
    with ExitStack() as ctx:
        sb = tensor_in(ctx)
        NT = PAIR_TOK
        Win = sb("Win", [P, 2, 2 * DI])
        Wx = sb("Wx", [P, KD, XD])
        Wout = sb("Wout", [P, KD, C])
        cw = sb("cw", [P, KD, DC])
        cb = sb("cb", [P, KD])
        Dp = sb("Dp", [P, KD])
        Alog = sb("Alog", [P, DS])
        negA = sb("negA", [P, DS])
        xpad = sb("xpad", [P, KD, 2, DC - 1 + T])
        xc = sb("xc", [P, KD, NT])
        ex = sb("ex", [P, KD, NT])
        xs = sb("xs", [P, KD, NT])
        zs = sb("zs", [P, KD, NT])
        ez = sb("ez", [P, KD, NT])
        xd = sb("xd", [XD, NT])
        BC = sb("BC", [P, XD, NT])
        dtw = sb("dtw", [P, 6, NT])
        dt = sb("dt", [P, NT])
        dA = sb("dA", [P, NT, DS])
        Bb = sb("Bb", [P, NT, DS])
        U = sb("U", [P, T, 2, KD, DS])
        carry = sb("carry", [P, 2, KD, DS])
        ysum = sb("ysum", [P, T, 2, KD])
        yg = sb("yg", [P, KD, NT])
        y2 = sb("y2", [P, KD, NT])
        scratch = nc.dram_tensor("xdbl_scratch", (XD * NT,), F32, kind="Internal").ap()
        psX, psZ, psD, psY = bank(psum, 0), bank(psum, 1), psum[0:XD, 1024:1024 + NT], bank(psum, 3, C)

        w_in = sem("ss_w_in")
        consts = sem("ss_consts")
        a_ready = sem("a_ready")
        in_done = sem("in_done")
        x_copied = sem("x_copied")
        taps = sem("taps")
        ex_done = sem("ex_done")
        silu = sem("silu")
        xd_done = sem("xd_done")
        xd_kept = sem("xd_kept")
        xd_out = sem("xd_out")
        xd_in = sem("xd_in")
        dt_step = sem("dt_step")
        dt_exp = sem("dt_exp")
        da_exp = sem("da_exp")
        bb_ready = sem("bb_ready")
        u_built = sem("u_built")
        scan = sem("scan")
        hc_done = sem("hc_done")
        y_step = sem("y_step")
        out_done = sem("out_done")
        x2_added = sem("x2_added")
        block = ctx.enter_context(nc.Block())
        SCAN = 3 * T - 1

        @block.sync
        def _(sp):
            sp.dma_start(Win[:, :, :], a["WinT"].rearrange("(k p) n -> p k n", p=P)).then_inc(w_in, 16)
            with nc.allow_non_contiguous_dma(reason="small parameters"):
                sp.dma_start(cw[:, :, :], a["convw"].rearrange("(k p) n -> p k n", p=P)).then_inc(w_in, 16)
                sp.dma_start(cb[:, :], a["convb"].rearrange("(k p) -> p k", p=P)).then_inc(w_in, 16)
                sp.dma_start(Dp[:, :], a["Dp"].rearrange("(k p) -> p k", p=P)).then_inc(w_in, 16)
            sp.dma_start(Alog[:, :], a["A_log"].partition_broadcast(P)).then_inc(w_in, 16)
            sp.dma_start(Wx[:, :, :], a["WxT"].rearrange("(k p) n -> p k n", p=P)).then_inc(w_in, 16)
            sp.dma_start(Wout[:, :, :], a["WoutT"].rearrange("(k p) n -> p k n", p=P)).then_inc(w_in, 16)
            with sp.Fori(0, NPAIR) as i:
                sp.wait_ge(xd_kept, i + 1)
                sp.dma_start(scratch.rearrange("(s n) -> s n", s=XD), xd[:, :]).then_inc(xd_out, 16)
                sp.wait_ge(xd_out, i * 16 + 16)
                sp.dma_start(BC[:, :, :].rearrange("p s n -> p (s n)"), scratch.partition_broadcast(P))\
                    .then_inc(xd_in, 16)

        @block.tensor
        def _(pe):
            pe.wait_ge(w_in, 112)
            with pe.Fori(0, NPAIR) as i:
                pe.wait_ge(x2_added, i + 1)
                for m, ps in ((0, psX), (KD, psZ)):
                    for g in range(KD):
                        for k in range(2):
                            ins = pe.matmul(ps[:, g * P:(g + 1) * P], Win[:, k, (m + g) * P:(m + g + 1) * P],
                                            xT[:, k, bass.ds(i * NT, NT)], start=(k == 0), stop=(k == 1))
                    ins.then_inc(in_done, 1)
                pe.wait_ge(silu, i * 6 + 3)
                for k in range(KD):
                    ins = pe.matmul(psD, Wx[:, k, :], xs[:, k, :], start=(k == 0), stop=(k == KD - 1))
                ins.then_inc(xd_done, 1)
                pe.wait_ge(y_step, i * 6 + 6)
                for k in range(KD):
                    ins = pe.matmul(psY, y2[:, k, :], Wout[:, k, :], start=(k == 0), stop=(k == KD - 1))
                ins.then_inc(out_done, 1)

        @block.scalar
        def _(act):
            act.wait_ge(w_in, 112)
            act.activation(negA[:, :], Alog[:, :], ACT.Exp).then_inc(a_ready, 1)
            act.wait_ge(consts, 1)
            with act.Fori(0, NPAIR) as i:
                act.wait_ge(in_done, i * 2 + 1)
                act.activation(xpad[:, :, :, DC - 1:], psX.rearrange("p (k b t) -> p k b t", k=KD, b=2), ACT.Copy)\
                    .then_inc(x_copied, 1)
                act.wait_ge(in_done, i * 2 + 2)
                act.activation(ez[:, :, :], psZ.rearrange("p (k n) -> p k n", k=KD), ACT.Exp, scale=-1.0)\
                    .then_inc(ex_done, 1)
                act.wait_ge(taps, i * 16 + 16)
                act.activation(ex[:, :, :], xc[:, :, :], ACT.Exp, scale=-1.0).then_inc(ex_done, 1)
                act.wait_ge(xd_done, i + 1)
                act.activation(xd[:, :], psD, ACT.Copy).then_inc(xd_kept, 1)
                act.wait_ge(dt_step, i * 13 + 1)
                act.activation(dtw[:, 1, :], dtw[:, 0, :], ACT.Exp).then_inc(dt_exp, 1)
                act.wait_ge(dt_step, i * 13 + 13)
                act.activation(dA[:, :, :], dA[:, :, :], ACT.Exp, scale=-1.0).then_inc(da_exp, 1)

        @block.gpsimd
        def _(pool):
            pool.memset(xpad[:, :, :, 0:DC - 1], 0.0).then_inc(consts, 1)
            with pool.Fori(0, NPAIR) as i:
                xt = xs[:, :, :].rearrange("p k (b t) -> p b t k", b=2)
                bb = Bb[:, :, :].rearrange("p (b t) s -> p b t s", b=2)
                cc = BC[:, DS:2 * DS, :].rearrange("p s (b t) -> p b t s", b=2)
                pool.wait_ge(bb_ready, i * 2 + 2)
                for b in range(2):
                    pool.tensor_tensor(U[:, :, b, :, :], bb[:, b, :, :][:, :, None, :].to_broadcast([P, T, KD, DS]),
                                       xt[:, b, :, :][:, :, :, None].to_broadcast([P, T, KD, DS]),
                                       ALU.mult).then_inc(u_built, 1)
                pool.wait_ge(scan, i * SCAN + SCAN)
                for b in range(2):
                    pool.tensor_tensor(U[:, :, b, :, :], U[:, :, b, :, :],
                                       cc[:, b, :, :][:, :, None, :].to_broadcast([P, T, KD, DS]),
                                       ALU.mult).then_inc(hc_done, 1)

        @block.vector
        def _(dve):
            dve.sem_inc(x2_added, 1)
            dve.wait_ge(w_in, 112)
            dve.wait_ge(a_ready, 1)
            with dve.Fori(0, NPAIR) as i:
                dve.wait_ge(x_copied, i + 1)
                for k in range(KD):
                    dve.tensor_scalar(xc[:, k, :].rearrange("p (b t) -> p b t", b=2), xpad[:, k, :, DC - 1:],
                                      cw[:, k, DC - 1:DC], cb[:, k:k + 1], ALU.mult, ALU.add).then_inc(taps, 1)
                for j in range(DC - 1):
                    for k in range(KD):
                        dve.wait_ge(taps, i * 16 + (4 * j + k + 1))
                        v = xc[:, k, :].rearrange("p (b t) -> p b t", b=2)
                        dve.scalar_tensor_tensor(v, xpad[:, k, :, j:j + T], cw[:, k, j:j + 1], v, ALU.mult,
                                                 ALU.add).then_inc(taps, 1)
                dve.wait_ge(ex_done, i * 2 + 2)
                dve.tensor_scalar(ex[:, :, :], ex[:, :, :], 1.0, None, ALU.add).then_inc(silu, 1)
                dve.wait_ge(silu, i * 6 + 1)
                dve.reciprocal(ex[:, :, :], ex[:, :, :]).then_inc(silu, 1)
                dve.wait_ge(silu, i * 6 + 2)
                dve.tensor_tensor(xs[:, :, :], xc[:, :, :], ex[:, :, :], ALU.mult).then_inc(silu, 1)
                dve.tensor_scalar(ez[:, :, :], ez[:, :, :], 1.0, None, ALU.add).then_inc(silu, 1)
                dve.wait_ge(silu, i * 6 + 4)
                dve.reciprocal(ez[:, :, :], ez[:, :, :]).then_inc(silu, 1)
                dve.wait_ge(silu, i * 6 + 5)
                dve.tensor_tensor(zs[:, :, :], psZ.rearrange("p (k n) -> p k n", k=KD), ez[:, :, :],
                                  ALU.mult).then_inc(silu, 1)
                dve.wait_ge(xd_in, i * 16 + 16)
                w = [dtw[:, n, :] for n in range(6)]
                done = [0]

                def step(ins):
                    ins.then_inc(dt_step, 1)
                    done[0] += 1

                def last():
                    dve.wait_ge(dt_step, i * 13 + done[0])

                step(dve.tensor_scalar(w[0], BC[:, XD - 1, :], 0.0, None, ALU.min))
                dve.wait_ge(dt_exp, i + 1)
                step(dve.tensor_scalar(w[2], w[1], 2.0, None, ALU.add))
                last()
                step(dve.reciprocal(w[3], w[2]))
                last()
                step(dve.tensor_tensor(w[4], w[1], w[3], ALU.mult))
                last()
                step(dve.tensor_tensor(w[5], w[4], w[4], ALU.mult))
                last()
                step(dve.tensor_scalar(w[2], w[5], 1.0 / 9, 1.0 / 7, ALU.mult, ALU.add))
                last()
                step(dve.tensor_tensor(w[3], w[2], w[5], ALU.mult))
                last()
                step(dve.scalar_tensor_tensor(w[2], w[3], 1.0 / 5, w[5], ALU.add, ALU.mult))
                last()
                step(dve.scalar_tensor_tensor(w[3], w[2], 1.0 / 3, w[5], ALU.add, ALU.mult))
                last()
                step(dve.scalar_tensor_tensor(w[2], w[3], 1.0, w[4], ALU.add, ALU.mult))
                last()
                step(dve.tensor_scalar(w[3], w[2], 2.0, 0.001, ALU.mult, ALU.max))
                last()
                dve.tensor_scalar(dt[:, :], w[3], 0.1, None, ALU.min).then_inc(dt_step, 1)
                done[0] += 1
                last()
                dtb = dt[:, :][:, :, None].to_broadcast([P, NT, DS])
                dve.tensor_tensor(dA[:, :, :], dtb, negA[:, :][:, None, :].to_broadcast([P, NT, DS]),
                                  ALU.mult).then_inc(scan, 1)
                dve.tensor_tensor(Bb[:, :, :], dtb, BC[:, 0:DS, :].rearrange("p s n -> p n s"),
                                  ALU.mult).then_inc(bb_ready, 1)
                dve.wait_ge(scan, i * SCAN + 1)
                dve.tensor_scalar(dA[:, :, :], dA[:, :, :], 20.0, 0.0, ALU.min, ALU.max).then_inc(dt_step, 1)
                dve.wait_ge(bb_ready, i * 2 + 1)
                dve.tensor_scalar(Bb[:, :, :], Bb[:, :, :], 10.0, -10.0, ALU.min, ALU.max).then_inc(bb_ready, 1)
                dve.wait_ge(u_built, i * 2 + 2)
                dve.wait_ge(da_exp, i + 1)
                flat = [U[:, t, :, :, :].rearrange("p b k s -> p (b k s)") for t in range(T)]
                dec = dA[:, :, :].rearrange("p (b t) s -> p t b s", b=2)
                dve.tensor_scalar(flat[0], flat[0], 100.0, -100.0, ALU.min, ALU.max).then_inc(scan, 1)
                n = 2
                for t in range(1, T):
                    dve.wait_ge(scan, i * SCAN + n)
                    dve.tensor_tensor(carry[:, :, :, :], U[:, t - 1, :, :, :],
                                      dec[:, t, :, :][:, :, None, :].to_broadcast([P, 2, KD, DS]),
                                      ALU.mult).then_inc(scan, 1)
                    dve.wait_ge(scan, i * SCAN + n + 1)
                    dve.tensor_tensor(flat[t], flat[t], carry[:, :, :, :].rearrange("p b k s -> p (b k s)"),
                                      ALU.add).then_inc(scan, 1)
                    dve.wait_ge(scan, i * SCAN + n + 2)
                    dve.tensor_scalar(flat[t], flat[t], 100.0, -100.0, ALU.min, ALU.max).then_inc(scan, 1)
                    n += 3
                assert n == SCAN
                dve.wait_ge(hc_done, i * 2 + 2)
                dve.tensor_reduce(ysum[:, :, :, :].rearrange("p t b k -> p (t b k)"),
                                  U[:, :, :, :, :].rearrange("p t b k s -> p (t b k) s"), AX_X,
                                  ALU.add).then_inc(y_step, 1)
                dve.wait_ge(y_step, i * 6 + 1)
                dve.tensor_tensor(yg[:, :, :].rearrange("p k (b t) -> p k b t", b=2),
                                  ysum[:, :, :, :].rearrange("p t b k -> p k b t"),
                                  zs[:, :, :].rearrange("p k (b t) -> p k b t", b=2), ALU.mult).then_inc(y_step, 1)
                dve.wait_ge(y_step, i * 6 + 2)
                for k in range(KD):
                    dve.scalar_tensor_tensor(y2[:, k, :], xs[:, k, :], Dp[:, k:k + 1], yg[:, k, :], ALU.mult,
                                             ALU.add).then_inc(y_step, 1)
                dve.wait_ge(out_done, i + 1)
                xp = X[:, bass.ds(i, 1), :].rearrange("p a c -> p (a c)")
                dve.tensor_tensor(xp, psY, xp, ALU.add).then_inc(x2_added, 1)


def experts(nc, a, out, sem, tensor_in, psum, X, ident, nhalf, xT):
    norm_phase(nc, "ln3", sem, tensor_in, psum, X, ident, nhalf, xT)
    with ExitStack() as ctx:
        sb = tensor_in(ctx)
        CH = 256
        NCH = B * T // CH
        NB = CH // T
        NPIECE = E + FT
        PW = 2 * DFF
        Whi = sb("Whi", [P, NPIECE, PW], F16)
        Wlo = sb("Wlo", [P, NPIECE, PW], F16)
        gW2 = sb("gW2", [P, 2, E])
        gb1 = sb("gb1", [P, 2])
        gb2b = sb("gb2b", [P, E])
        gb2c = sb("gb2c", [E, 1])
        hs = sb("hs", [P, 2, T])
        hsd = sb("hsd", [P, 2, 2, T])
        G = sb("G", [P, E, T])
        Gt = sb("Gt", [P, E])
        B1 = sb("B1", [P, FT, T])
    
        w_small = sem("ff_w_small")
        piece_in = [sem("piece_in0"), sem("piece_in1")]
        piece_hi = sem("piece_hi")
        piece_lo = sem("piece_lo")
        gate_h = sem("gate_h")
        gate_relu = sem("gate_relu")
        g_step = sem("g_step")
        g_mm = sem("g_mm")
        g_kept = sem("g_kept")

        with ExitStack() as cs:
            sbs = tensor_in(cs)
            stage = [sbs(f"wstage{n}", [P, PW]) for n in range(2)]
            gW1 = sbs("gW1", [P, 2, C])
            eb1 = sbs("eb1", [E, DFF])
            eb2 = sbs("eb2", [E, C])
            G8 = sbs("G8", [E, PAIR_TOK])
            gW2w = sbs("gW2w", [P, 2, E, P])
            Hr = sbs("Hr", [P, 4, 512])
            block = cs.enter_context(nc.Block())

            @block.sync
            def _(sp):
                sp.dma_start(gW1[:, :, :], a["gW1T"].rearrange("(k p) n -> p k n", p=P)).then_inc(w_small, 16)
                with nc.allow_non_contiguous_dma(reason="small parameters"):
                    sp.dma_start(gW2[:, :, :], a["gW2T"].rearrange("(k p) n -> p k n", p=P)).then_inc(w_small, 16)
                    sp.dma_start(gb1[:, :], a["gb1"].rearrange("(k p) -> p k", p=P)).then_inc(w_small, 16)
                    sp.dma_start(gb2c[:, :], a["gb2"].rearrange("(e o) -> e o", o=1)).then_inc(w_small, 16)
                sp.dma_start(gb2b[:, :], a["gb2"].partition_broadcast(P)).then_inc(w_small, 16)
                sp.dma_start(eb1[:, :], a["eb1"]).then_inc(w_small, 16)
                sp.dma_start(eb2[:, :], a["eb2"]).then_inc(w_small, 16)
                with sp.Fori(0, NPIECE // 2) as i:
                    for u in range(2):
                        sp.wait_ge(piece_lo, i * 2 + (u + 1))
                        sp.dma_start(stage[u][:, :], a["WF"][bass.ds(i * 2 + u, 1)].rearrange("a p n -> (a p) n"))\
                            .then_inc(piece_in[u], 16)

            @block.scalar
            def _(act):
                act.wait_ge(w_small, 112)
                for n in range(8):
                    m, c = divmod(n, 4)
                    act.wait_ge(gate_h, n + 1)
                    if n == 4:
                        act.wait_ge(g_step, 2)
                    act.activation(Hr[:, c, :], bank(psum, n % 2), ACT.Relu, bias=gb1[:, m:m + 1])\
                        .then_inc(gate_relu, 1)
                with act.Fori(0, NPIECE // 2) as i:
                    for u in range(2):
                        act.wait_ge(piece_in[u], i * 16 + 16)
                        act.nop(nofuse=True)
                        act.activation(Whi[:, bass.ds(i * 2 + u, 1), :].rearrange("p a n -> p (a n)"), stage[u][:, :],
                                       ACT.Copy).then_inc(piece_hi, 1)

            @block.vector
            def _(dve):
                dve.sem_inc(piece_lo, 2)
                dve.wait_ge(w_small, 112)
                dve.tensor_copy(gW2w[:, :, :, :], gW2[:, :, :][:, :, :, None].to_broadcast([P, 2, E, P]))\
                   .then_inc(g_step, 1)
                for m in range(2):
                    dve.wait_ge(gate_relu, 4 * m + 4)
                    dve.tensor_reduce(hs[:, m, :], Hr[:, :, :].rearrange("p c (b t) -> p t (c b)", t=T), AX_X,
                                      ALU.add).then_inc(g_step, 1)
                dve.wait_ge(g_step, 3)
                dve.tensor_scalar(hsd[:, :, :, :].rearrange("p m d t -> p m d t"),
                                  hs[:, :, :][:, :, None, :].to_broadcast([P, 2, 2, T]), 1.0 / B, None,
                                  ALU.mult).then_inc(g_step, 1)
                dve.wait_ge(g_mm, 1)
                dve.tensor_tensor(G[:, :, :], bank(psum, 2).rearrange("p (e t) -> p e t", e=E),
                                  gb2b[:, :][:, :, None].to_broadcast([P, E, T]), ALU.add).then_inc(g_kept, 1)
                dve.wait_ge(g_mm, 2)
                dve.tensor_tensor(Gt[:, :], bank(psum, 3, E), gb2b[:, :], ALU.add).then_inc(g_kept, 1)
                dve.wait_ge(g_mm, 3)
                dve.tensor_scalar(G8[:, :], psum[0:E, 4 * 512:4 * 512 + PAIR_TOK], gb2c[:, :], None,
                                  ALU.add).then_inc(g_kept, 1)
                dve.wait_ge(g_mm, 4)
                dve.tensor_copy(B1[:, :, :], bank(psum, 5).rearrange("p (f t) -> p f t", f=FT)).then_inc(g_kept, 1)
                dve.wait_ge(g_mm, 5)
                dve.tensor_tensor(X[:, :, :], X[:, :, :], bank(psum, 6, C)[:, None, :].to_broadcast([P, NPAIR, C]), ALU.add)
                with dve.Fori(0, NPIECE // 2) as i:
                    for u in range(2):
                        dve.wait_ge(piece_hi, i * 2 + (u + 1))
                        dve.tensor_tensor(Wlo[:, bass.ds(i * 2 + u, 1), :].rearrange("p a n -> p (a n)"), stage[u][:, :],
                                          Whi[:, bass.ds(i * 2 + u, 1), :].rearrange("p a n -> p (a n)"),
                                          ALU.subtract).then_inc(piece_lo, 1)

            @block.tensor
            def _(pe):
                pe.wait_ge(w_small, 112)
                for n in range(8):
                    m, c = divmod(n, 4)
                    if n >= 2:
                        pe.wait_ge(gate_relu, n - 1)
                    for k in range(2):
                        ins = pe.matmul(bank(psum, n % 2), gW1[:, k, m * P:(m + 1) * P], xT[:, k, c * 512:(c + 1) * 512],
                                        start=(k == 0), stop=(k == 1))
                    ins.then_inc(gate_h, 1)
                pe.wait_ge(g_step, 4)
                for e in range(E):
                    for m in range(2):
                        ins = pe.matmul(bank(psum, 2)[:, e * T:(e + 1) * T], gW2w[:, m, e, :], hsd[:, m, 0, :],
                                        start=(m == 0), stop=(m == 1))
                ins.then_inc(g_mm, 1)
                for m in range(2):
                    ins = pe.matmul(bank(psum, 3, E), hsd[:, m, :, :].rearrange("p d t -> p (d t)"), gW2[:, m, :],
                                    start=(m == 0), stop=(m == 1))
                ins.then_inc(g_mm, 1)
                for m in range(2):
                    ins = pe.matmul(psum[0:E, 4 * 512:4 * 512 + PAIR_TOK], gW2[:, m, :],
                                    hsd[:, m, :, :].rearrange("p d t -> p (d t)"), start=(m == 0), stop=(m == 1))
                ins.then_inc(g_mm, 1)
                pe.wait_ge(g_kept, 3)
                for f in range(FT):
                    ins = pe.matmul(bank(psum, 5)[:, f * T:(f + 1) * T], eb1[:, f * P:(f + 1) * P], G8[:, 0:T],
                                    start=True, stop=True)
                ins.then_inc(g_mm, 1)
                pe.matmul(bank(psum, 6, C), G8[:, :], eb2[:, :], start=True, stop=True).then_inc(g_mm, 1)

        Xg = sb("Xg", [P, E, CH])
        Xhi = sb("Xhi", [P, 2, E, CH], F16)
        Xlo = sb("Xlo", [P, 2, E, CH], F16)
        pre = [sb(f"pre{n}", [P, CH]) for n in range(2)]
        Hhi = sb("Hhi", [P, FT, CH], F16)
        Hlo = sb("Hlo", [P, FT, CH], F16)
        acc = [sb(f"acc{n}", [P, 2, C]) for n in range(2)]

        x_gated = sem("x_gated")
        x_hi = sem("x_hi")
        x_lo = sem("x_lo")
        h_done = sem("h_done")
        h_pre = sem("h_pre")
        h_hi = sem("h_hi")
        h_lo = sem("h_lo")
        u_done = sem("u_done")
        mixed = sem("mixed")
        stored = sem("stored")
        block = ctx.enter_context(nc.Block())
        UA = 8

        @block.tensor
        def _(pe):
            with pe.Fori(0, NCH) as i:
                for f in range(FT):
                    if f == 0:
                        pe.wait_ge(x_lo, i * 2 + 2)
                    pe.wait_ge(h_pre, i * 8 + (f - 1) + 2)
                    ps = bank(psum, f % 2, CH)
                    n = 0
                    for e in range(E):
                        for k in range(2):
                            cols = slice(k * DFF + f * P, k * DFF + (f + 1) * P)
                            for w, x in ((Whi, Xhi), (Whi, Xlo), (Wlo, Xhi)):
                                ins = pe.matmul(ps, w[:, e, cols], x[:, k, e, :], start=(n == 0), stop=(n == 6 * E - 1))
                                n += 1
                    ins.then_inc(h_done, 1)
                pe.wait_ge(h_lo, i * 8 + 8)
                for tt in range(2):
                    tok = slice(tt * P, (tt + 1) * P)
                    for ep in range(4):
                        pe.wait_ge(mixed, i * 16 + (8 * tt + 2 * ep + 2))
                        n = 0
                        for f in range(FT):
                            cols = slice(ep * 512, (ep + 1) * 512)
                            for h, w in ((Hhi, Whi), (Hhi, Wlo), (Hlo, Whi)):
                                ins = pe.matmul(bank(psum, 2 + ep), h[:, f, tok], w[:, E + f, cols],
                                                start=(n == 0), stop=(n == 3 * FT - 1))
                                n += 1
                        ins.then_inc(u_done, 1)

        @block.scalar
        def _(act):
            def split(v):
                for k in range(2):
                    act.wait_ge(x_gated, v(k + 1))
                    act.activation(Xhi[:, k, :, :], Xg[:, :, :], ACT.Copy).then_inc(x_hi, 1)

            split(lambda n: n)
            with act.Fori(0, NCH) as i:
                for f in range(FT):
                    act.wait_ge(h_pre, i * 8 + (f + 1) + 2)
                    act.activation(Hhi[:, f, :], pre[f % 2][:, :], ACT.Relu).then_inc(h_hi, 1)
                split(lambda n: i * 2 + (n + 2))

        @block.vector
        def _(dve):
            def gate_input(step, v):
                for k in range(2):
                    if isinstance(step, int):
                        src = xT[:, k, step * CH:(step + 1) * CH]
                    else:
                        src = xT[:, k, bass.ds(step * CH, CH)]
                    for q in range(NB):
                        ins = dve.tensor_tensor(Xg[:, :, q * T:(q + 1) * T], G[:, :, :],
                                                (xT[:, k, step * CH + q * T:step * CH + (q + 1) * T] if isinstance(step, int)
                                                 else xT[:, k, bass.ds(step * CH + q * T, T)])
                                                [:, None, :].to_broadcast([P, E, T]), ALU.mult)
                    ins.then_inc(x_gated, 1)
                    dve.wait_ge(x_hi, v(k + 1))
                    dve.tensor_tensor(Xlo[:, k, :, :], Xg[:, :, :], Xhi[:, k, :, :], ALU.subtract).then_inc(x_lo, 1)
                    dve.wait_ge(x_lo, v(k + 1))

            dve.sem_inc(h_pre, 2)
            dve.sem_inc(mixed, UA)
            gate_input(0, lambda n: n)
            with dve.Fori(0, NCH) as i:
                for f in range(FT):
                    dve.wait_ge(h_done, i * 8 + (f + 1))
                    dve.tensor_tensor(pre[f % 2][:, :].rearrange("p (b t) -> p b t", t=T),
                                      bank(psum, f % 2, CH).rearrange("p (b t) -> p b t", t=T),
                                      B1[:, f, :][:, None, :].to_broadcast([P, NB, T]), ALU.add).then_inc(h_pre, 1)
                    dve.wait_ge(h_hi, i * 8 + (f + 1))
                    dve.scalar_tensor_tensor(Hlo[:, f, :], pre[f % 2][:, :], 0.0, Hhi[:, f, :], ALU.max,
                                             ALU.subtract).then_inc(h_lo, 1)
                    dve.wait_ge(h_lo, i * 8 + (f + 1))
                gate_input(i + 1, lambda n: i * 2 + (n + 2))
                for tt in range(2):
                    for e in range(E):
                        if e % 2 == 0:
                            dve.wait_ge(u_done, i * 8 + (4 * tt + e // 2 + 1))
                        ps = bank(psum, 2 + e // 2)[:, (e % 2) * C:(e % 2 + 1) * C]
                        src = (X[:, bass.ds(i * 2 + tt, 1), :].rearrange("p a c -> p (a c)") if e == 0
                               else acc[(e - 1) % 2][:, tt, :])
                        if e == 0:
                            dve.wait_ge(stored, i * 16 + 16)
                        else:
                            dve.wait_ge(mixed, i * 16 + (8 * tt + e) + UA)
                        dve.scalar_tensor_tensor(acc[e % 2][:, tt, :], ps, Gt[:, e:e + 1], src, ALU.mult,
                                                 ALU.add).then_inc(mixed, 1)

        @block.sync
        def _(sp):
            sp.sem_inc(stored, 16)
            with sp.Fori(0, NCH) as i:
                sp.wait_ge(mixed, i * 16 + 16 + UA)
                sp.dma_start(out[bass.ds(i * CH, CH), :].rearrange("(n p) c -> p n c", p=P),
                             acc[(E - 1) % 2][:, :, :]).then_inc(stored, 16)
            sp.wait_ge(stored, 16 * (NCH + 1))


def kernel(**inputs):
    import concourse.bacc as bacc
    from concourse.bass_utils import run_bass_kernel_spmd

    given = {k.removeprefix("L0_"): np.asarray(v) for k, v in inputs.items()}
    Wkv, ctx = given["xattn_Wkv"], given["ctx_768"]
    HD = H * DK
    wk, wv = (w.T.reshape(HP, 2, DK, CTX) for w in (Wkv[:, :HD], Wkv[:, HD:]))
    WkS = np.zeros((2, DK, HP, 2, 2 * P), np.float32)
    WvS = np.zeros((2, DK, HP, 3, P), np.float32)
    for h2 in range(2):
        k, v = wk[:, h2].transpose(1, 0, 2), wv[:, h2].transpose(1, 0, 2)
        WkS[h2, :, :, h2, :CTX] = k
        WkS[h2, :, :, h2, CTX:] = k[:, :, P:]
        WvS[h2, :, :, h2] = v[:, :, :P]
        WvS[h2, :, :, 2, h2 * C1:(h2 + 1) * C1] = v[:, :, P:]
    w1 = given["ffn_eW1"].reshape(E, DFF, 2, P).transpose(0, 3, 2, 1)
    w2 = given["ffn_eW2"].reshape(E, C, FT, P).transpose(2, 3, 0, 1)
    arrays = {
        "x": given["x"].reshape(B * T, C),
        "ident": np.eye(P, dtype=np.float32),
        "ctxT": ctx.transpose(0, 2, 1),
        "ctxN": ctx[:, :JT * P].reshape(B, JT, P, CTX).transpose(0, 2, 1, 3),
        "ctxR": ctx[:, JT * P:],
        "Wq": given["xattn_Wq"], "WkS": WkS.reshape(P, HP, 2, 2 * P), "WvS": WvS.reshape(P, HP, 3, P),
        "Wproj": given["xattn_Wproj"], "bproj": given["xattn_bproj"],
        "WinT": given["attn_W_in"].T, "convw": given["attn_conv_w"], "convb": given["attn_conv_b"],
        "WxT": given["attn_W_xproj"].T, "A_log": given["attn_A_log"], "Dp": given["attn_D_param"],
        "WoutT": given["attn_W_out"].T,
        "gW1T": given["ffn_gW1"].T, "gb1": given["ffn_gb1"], "gW2T": given["ffn_gW2"].T, "gb2": given["ffn_gb2"],
        "eb1": given["ffn_eb1"], "eb2": given["ffn_eb2"],
        "WF": np.concatenate([w1.reshape(E, P, 2 * DFF), w2.reshape(FT, P, E * C)]),
    }
    arrays = {f"in_{k}": np.ascontiguousarray(v) for k, v in arrays.items()}
    nc = bacc.Bacc("TRN2", target_bir_lowering=False, num_devices=1)
    a = {k.removeprefix("in_"): nc.dram_tensor(k, v.shape, F32, kind="ExternalInput").ap() for k, v in arrays.items()}
    out = nc.dram_tensor("out_0", (B * T, C), F32, kind="ExternalOutput").ap()
    build(nc, a, out)
    r = run_bass_kernel_spmd(nc, [arrays], core_ids=[0])
    return r.results[0]["out_0"].reshape(B, T, C)
```

```python
from contextlib import ExitStack

import numpy as np
import concourse.bass as bass
from concourse import mybir

F32 = mybir.dt.float32
F16 = mybir.dt.float16
ALU = mybir.AluOpType
ACT = mybir.ActivationFunctionType
AX_X = mybir.AxisListType.X

P = 128
B, T, C = 32, 64, 256
J, CTX = 1601, 192
H, DK = 16, 64
HP = H // 2
PAIR_TOK = 2 * T
NPAIR = B // 2
JT = J // P
JR = J - JT * P
JN = JT + 1
C1 = CTX - P
SCALE = DK ** -0.5
EPS = 1e-5

DI, DS, DC = 512, 16, 4
KD = DI // P
XD = 2 * DS + 1
E, DFF = 8, 1024
FT = DFF // P


def bank(psum, i, n=512):
    return psum[:, 512 * i:512 * i + n]


class LayerNorm:

    def __init__(self, nc, ctx, tag, X, ident, psum, xT, nhalf):
        def sb(name, shape):
            return ctx.enter_context(nc.sbuf_tensor(f"{tag}_{name}", shape, F32))

        def sem(name):
            return ctx.enter_context(nc.semaphore(f"{tag}_{name}"))

        self.X, self.ident, self.psum, self.xT, self.nhalf = X, ident, psum, xT, nhalf
        self.stats = sb("stats", [P, NPAIR, 6])
        self.diff = sb("diff", [P, NPAIR])
        self.var = sb("var", [P, NPAIR])
        self.mean = sb("mean", [P, NPAIR])
        self.rstd = sb("rstd", [P, NPAIR])
        self.xn = sb("xn", [P, NPAIR, C])
        self.stats_done = sem("stats_done")
        self.var_done = sem("var_done")
        self.rstd_done = sem("rstd_done")
        self.centred = sem("centred")
        self.normed = sem("normed")
        self.turned = sem("turned")
        self.kept = sem("kept")

    def vector(self, dve):
        st = self.stats
        with dve.Fori(0, NPAIR) as n:
            dve.bn_stats(st[:, bass.ds(n, 1), :].rearrange("p a s -> p (a s)"),
                         self.X[:, bass.ds(n, 1), :].rearrange("p a c -> p (a c)")).then_inc(self.stats_done, 1)
        dve.wait_ge(self.stats_done, NPAIR)
        dve.tensor_tensor(self.diff[:, :], st[:, :, 1], st[:, :, 4], ALU.subtract).then_inc(self.stats_done, 1)
        dve.tensor_tensor(self.mean[:, :], st[:, :, 1], st[:, :, 4], ALU.add).then_inc(self.stats_done, 1)
        dve.tensor_tensor(self.var[:, :], st[:, :, 2], st[:, :, 5], ALU.add).then_inc(self.stats_done, 1)
        dve.wait_ge(self.stats_done, NPAIR + 1)
        dve.scalar_tensor_tensor(self.rstd[:, :], self.diff[:, :], 0.25, self.diff[:, :], ALU.mult,
                                 ALU.mult).then_inc(self.stats_done, 1)
        dve.wait_ge(self.stats_done, NPAIR + 4)
        dve.tensor_scalar(self.mean[:, :], self.mean[:, :], 0.5, None, ALU.mult).then_inc(self.stats_done, 1)
        dve.scalar_tensor_tensor(self.diff[:, :], self.var[:, :], 1.0 / C, self.rstd[:, :], ALU.mult,
                                 ALU.add).then_inc(self.stats_done, 1)
        dve.wait_ge(self.stats_done, NPAIR + 6)
        dve.tensor_scalar(self.var[:, :], self.diff[:, :], EPS, None, ALU.add).then_inc(self.var_done, 1)
        dve.tensor_tensor(self.xn[:, :, :], self.X[:, :, :],
                          self.mean[:, :][:, :, None].to_broadcast([P, NPAIR, C]),
                          ALU.subtract).then_inc(self.centred, 1)
        dve.wait_ge(self.centred, 1)
        dve.wait_ge(self.rstd_done, 1)
        dve.tensor_tensor(self.xn[:, :, :], self.xn[:, :, :],
                          self.rstd[:, :][:, :, None].to_broadcast([P, NPAIR, C]),
                          ALU.mult).then_inc(self.normed, 1)

    def gpsimd(self, pool):
        pool.wait_ge(self.var_done, 1)
        pool.tensor_tensor(self.rstd[:, :], self.var[:, :], self.nhalf[:, :], ALU.pow).then_inc(self.rstd_done, 1)

    def tensor(self, pe):
        pe.wait_ge(self.normed, 1)
        for g in range(NPAIR // 2):
            if g >= 2:
                pe.wait_ge(self.kept, g - 1)
            for n in range(2):
                for k in range(2):
                    ins = pe.transpose(bank(self.psum, g % 2)[:, (2 * n + k) * P:(2 * n + k + 1) * P],
                                       self.xn[:, 2 * g + n, k * P:(k + 1) * P], self.ident[:, :])
            ins.then_inc(self.turned, 1)

    def scalar(self, act):
        for g in range(NPAIR // 2):
            act.wait_ge(self.turned, g + 1)
            act.activation(self.xT[:, :, 2 * g * P:(2 * g + 2) * P].rearrange("p k (n t) -> p k n t", n=2),
                           bank(self.psum, g % 2).rearrange("p (n k t) -> p k n t", n=2, k=2),
                           ACT.Copy).then_inc(self.kept, 1)


def build(nc, a, out):
    with ExitStack() as top:
        def sem(name):
            return top.enter_context(nc.semaphore(name))

        def tensor_in(ctx):
            def sb(name, shape, dt=F32):
                return ctx.enter_context(nc.sbuf_tensor(name, shape, dt))
            return sb

        sb = tensor_in(top)
        psum = top.enter_context(nc.psum_tensor("psum", [P, 8 * 512], F32))
        X = sb("X", [P, NPAIR, C])
        ident = sb("ident", [P, P])
        nhalf = sb("nhalf", [P, NPAIR])
        xT = sb("xT", [P, 2, B * T + 2 * PAIR_TOK])

        attention(nc, a, sem, tensor_in, psum, X, ident, nhalf, xT)
        state_space(nc, a, sem, tensor_in, psum, X, ident, nhalf, xT)
        experts(nc, a, out, sem, tensor_in, psum, X, ident, nhalf, xT)


def attention(nc, a, sem, tensor_in, psum, X, ident, nhalf, xT):
    with ExitStack() as ctx:
        sb = tensor_in(ctx)
        Wq = sb("Wq", [P, 2, H * DK])
        WkS = sb("WkS", [P, HP, 2, 2 * P])
        Wvp = sb("Wvp", [P, 3 * HP, C])

        with ExitStack() as cs:
            sbs = tensor_in(cs)
            WvS = sbs("WvS", [P, HP, 3, P])
            Wpr = sbs("Wpr", [P, HP, C])
            bpr = sbs("bpr", [P, C])
            x_in, w_in = sem("x_in"), sem("w_in")
            half_set, wvp_done, wvp_kept, bias_in, wrap = (
                sem("half_set"), sem("wvp_done"), sem("wvp_kept"), sem("bias_in"), sem("wrap"))
            ln = LayerNorm(nc, cs, "ln1", X, ident, psum, xT, nhalf)
            block = cs.enter_context(nc.Block())

            @block.sync
            def _(sp):
                sp.dma_start(X[:, :, :], a["x"].rearrange("(n p) c -> p n c", p=P)).then_inc(x_in, 16)
                sp.dma_start(ident[:, :], a["ident"]).then_inc(x_in, 16)
                sp.dma_start(bpr[:, :], a["bproj"].partition_broadcast(P)).then_inc(bias_in, 16)
                sp.dma_start(WvS[:, :, :, :], a["WvS"]).then_inc(w_in, 16)
                sp.dma_start(Wpr[:, :, :], a["Wproj"].rearrange("(g p) n -> p g n", p=P)).then_inc(w_in, 16)
                sp.dma_start(Wq[:, :, :], a["Wq"].rearrange("(k p) n -> p k n", p=P)).then_inc(w_in, 16)
                sp.dma_start(WkS[:, :, :, :], a["WkS"]).then_inc(w_in, 16)
                sp.wait_ge(w_in, 64)

            @block.vector
            def _(dve):
                dve.memset(nhalf[:, :], -0.5).then_inc(half_set, 1)
                dve.wait_ge(x_in, 32)
                ln.vector(dve)
                dve.wait_ge(bias_in, 16)
                dve.wait_ge(ln.normed, 1)
                dve.tensor_tensor(X[:, :, :], X[:, :, :], bpr[:, :][:, None, :].to_broadcast([P, NPAIR, C]), ALU.add)

            @block.gpsimd
            def _(pool):
                pool.wait_ge(half_set, 1)
                ln.gpsimd(pool)
                pool.wait_ge(ln.kept, 1)
                pool.tensor_copy(xT[:, :, B * T:B * T + PAIR_TOK], xT[:, :, 0:PAIR_TOK]).then_inc(wrap, 1)

            @block.tensor
            def _(pe):
                pe.wait_ge(x_in, 32)
                ln.tensor(pe)
                pe.wait_ge(w_in, 64)
                for g in range(HP):
                    for s in range(3):
                        n = 3 * g + s
                        if n >= 2:
                            pe.wait_ge(wvp_kept, n - 1)
                        pe.matmul(bank(psum, 2 + n % 2, C), WvS[:, g, s, :], Wpr[:, g, :],
                                  start=True, stop=True).then_inc(wvp_done, 1)

            @block.scalar
            def _(act):
                ln.scalar(act)
                for g in range(HP):
                    for s in range(3):
                        n = 3 * g + s
                        act.wait_ge(wvp_done, n + 1)
                        act.activation(Wvp[:, 2 * g + s if s < 2 else H + g, :], bank(psum, 2 + n % 2, C),
                                       ACT.Copy).then_inc(wvp_kept, 1)

        qT = sb("qT", [P, HP, PAIR_TOK])
        Q = [sb(f"Q{i}", [P, 4, 2, H * T], F16) for i in range(2)]
        yN = [sb(f"yN{i}", [P, JN, 2 * CTX], F16) for i in range(2)]
        yT = [sb(f"yT{i}", [P, 3, J], F16) for i in range(2)]
        stage = [sb(f"stage{i}", [P, J]) for i in range(2)]
        prob = sb("prob", [P, J])
        pT = [sb(f"pT{i}", [P, JN, P], F16) for i in range(2)]
        On = sb("On", [P, 2 * P])
        Olo = sb("Olo", [P, CTX])
        OT = sb("OT", [P, 3 * HP, PAIR_TOK])
        mx = sb("mx", [P, 4])
        nb = sb("nb", [P, 2])
        den = sb("den", [P, 2])
        rden = sb("rden", [P, 2])
        psS = psum[:, 0:2048]
        psT = [bank(psum, 4), bank(psum, 5)]
        psO = bank(psum, 6)
        psM = bank(psum, 7)
        psP = psum[:, 1536:1536 + C]

        loaded = [sem("loaded0"), sem("loaded1")]
        stage_free = [sem("stage0_free"), sem("stage1_free")]
        hi_cut = sem("hi_cut")
        ctx_ready = sem("ctx_ready")
        scored = sem("scored")
        maxed = sem("maxed")
        biased = sem("biased")
        expd = sem("expd")
        recip = sem("recip")
        turned = sem("turned")
        hi_kept = sem("hi_kept")
        lo_kept = sem("lo_kept")
        summed = sem("summed")
        olo_kept = sem("olo_kept")
        normed = sem("normed")
        o_turned = sem("o_turned")
        o_kept = sem("o_kept")
        q_done = sem("q_done")
        q_kept = sem("q_kept")
        qk_done = sem("qk_done")
        qk_hi = sem("qk_hi")
        qk_lo = sem("qk_lo")
        projected = sem("projected")
        x_added = sem("x_added")
        AHEAD, LO_AHEAD, CTX_AHEAD = 16, 4, 2
        GROUPS = [(0, 4), (4, 8), (8, 12), (12, 13)]
        block = ctx.enter_context(nc.Block())

        def per_pair(i, u, n, k):
            return i * (2 * n) + (u * n + k)

        @block.sync
        def _(sp):
            with sp.Fori(0, NPAIR // 2) as i:
                for u in range(2):
                    for b in range(2):
                        be = i * 4 + (2 * u + b)
                        n = 2 * (2 * u + b)
                        yt = a["ctxT"][bass.ds(be, 1)].rearrange("a c j -> (a c) j")
                        yn = a["ctxN"][bass.ds(be, 1)].rearrange("a p m c -> (a p) m c")
                        yr = a["ctxR"][bass.ds(be, 1)].rearrange("a p c -> (a p) c")
                        half = 7 * CTX
                        sp.wait_ge(stage_free[0], i * 8 + (n + 1))
                        sp.dma_start(stage[0][:, :], yt[0:P, :]).then_inc(loaded[0], 16)
                        sp.wait_ge(ctx_ready, i * 8 + (n + CTX_AHEAD))
                        sp.dma_start(stage[1][0:C1, :], yt[P:CTX, :]).then_inc(loaded[1], 16)
                        sp.dma_start(stage[1][C1:P, :], yt[P:CTX, :]).then_inc(loaded[1], 16)
                        sp.wait_ge(stage_free[0], i * 8 + (n + 2))
                        sp.dma_start(stage[0][:, 0:half].rearrange("p (m c) -> p m c", c=CTX),
                                     yn[:, 0:7, :]).then_inc(loaded[0], 16)
                        sp.wait_ge(stage_free[1], i * 4 + (n // 2 + 1))
                        sp.dma_start(stage[1][:, 0:5 * CTX].rearrange("p (m c) -> p m c", c=CTX),
                                     yn[:, 7:12, :]).then_inc(loaded[1], 16)
                        sp.dma_start(stage[1][0:JR, 5 * CTX:6 * CTX], yr).then_inc(loaded[1], 16)

        @block.gpsimd
        def _(pool):
            pool.sem_inc(stage_free[0], 1)
            pool.sem_inc(ctx_ready, CTX_AHEAD)
            with pool.Fori(0, NPAIR // 2) as i:
                for u in range(2):
                    for b in range(2):
                        n = 2 * u + b
                        s0, s1, N_, T_ = stage[0], stage[1], yN[b], yT[b]
                        pool.wait_ge(normed, i * 32 + (AHEAD + (n - 1) * HP))
                        pool.wait_ge(loaded[0], i * 128 + (32 * n + 16))
                        pool.nop(nofuse=True)
                        pool.tensor_copy(T_[:, 0, :], s0[:, :]).then_inc(hi_cut, 1)
                        pool.wait_ge(hi_cut, i * 20 + (5 * n + 1))
                        pool.tensor_tensor(T_[:, 2, :], s0[:, :], T_[:, 0, :], ALU.subtract)\
                            .then_inc(stage_free[0], 1)
                        pool.wait_ge(loaded[1], i * 256 + (64 * n + 32))
                        pool.nop(nofuse=True)
                        pool.tensor_copy(T_[:, 1, :], s1[:, :]).then_inc(hi_cut, 1)
                        pool.wait_ge(hi_cut, i * 20 + (5 * n + 2))
                        pool.tensor_tensor(T_[0:C1, 1, :], s1[0:C1, :], T_[0:C1, 1, :], ALU.subtract)\
                            .then_inc(stage_free[1], 1)
                        v0 = s0[:, 0:7 * CTX].rearrange("p (m c) -> p m c", c=CTX)
                        pool.wait_ge(loaded[0], i * 128 + (32 * n + 32))
                        pool.nop(nofuse=True)
                        pool.tensor_copy(N_[:, 0:7, 0:CTX], v0).then_inc(hi_cut, 1)
                        pool.wait_ge(hi_cut, i * 20 + (5 * n + 3))
                        pool.tensor_tensor(N_[:, 0:7, CTX:], v0, N_[:, 0:7, 0:CTX], ALU.subtract)\
                            .then_inc(stage_free[0], 1)
                        v1 = s1[:, 0:5 * CTX].rearrange("p (m c) -> p m c", c=CTX)
                        vr = s1[0:JR, 5 * CTX:6 * CTX]
                        pool.wait_ge(loaded[1], i * 256 + (64 * n + 64))
                        pool.nop(nofuse=True)
                        pool.tensor_copy(N_[:, 7:12, 0:CTX], v1).then_inc(hi_cut, 1)
                        pool.tensor_copy(N_[0:JR, 12, 0:CTX], vr).then_inc(hi_cut, 1)
                        pool.wait_ge(hi_cut, i * 20 + (5 * n + 5))
                        pool.tensor_tensor(N_[:, 7:12, CTX:], v1, N_[:, 7:12, 0:CTX], ALU.subtract)\
                            .then_inc(ctx_ready, 1)
                        pool.tensor_tensor(N_[0:JR, 12, CTX:], vr, N_[0:JR, 12, 0:CTX], ALU.subtract)\
                            .then_inc(ctx_ready, 1)

        @block.tensor
        def _(pe):
            def q_half(pair, half, misc_free):
                misc_free()
                for g in range(4):
                    for k in range(2):
                        ins = pe.matmul(psM[:, g * P:(g + 1) * P],
                                        Wq[:, k, (4 * half + g) * P:(4 * half + g + 1) * P],
                                        xT[:, k, bass.ds(pair * PAIR_TOK, PAIR_TOK)]
                                        if not isinstance(pair, int) else
                                        xT[:, k, pair * PAIR_TOK:(pair + 1) * PAIR_TOK],
                                        start=(k == 0), stop=(k == 1))
                ins.then_inc(q_done, 1)

            def qk_group(g, misc_free):
                misc_free()
                for c in range(2):
                    for h2 in range(2):
                        ins = pe.matmul(psM[:, (2 * c + h2) * P:(2 * c + h2 + 1) * P],
                                        WkS[:, g, h2, c * P:(c + 1) * P], qT[:, g, :], start=True, stop=True)
                ins.then_inc(qk_done, 1)

            def wait_for(s, v):
                return lambda: pe.wait_ge(s, v)

            q_half(0, 0, lambda: None)
            q_half(0, 1, wait_for(q_kept, 1))
            pe.wait_ge(q_kept, 2)
            for g in range(HP):
                qk_group(g, wait_for(qk_lo, g) if g else (lambda: None))

            with pe.Fori(0, NPAIR // 2) as i:
                for u in range(2):
                    nxt = i * 2 + (u + 1)

                    def at(n, k, u=u, i=i):
                        return per_pair(i, u, n, k)

                    def score(t, chunks, u=u, at=at):
                        b, tt = divmod(t, HP)
                        if 0 in chunks:
                            if tt == 0:
                                pe.wait_ge(ctx_ready, at(4, 2 * b + 2) + CTX_AHEAD)
                            if t == 0:
                                pe.wait_ge(qk_lo, at(8, 8))
                            if t > 0:
                                pe.wait_ge(expd, at(16, t))
                        for c in chunks:
                            lo, hi = 512 * c, min(J, 512 * (c + 1))
                            if t == 0 and c == 3:
                                pe.wait_ge(x_added, at(1, 1))
                            for n, (q, y) in enumerate([(0, 0), (1, 1), (0, 2), (2, 0), (3, 1)]):
                                ins = pe.matmul(psS[:, lo:hi], Q[u][:, q, b, tt * P:(tt + 1) * P],
                                                yT[b][:, y, lo:hi], start=(n == 0), stop=(n == 4))
                            if c in (1, 3):
                                ins.then_inc(scored, 1)

                    def turn(t, g, at=at):
                        if g == 0:
                            pe.wait_ge(expd, at(16, t + 1))
                        pe.wait_ge(lo_kept, at(64, 4 * t + g - 1) + LO_AHEAD)
                        lo, hi = GROUPS[g]
                        for n in range(lo, hi):
                            w = P if n < JT else JR
                            ins = pe.transpose(psT[g % 2][0:w, (n - lo) * P:(n - lo + 1) * P],
                                               prob[:, n * P:n * P + w], ident[:, :])
                        ins.then_inc(turned, 1)

                    def gather(t, at=at):
                        b = t // HP
                        pe.wait_ge(normed, at(16, t) + AHEAD)
                        for n in range(JN):
                            k = P if n < JT else JR
                            if n % 4 == 0:
                                pe.wait_ge(lo_kept, at(64, 4 * t + n // 4 + 1) + LO_AHEAD)
                            pe.matmul(psO[:, 0:2 * CTX], pT[0][0:k, n, :], yN[b][0:k, n, :],
                                      start=(n == 0), stop=False)
                            ins = pe.matmul(psO[:, 0:CTX], pT[1][0:k, n, :], yN[b][0:k, n, 0:CTX],
                                            start=False, stop=(n == JN - 1))
                        ins.then_inc(summed, 1)

                    def turn_o(t, misc_free, at=at):
                        pe.wait_ge(normed, at(16, t + 1) + AHEAD)
                        misc_free()
                        for k in range(2):
                            ins = pe.transpose(psM[:, k * P:(k + 1) * P], On[:, k * P:(k + 1) * P], ident[:, :])
                        ins.then_inc(o_turned, 1)

                    def project(chunks, first=False, last=False):
                        for n, k in enumerate(chunks):
                            ins = pe.matmul(psP, OT[:, k, :], Wvp[:, k, :],
                                            start=(first and n == 0), stop=(last and n == len(chunks) - 1))
                        if last:
                            ins.then_inc(projected, 1)

                    def o_free(t, at=at):
                        return wait_for(o_kept, at(16, t) + AHEAD)

                    def qk_free(n, at=at):
                        return wait_for(qk_lo, at(8, n) + 8)

                    def q_free(n, at=at):
                        return wait_for(q_kept, at(2, n) + 2)

                    score(0, [0, 1, 2, 3])
                    q_half(nxt, 0, o_free(0))
                    for t in range(1, 16):
                        turn(t - 1, 0)
                        turn(t - 1, 1)
                        score(t, [0])
                        turn(t - 1, 2)
                        score(t, [1])
                        turn(t - 1, 3)
                        score(t, [2, 3])
                        if t >= 2:
                            turn_o(t - 2, q_free(2) if t == 2 else qk_free(t - 2) if t <= 9 else o_free(t - 2))
                        gather(t - 1)
                        if t == 1:
                            q_half(nxt, 1, q_free(1))
                        elif t <= 8:
                            qk_group(t - 2, o_free(t - 1))
                    for g in range(4):
                        turn(15, g)
                    qk_group(7, o_free(14))
                    gather(15)
                    turn_o(14, qk_free(8))
                    pe.wait_ge(o_kept, at(16, 15) + AHEAD)
                    pe.wait_ge(expd, at(16, 16))
                    project(range(0, 12), first=True)
                    turn_o(15, lambda: None)
                    project([12, 13] + list(range(16, 23)))
                    pe.wait_ge(o_kept, at(16, 16) + AHEAD)
                    project([14, 15, 23], last=True)

        @block.scalar
        def _(act):
            act.sem_inc(o_kept, AHEAD)

            def q_copy(half, v):
                act.wait_ge(q_done, v)
                act.activation(qT[:, 4 * half:4 * half + 4, :], psM.rearrange("p (g t) -> p g t", g=4),
                               ACT.Copy).then_inc(q_kept, 1)

            def qk_high(g, dst, v):
                act.wait_ge(qk_done, v)
                for c in range(2):
                    ins = act.activation(dst[:, c, :, 2 * g * T:(2 * g + 2) * T].rearrange("p b (h t) -> p h b t", h=2),
                                         psM[:, 2 * c * P:(2 * c + 2) * P].rearrange("p (h b t) -> p h b t", h=2, b=2),
                                         ACT.Copy)
                ins.then_inc(qk_hi, 1)

            q_copy(0, 1)
            q_copy(1, 2)
            for g in range(HP):
                qk_high(g, Q[0], g + 1)

            with act.Fori(0, NPAIR // 2) as i:
                for u in range(2):
                    def at(n, k, u=u, i=i):
                        return per_pair(i, u, n, k)

                    def exponentials(t, at=at):
                        act.wait_ge(biased, at(16, t + 1))
                        act.activation(prob[:, :], psS[:, 0:J], ACT.Exp, bias=nb[:, t % 2:t % 2 + 1], scale=SCALE,
                                       accum_out=den[:, t % 2:t % 2 + 1]).then_inc(expd, 1)

                    def high(t, at=at):
                        for g, (lo, hi) in enumerate(GROUPS):
                            act.wait_ge(turned, at(64, 4 * t + g + 1))
                            w = P if g < 3 else JR
                            act.activation(pT[0][0:w, lo:hi, :],
                                           psT[g % 2][0:w, 0:(hi - lo) * P].rearrange("p (n h) -> p n h", h=P),
                                           ACT.Copy).then_inc(hi_kept, 1)

                    def sum_low(t, at=at):
                        act.wait_ge(summed, at(16, t + 1))
                        act.wait_ge(recip, at(16, t + 1))
                        act.activation(Olo[:, :], psO[:, CTX:2 * CTX], ACT.Copy,
                                       scale=rden[:, t % 2:t % 2 + 1]).then_inc(olo_kept, 1)

                    def o_copy(t, at=at):
                        b, tt = divmod(t, HP)
                        act.wait_ge(o_turned, at(16, t + 1))
                        if t == 0:
                            act.wait_ge(x_added, at(1, 1))
                        tok = slice(b * T, (b + 1) * T)
                        act.activation(OT[:, 2 * tt:2 * tt + 2, tok], psM[:, 0:P].rearrange("p (h t) -> p h t", h=2),
                                       ACT.Copy)
                        act.activation(OT[0:C1, H + tt, tok], psM[0:C1, P:P + T], ACT.Copy)
                        act.activation(OT[C1:P, H + tt, tok], psM[C1:P, P + T:2 * P], ACT.Copy).then_inc(o_kept, 1)

                    exponentials(0)
                    q_copy(0, at(2, 1) + 2)
                    for t in range(1, 16):
                        high(t - 1)
                        if t >= 2:
                            o_copy(t - 2)
                        exponentials(t)
                        sum_low(t - 1)
                        if t == 1:
                            q_copy(1, at(2, 2) + 2)
                        elif t <= 8:
                            qk_high(t - 2, Q[1 - u], at(8, t - 1) + 8)
                    high(15)
                    qk_high(7, Q[1 - u], at(8, 8) + 8)
                    sum_low(15)
                    o_copy(14)
                    o_copy(15)

        @block.vector
        def _(dve):
            dve.sem_inc(normed, AHEAD)
            dve.sem_inc(x_added, 1)
            dve.sem_inc(lo_kept, LO_AHEAD)

            def qk_low(g, dst, v):
                dve.wait_ge(qk_hi, v)
                for c in range(2):
                    hi, lo = (dst[:, s, :, 2 * g * T:(2 * g + 2) * T].rearrange("p b (h t) -> p h b t", h=2)
                              for s in (c, 2 + c))
                    ins = dve.tensor_tensor(lo, psM[:, 2 * c * P:(2 * c + 2) * P].rearrange("p (h b t) -> p h b t", h=2, b=2),
                                            hi, ALU.subtract)
                ins.then_inc(qk_lo, 1)

            for g in range(HP):
                qk_low(g, Q[0], g + 1)

            with dve.Fori(0, NPAIR // 2) as i:
                for u in range(2):
                    pair = i * 2 + u

                    def at(n, k, u=u, i=i):
                        return per_pair(i, u, n, k)

                    def maximum(t, at=at):
                        for n, (lo, hi) in enumerate([(0, 1024), (1024, J)]):
                            dve.wait_ge(scored, at(32, 2 * t + n + 1))
                            dve.tensor_reduce(mx[:, 2 * (t % 2) + n:2 * (t % 2) + n + 1], psS[:, lo:hi], AX_X,
                                              ALU.max).then_inc(maxed, 1)
                        dve.wait_ge(maxed, at(32, 2 * t + 2))
                        m = 2 * (t % 2)
                        dve.tensor_scalar(nb[:, t % 2:t % 2 + 1], mx[:, m:m + 1], mx[:, m + 1:m + 2], -SCALE,
                                          ALU.max, ALU.mult).then_inc(biased, 1)

                    def low(t, at=at):
                        for g, (lo, hi) in enumerate(GROUPS):
                            dve.wait_ge(hi_kept, at(64, 4 * t + g + 1))
                            w = P if g < 3 else JR
                            dve.tensor_tensor(pT[1][0:w, lo:hi, :],
                                              psT[g % 2][0:w, 0:(hi - lo) * P].rearrange("p (n h) -> p n h", h=P),
                                              pT[0][0:w, lo:hi, :], ALU.subtract).then_inc(lo_kept, 1)

                    def reciprocal(t, at=at):
                        dve.wait_ge(expd, at(16, t + 1))
                        dve.reciprocal(rden[:, t % 2:t % 2 + 1], den[:, t % 2:t % 2 + 1]).then_inc(recip, 1)

                    def normalise(t, at=at):
                        dve.wait_ge(olo_kept, at(16, t + 1))
                        if t == 15:
                            dve.wait_ge(o_turned, at(16, 15))
                        r = rden[:, t % 2:t % 2 + 1]
                        dve.scalar_tensor_tensor(On[:, 0:CTX], psO[:, 0:CTX], r, Olo[:, :], ALU.mult, ALU.add)
                        dve.scalar_tensor_tensor(On[:, CTX:2 * P], psO[:, P:CTX], r, Olo[:, P:CTX], ALU.mult,
                                                 ALU.add).then_inc(normed, 1)

                    maximum(0)
                    reciprocal(0)
                    for t in range(1, 16):
                        low(t - 1)
                        maximum(t)
                        reciprocal(t)
                        normalise(t - 1)
                        if 2 <= t <= 8:
                            qk_low(t - 2, Q[1 - u], at(8, t - 1) + 8)
                    low(15)
                    qk_low(7, Q[1 - u], at(8, 8) + 8)
                    normalise(15)
                    dve.wait_ge(projected, at(1, 1))
                    xp = X[:, bass.ds(pair, 1), :].rearrange("p a c -> p (a c)")
                    dve.tensor_tensor(xp, psP, xp, ALU.add).then_inc(x_added, 1)


def norm_phase(nc, tag, sem, tensor_in, psum, X, ident, nhalf, xT):
    with ExitStack() as ctx:
        ln = LayerNorm(nc, ctx, tag, X, ident, psum, xT, nhalf)
        block = ctx.enter_context(nc.Block())

        @block.vector
        def _(dve):
            ln.vector(dve)

        @block.gpsimd
        def _(pool):
            ln.gpsimd(pool)
            pool.wait_ge(ln.kept, 1)
            pool.tensor_copy(xT[:, :, B * T:], xT[:, :, 0:2 * PAIR_TOK]).then_inc(ln.centred, 1)

        @block.tensor
        def _(pe):
            ln.tensor(pe)

        @block.scalar
        def _(act):
            ln.scalar(act)


def state_space(nc, a, sem, tensor_in, psum, X, ident, nhalf, xT):
    norm_phase(nc, "ln2", sem, tensor_in, psum, X, ident, nhalf, xT)
    GB = P // DS
    NG = B // GB
    GT = GB * T
    TB = T // 8
    WIN = (2 * GB - 1) * DS
    with ExitStack() as ctx:
        sb = tensor_in(ctx)
        xD = sb("xD", [P, KD, B * T])
        zs = sb("zs", [P, KD, B * T])
        Xtm = sb("Xtm", [P, NG * TB, DI], F16)
        ABC = sb("ABC", [P, 3, NG, T])
        Dp = sb("Dp", [P, KD])
        eA = sb("eA", [P, 1])
        Wout = sb("Wout", [P, KD, C])
        ss_in = sem("ss_in")
        ea_ready = sem("ea_ready")
        abc_kept = sem("abc_kept")

        with ExitStack() as cs:
            sbs = tensor_in(cs)
            Win = sbs("Win", [P, 2, 2 * DI])
            WxW = sbs("WxW", [P, KD, 3, WIN])
            cw = sbs("cw", [P, KD, DC])
            cb = sbs("cb", [P, KD])
            ident16 = sbs("ident16", [P, P], F16)
            xpad = sbs("xpad", [P, KD, GB, DC - 1 + T])
            xc = sbs("xc", [P, KD, GT])
            sg = sbs("sg", [P, KD, GT])
            xs = xc
            x16 = sbs("x16", [P, KD, TB, 2, 8 * GB], F16)
            in_done = sem("in_done")
            x_copied = sem("x_copied")
            taps = sem("taps")
            sig_exp = sem("sig_exp")
            sig_one = sem("sig_one")
            sig_rec = sem("sig_rec")
            xs_done = sem("xs_done")
            zs_done = sem("zs_done")
            xd_kept = sem("xd_kept")
            x_hi = sem("x16_hi")
            x_lo = sem("x16_lo")
            x_turned = sem("x_turned")
            xtm_kept = sem("xtm_kept")
            abc_done = sem("abc_done")
            pad_set = sem("pad_set")
            block = cs.enter_context(nc.Block())

            @block.sync
            def _(sp):
                sp.dma_start(Win[:, :, :], a["WinT"].rearrange("(k p) n -> p k n", p=P)).then_inc(ss_in, 16)
                with nc.allow_non_contiguous_dma(reason="small parameters"):
                    sp.dma_start(cw[:, :, :], a["convw"].rearrange("(k p) n -> p k n", p=P)).then_inc(ss_in, 16)
                    sp.dma_start(cb[:, :], a["convb"].rearrange("(k p) -> p k", p=P)).then_inc(ss_in, 16)
                    sp.dma_start(Dp[:, :], a["Dp"].rearrange("(k p) -> p k", p=P)).then_inc(ss_in, 16)
                sp.dma_start(WxW[:, :, :, :], a["WxW"].rearrange("(k p) q n -> p k q n", p=P)).then_inc(ss_in, 16)
                sp.dma_start(eA[:, :], a["A_log8"]).then_inc(ss_in, 16)
                sp.dma_start(ident16[:, :], a["ident16"]).then_inc(ss_in, 16)
                sp.dma_start(Wout[:, :, :], a["WoutT"].rearrange("(k p) n -> p k n", p=P)).then_inc(ss_in, 16)

            @block.tensor
            def _(pe):
                pe.wait_ge(ss_in, 128)
                with pe.Fori(0, NG) as g:
                    pe.wait_ge(abc_kept, g + 1)
                    for m in range(2):
                        if m == 1:
                            pe.wait_ge(xtm_kept, g * 4 + 4)
                        for k in range(KD):
                            for half in range(2):
                                ins = pe.matmul(bank(psum, 4 * m + k),
                                                Win[:, half, (4 * m + k) * P:(4 * m + k + 1) * P],
                                                xT[:, half, bass.ds(g * GT, GT)], start=(half == 0), stop=(half == 1))
                        ins.then_inc(in_done, 1)
                    pe.wait_ge(x_lo, g + 1)
                    pe.wait_ge(zs_done, g + 1)
                    for q in range(4):
                        half = bank(psum, 4 + q).bitcast(F16)
                        for n in range(2):
                            for k in range(KD):
                                ins = pe.transpose(half[:, (4 * n + k) * P:(4 * n + k + 1) * P],
                                                   x16[:, k, 2 * q + n, :, :].rearrange("p h n -> p (h n)"),
                                                   ident16[:, :])
                        ins.then_inc(x_turned, 1)
                    for q in range(3):
                        for b in range(GB):
                            lo = (GB - 1 - b) * DS
                            for k in range(KD):
                                ins = pe.matmul(psum[:, q * T:(q + 1) * T], WxW[:, k, q, lo:lo + P],
                                                xs[:, k, b * T:(b + 1) * T], start=(b == 0 and k == 0),
                                                stop=(b == GB - 1 and k == KD - 1))
                    ins.then_inc(abc_done, 1)

            @block.scalar
            def _(act):
                act.sem_inc(abc_kept, 1)
                act.wait_ge(ss_in, 128)
                act.activation(eA[:, :], eA[:, :], ACT.Exp).then_inc(ea_ready, 1)
                act.wait_ge(pad_set, 1)
                with act.Fori(0, NG) as g:
                    act.wait_ge(in_done, g * 2 + 1)
                    act.activation(xpad[:, :, :, DC - 1:], psum[:, 0:2048].rearrange("p (k b t) -> p k b t", k=KD, b=GB),
                                   ACT.Copy).then_inc(x_copied, 1)
                    act.wait_ge(taps, g * 16 + 16)
                    act.activation(sg[:, :, :], xc[:, :, :], ACT.Exp, scale=-1.0).then_inc(sig_exp, 1)
                    act.wait_ge(sig_exp, g * 2 + 1)
                    act.activation(sg[:, :, :], sg[:, :, :], ACT.Copy, bias=1.0).then_inc(sig_one, 1)
                    act.wait_ge(xs_done, g + 1)
                    for k in range(KD):
                        ins = act.activation(x16[:, k, :, 0, :].rearrange("p c (t b) -> p b c t", b=GB),
                                             xs[:, k, :].rearrange("p (b c t) -> p b c t", b=GB, c=TB), ACT.Copy)
                    ins.then_inc(x_hi, 1)
                    act.wait_ge(in_done, g * 2 + 2)
                    act.activation(sg[:, :, :], psum[:, 2048:].rearrange("p (k n) -> p k n", k=KD), ACT.Exp,
                                   scale=-1.0).then_inc(sig_exp, 1)
                    act.wait_ge(sig_exp, g * 2 + 2)
                    act.activation(sg[:, :, :], sg[:, :, :], ACT.Copy, bias=1.0).then_inc(sig_one, 1)
                    act.nop(nofuse=True)
                    for k in range(KD):
                        act.activation(xD[:, k, bass.ds(g * GT, GT)], xs[:, k, :], ACT.Copy, scale=Dp[:, k:k + 1])
                    act.wait_ge(abc_done, g + 1)
                    act.nop(nofuse=True)
                    act.activation(ABC[:, :, bass.ds(g, 1), :].rearrange("p q a t -> p q (a t)"),
                                   psum[:, 0:3 * T].rearrange("p (q t) -> p q t", q=3), ACT.Copy).then_inc(abc_kept, 1)

            @block.gpsimd
            def _(pool):
                pool.memset(xpad[:, :, :, 0:DC - 1], 0.0).then_inc(pad_set, 1)
                with pool.Fori(0, NG) as g:
                    pool.wait_ge(x_hi, g + 1)
                    for k in range(KD):
                        v = x16[:, k, :, :, :].rearrange("p c h (t b) -> p h b c t", b=GB)
                        ins = pool.tensor_tensor(v[:, 1], xs[:, k, :].rearrange("p (b c t) -> p b c t", b=GB, c=TB),
                                                 v[:, 0], ALU.subtract)
                    ins.then_inc(x_lo, 1)

            @block.vector
            def _(dve):
                dve.sem_inc(xtm_kept, 4)
                dve.wait_ge(ss_in, 128)
                with dve.Fori(0, NG) as g:
                    dve.wait_ge(x_copied, g + 1)
                    dve.wait_ge(abc_kept, g + 1)
                    for k in range(KD):
                        dve.tensor_scalar(xc[:, k, :].rearrange("p (b t) -> p b t", b=GB), xpad[:, k, :, DC - 1:],
                                          cw[:, k, DC - 1:DC], cb[:, k:k + 1], ALU.mult, ALU.add).then_inc(taps, 1)
                    for j in range(DC - 1):
                        for k in range(KD):
                            dve.wait_ge(taps, g * 16 + (4 * j + k + 1))
                            v = xc[:, k, :].rearrange("p (b t) -> p b t", b=GB)
                            dve.scalar_tensor_tensor(v, xpad[:, k, :, j:j + T], cw[:, k, j:j + 1], v, ALU.mult,
                                                     ALU.add).then_inc(taps, 1)
                    dve.wait_ge(sig_one, g * 2 + 1)
                    dve.reciprocal(sg[:, :, :], sg[:, :, :]).then_inc(sig_rec, 1)
                    dve.wait_ge(sig_rec, g * 2 + 1)
                    dve.tensor_tensor(xs[:, :, :], xc[:, :, :], sg[:, :, :], ALU.mult).then_inc(xs_done, 1)
                    dve.wait_ge(sig_one, g * 2 + 2)
                    dve.reciprocal(sg[:, :, :], sg[:, :, :]).then_inc(sig_rec, 1)
                    dve.wait_ge(sig_rec, g * 2 + 2)
                    dve.tensor_tensor(zs[:, :, bass.ds(g * GT, GT)], psum[:, 2048:].rearrange("p (k n) -> p k n", k=KD),
                                      sg[:, :, :], ALU.mult).then_inc(zs_done, 1)
                    for q in range(4):
                        dve.wait_ge(x_turned, g * 4 + (q + 1))
                        dve.tensor_copy(Xtm[:, bass.ds(g * TB + 2 * q, 2), :].rearrange("p a c -> p (a c)"),
                                        bank(psum, 4 + q).bitcast(F16)).then_inc(xtm_kept, 1)

        NS = 8 * NG
        sel = sb("sel", [P, 8, P], F16)
        m8 = sb("m8", [P, GB])
        w = [sb(f"dtw{n}", [P, NG * T]) for n in range(6)]
        dec = sb("dec", [P, NG, T])
        Bb = sb("Bb", [P, NG, T])
        decb = sb("decb", [P, NG, 8])
        Bbb = sb("Bbb", [P, NG, 8])
        LC = sb("LC", [P, NG, 8, GB])
        h1 = [sb(f"h1_{g}", [P, DI]) for g in range(NG)]
        h2 = [sb(f"h2_{g}", [P, DI]) for g in range(NG)]
        hs = [[sb(f"hs_{g}_{n}", [P, DI]) for n in range(2)] for g in range(NG)]
        yb = sb("yb", [P, NG, 8, KD, GB])
        psU = [bank(psum, g) for g in range(NG)]
        psY = psum[:, 4 * 512:4 * 512 + NG * 8 * KD * GB]
        psW = [bank(psum, 6, C), bank(psum, 7, C)]

        sel_in = sem("sel_in")
        dt_step = sem("dt_step")
        dt_exp = sem("dt_exp")
        scal_a = sem("scal_a")
        lc_done = sem("lc_done")
        u_done = sem("ss_u_done")
        h1_done = sem("h1_done")
        h2_done = sem("h2_done")
        clipped = sem("clipped")
        y_done = sem("ss_y_done")
        yb_kept = sem("yb_kept")
        gated = sem("gated")
        y_ready = sem("y_ready")
        out_done = sem("ss_out_done")
        x2_added = sem("x2_added")
        block = ctx.enter_context(nc.Block())

        @block.sync
        def _(sp):
            sp.dma_start(sel[:, :, :], a["sel"]).then_inc(sel_in, 16)
            sp.dma_start(m8[:, :], a["m8"]).then_inc(sel_in, 16)

        @block.vector
        def _(dve):
            dve.sem_inc(h2_done, 4)
            for g in range(NG):
                dve.memset(hs[g][1][:, :], 0.0).then_inc(clipped, 1)
            n = [0]

            def step(ins):
                ins.then_inc(dt_step, 1)
                n[0] += 1

            def last():
                dve.wait_ge(dt_step, n[0])

            step(dve.tensor_scalar(w[0][:, :], ABC[:, 2, :, :].rearrange("p g t -> p (g t)"), 0.0, None, ALU.min))
            dve.wait_ge(dt_exp, 1)
            step(dve.tensor_scalar(w[2][:, :], w[1][:, :], 2.0, None, ALU.add))
            last()
            step(dve.reciprocal(w[3][:, :], w[2][:, :]))
            last()
            step(dve.tensor_tensor(w[4][:, :], w[1][:, :], w[3][:, :], ALU.mult))
            last()
            step(dve.tensor_tensor(w[5][:, :], w[4][:, :], w[4][:, :], ALU.mult))
            last()
            step(dve.tensor_scalar(w[2][:, :], w[5][:, :], 1.0 / 9, 1.0 / 7, ALU.mult, ALU.add))
            last()
            step(dve.tensor_tensor(w[3][:, :], w[2][:, :], w[5][:, :], ALU.mult))
            last()
            step(dve.scalar_tensor_tensor(w[2][:, :], w[3][:, :], 1.0 / 5, w[5][:, :], ALU.add, ALU.mult))
            last()
            step(dve.scalar_tensor_tensor(w[3][:, :], w[2][:, :], 1.0 / 3, w[5][:, :], ALU.add, ALU.mult))
            last()
            step(dve.scalar_tensor_tensor(w[2][:, :], w[3][:, :], 1.0, w[4][:, :], ALU.add, ALU.mult))
            last()
            step(dve.tensor_scalar(w[3][:, :], w[2][:, :], 2.0, 0.001, ALU.mult, ALU.max))
            last()
            step(dve.tensor_scalar(w[0][:, :], w[3][:, :], 0.1, None, ALU.min))
            last()
            step(dve.tensor_scalar(w[2][:, :], w[0][:, :], eA[:, 0:1], 20.0, ALU.mult, ALU.min))
            step(dve.tensor_tensor(w[3][:, :], w[0][:, :], ABC[:, 0, :, :].rearrange("p g t -> p (g t)"), ALU.mult))
            last()
            step(dve.tensor_scalar(w[4][:, :], w[2][:, :], 0.0, None, ALU.max))
            step(dve.tensor_scalar(Bb[:, :, :].rearrange("p g t -> p (g t)"), w[3][:, :], 10.0, -10.0, ALU.min, ALU.max))
            assert n[0] == 16
            dve.wait_ge(sel_in, 32)

            with dve.Fori(0, TB) as i:
                def clip(k, i=i):
                    t, g = divmod(k, NG)
                    dve.wait_ge(h2_done, i * NS + (k + 1 + 4))
                    dve.wait_ge(y_done, i * NS + (k + 1))
                    dve.tensor_scalar(hs[g][t % 2][:, :], h2[g][:, :], 100.0, -100.0, ALU.min,
                                      ALU.max).then_inc(clipped, 1)

                dve.wait_ge(y_done, i * NS + 8)
                dve.tensor_tensor(LC[:, :, :, :],
                                  ABC[:, 1, :, bass.ds(i * 8, 8)][:, :, :, None].to_broadcast([P, NG, 8, GB]),
                                  m8[:, :][:, None, None, :].to_broadcast([P, NG, 8, GB]),
                                  ALU.mult).then_inc(lc_done, 1)
                for k in range(NS):
                    t, g = divmod(k, NG)
                    if k == 0:
                        dve.wait_ge(scal_a, i + 1)
                    dve.wait_ge(u_done, i * NS + (k + 1))
                    dve.wait_ge(h1_done, i * NS + (k + 1))
                    dve.scalar_tensor_tensor(h2[g][:, :], psU[g], Bbb[:, g, t:t + 1], h1[g][:, :], ALU.mult,
                                             ALU.add).then_inc(h2_done, 1)
                    if k:
                        clip(k - 1)
                clip(NS - 1)

            for p in range(NPAIR):
                dve.wait_ge(out_done, p + 1)
                dve.tensor_tensor(X[:, p, :], psW[p % 2], X[:, p, :], ALU.add).then_inc(x2_added, 1)

        @block.scalar
        def _(act):
            act.sem_inc(yb_kept, 1)
            act.wait_ge(dt_step, 1)
            act.activation(w[1][:, :], w[0][:, :], ACT.Exp).then_inc(dt_exp, 1)
            act.wait_ge(dt_step, 16)
            act.activation(dec[:, :, :].rearrange("p g t -> p (g t)"), w[4][:, :], ACT.Exp, scale=-1.0)\
               .then_inc(dt_exp, 1)
            act.wait_ge(dt_exp, 2)
            with act.Fori(0, TB) as i:
                act.wait_ge(clipped, i * NS + 4)
                act.nop(nofuse=True)
                act.activation(decb[:, :, :], dec[:, :, bass.ds(i * 8, 8)], ACT.Copy)
                act.activation(Bbb[:, :, :], Bb[:, :, bass.ds(i * 8, 8)], ACT.Copy).then_inc(scal_a, 1)
                act.wait_ge(scal_a, i + 1)
                for k in range(NS):
                    t, g = divmod(k, NG)
                    act.wait_ge(clipped, i * NS + (k + 1))
                    act.activation(h1[g][:, :], hs[g][(t + 1) % 2][:, :], ACT.Copy,
                                   scale=decb[:, g, t:t + 1]).then_inc(h1_done, 1)
                act.wait_ge(y_done, i * NS + (NS + 8))
                act.wait_ge(gated, i * 4 + 4)
                act.activation(yb[:, :, :, :, :].rearrange("p g t k b -> p (g t k b)"), psY, ACT.Copy)\
                   .then_inc(yb_kept, 1)

        @block.gpsimd
        def _(pool):
            pool.sem_inc(gated, 4)
            with pool.Fori(0, TB) as i:
                for g in range(NG):
                    def span(v, g=g, i=i):
                        return v[:, :, g * GT:(g + 1) * GT].rearrange("p k (b t) -> p k b t", b=GB)[:, :, :, bass.ds(i * 8, 8)]
                    z = span(zs)
                    if g == 0:
                        pool.wait_ge(yb_kept, i + 2)
                    pool.tensor_tensor(z, z, yb[:, g, :, :, :].rearrange("p t k b -> p k b t"), ALU.mult)\
                        .then_inc(gated, 1)
                for g in range(NG):
                    z, x = (v[:, :, g * GT:(g + 1) * GT].rearrange("p k (b t) -> p k b t", b=GB)[:, :, :, bass.ds(i * 8, 8)]
                            for v in (zs, xD))
                    pool.wait_ge(gated, i * 4 + (g + 5))
                    pool.tensor_tensor(z, z, x, ALU.add).then_inc(y_ready, 1)

        @block.tensor
        def _(pe):
            pe.sem_inc(y_done, 8)
            pe.wait_ge(sel_in, 32)
            with pe.Fori(0, TB) as i:
                def sums(k, i=i):
                    t, g = divmod(k, NG)
                    if k == 0:
                        pe.wait_ge(lc_done, i + 1)
                        pe.wait_ge(yb_kept, i + 1)
                    pe.wait_ge(clipped, i * NS + (k + 1 + 4))
                    for n in range(KD):
                        at = ((g * 8 + t) * KD + n) * GB
                        ins = pe.matmul(psY[:, at:at + GB], hs[g][t % 2][:, n * P:(n + 1) * P], LC[:, g, t, :],
                                        start=True, stop=True)
                    ins.then_inc(y_done, 1)

                for k in range(NS):
                    t, g = divmod(k, NG)
                    pe.wait_ge(h2_done, i * NS + (k + 1))
                    pe.matmul(psU[g], sel[:, t, :], Xtm[:, bass.ds(i + g * TB, 1), :].rearrange("p a c -> p (a c)"),
                              start=True, stop=True).then_inc(u_done, 1)
                    if k >= 4:
                        sums(k - 4)
                for k in range(NS - 4, NS):
                    sums(k)
            pe.wait_ge(y_ready, 4 * TB)
            for p in range(NPAIR):
                if p >= 2:
                    pe.wait_ge(x2_added, p - 1)
                for k in range(KD):
                    ins = pe.matmul(psW[p % 2], zs[:, k, p * PAIR_TOK:(p + 1) * PAIR_TOK], Wout[:, k, :],
                                    start=(k == 0), stop=(k == KD - 1))
                ins.then_inc(out_done, 1)


def experts(nc, a, out, sem, tensor_in, psum, X, ident, nhalf, xT):
    norm_phase(nc, "ln3", sem, tensor_in, psum, X, ident, nhalf, xT)
    with ExitStack() as ctx:
        sb = tensor_in(ctx)
        CH = 256
        NCH = B * T // CH
        NB = CH // T
        NPIECE = E + FT
        PW = 2 * DFF
        Whi = sb("Whi", [P, NPIECE, PW], F16)
        Wlo = sb("Wlo", [P, NPIECE, PW], F16)
        gW2 = sb("gW2", [P, 2, E])
        gb1 = sb("gb1", [P, 2])
        gb2b = sb("gb2b", [P, E])
        gb2c = sb("gb2c", [E, 1])
        hs = sb("hs", [P, 2, T])
        hsd = sb("hsd", [P, 2, 2, T])
        G = sb("G", [P, E, T])
        Gt = sb("Gt", [P, E])
        B1 = sb("B1", [P, FT, T])
    
        w_small = sem("ff_w_small")
        piece_in = [sem("piece_in0"), sem("piece_in1")]
        piece_hi = sem("piece_hi")
        piece_lo = sem("piece_lo")
        gate_h = sem("gate_h")
        gate_relu = sem("gate_relu")
        g_step = sem("g_step")
        g_mm = sem("g_mm")
        g_kept = sem("g_kept")

        with ExitStack() as cs:
            sbs = tensor_in(cs)
            stage = [sbs(f"wstage{n}", [P, PW]) for n in range(2)]
            gW1 = sbs("gW1", [P, 2, C])
            eb1 = sbs("eb1", [E, DFF])
            eb2 = sbs("eb2", [E, C])
            G8 = sbs("G8", [E, PAIR_TOK])
            gW2w = sbs("gW2w", [P, 2, E, P])
            Hr = sbs("Hr", [P, 4, 512])
            block = cs.enter_context(nc.Block())

            @block.sync
            def _(sp):
                sp.dma_start(gW1[:, :, :], a["gW1T"].rearrange("(k p) n -> p k n", p=P)).then_inc(w_small, 16)
                with nc.allow_non_contiguous_dma(reason="small parameters"):
                    sp.dma_start(gW2[:, :, :], a["gW2T"].rearrange("(k p) n -> p k n", p=P)).then_inc(w_small, 16)
                    sp.dma_start(gb1[:, :], a["gb1"].rearrange("(k p) -> p k", p=P)).then_inc(w_small, 16)
                    sp.dma_start(gb2c[:, :], a["gb2"].rearrange("(e o) -> e o", o=1)).then_inc(w_small, 16)
                sp.dma_start(gb2b[:, :], a["gb2"].partition_broadcast(P)).then_inc(w_small, 16)
                sp.dma_start(eb1[:, :], a["eb1"]).then_inc(w_small, 16)
                sp.dma_start(eb2[:, :], a["eb2"]).then_inc(w_small, 16)
                with sp.Fori(0, NPIECE // 2) as i:
                    for u in range(2):
                        sp.wait_ge(piece_lo, i * 2 + (u + 1))
                        sp.dma_start(stage[u][:, :], a["WF"][bass.ds(i * 2 + u, 1)].rearrange("a p n -> (a p) n"))\
                            .then_inc(piece_in[u], 16)

            @block.scalar
            def _(act):
                act.wait_ge(w_small, 112)
                for n in range(8):
                    m, c = divmod(n, 4)
                    act.wait_ge(gate_h, n + 1)
                    if n == 4:
                        act.wait_ge(g_step, 2)
                    act.activation(Hr[:, c, :], bank(psum, n % 2), ACT.Relu, bias=gb1[:, m:m + 1])\
                        .then_inc(gate_relu, 1)
                with act.Fori(0, NPIECE // 2) as i:
                    for u in range(2):
                        act.wait_ge(piece_in[u], i * 16 + 16)
                        act.nop(nofuse=True)
                        act.activation(Whi[:, bass.ds(i * 2 + u, 1), :].rearrange("p a n -> p (a n)"), stage[u][:, :],
                                       ACT.Copy).then_inc(piece_hi, 1)

            @block.vector
            def _(dve):
                dve.sem_inc(piece_lo, 2)
                dve.wait_ge(w_small, 112)
                dve.tensor_copy(gW2w[:, :, :, :], gW2[:, :, :][:, :, :, None].to_broadcast([P, 2, E, P]))\
                   .then_inc(g_step, 1)
                for m in range(2):
                    dve.wait_ge(gate_relu, 4 * m + 4)
                    dve.tensor_reduce(hs[:, m, :], Hr[:, :, :].rearrange("p c (b t) -> p t (c b)", t=T), AX_X,
                                      ALU.add).then_inc(g_step, 1)
                dve.wait_ge(g_step, 3)
                dve.tensor_scalar(hsd[:, :, :, :].rearrange("p m d t -> p m d t"),
                                  hs[:, :, :][:, :, None, :].to_broadcast([P, 2, 2, T]), 1.0 / B, None,
                                  ALU.mult).then_inc(g_step, 1)
                dve.wait_ge(g_mm, 1)
                dve.tensor_tensor(G[:, :, :], bank(psum, 2).rearrange("p (e t) -> p e t", e=E),
                                  gb2b[:, :][:, :, None].to_broadcast([P, E, T]), ALU.add).then_inc(g_kept, 1)
                dve.wait_ge(g_mm, 2)
                dve.tensor_tensor(Gt[:, :], bank(psum, 3, E), gb2b[:, :], ALU.add).then_inc(g_kept, 1)
                dve.wait_ge(g_mm, 3)
                dve.tensor_scalar(G8[:, :], psum[0:E, 4 * 512:4 * 512 + PAIR_TOK], gb2c[:, :], None,
                                  ALU.add).then_inc(g_kept, 1)
                dve.wait_ge(g_mm, 4)
                dve.tensor_copy(B1[:, :, :], bank(psum, 5).rearrange("p (f t) -> p f t", f=FT)).then_inc(g_kept, 1)
                dve.wait_ge(g_mm, 5)
                dve.tensor_tensor(X[:, :, :], X[:, :, :], bank(psum, 6, C)[:, None, :].to_broadcast([P, NPAIR, C]), ALU.add)
                with dve.Fori(0, NPIECE // 2) as i:
                    for u in range(2):
                        dve.wait_ge(piece_hi, i * 2 + (u + 1))
                        dve.tensor_tensor(Wlo[:, bass.ds(i * 2 + u, 1), :].rearrange("p a n -> p (a n)"), stage[u][:, :],
                                          Whi[:, bass.ds(i * 2 + u, 1), :].rearrange("p a n -> p (a n)"),
                                          ALU.subtract).then_inc(piece_lo, 1)

            @block.tensor
            def _(pe):
                pe.wait_ge(w_small, 112)
                for n in range(8):
                    m, c = divmod(n, 4)
                    if n >= 2:
                        pe.wait_ge(gate_relu, n - 1)
                    for k in range(2):
                        ins = pe.matmul(bank(psum, n % 2), gW1[:, k, m * P:(m + 1) * P], xT[:, k, c * 512:(c + 1) * 512],
                                        start=(k == 0), stop=(k == 1))
                    ins.then_inc(gate_h, 1)
                pe.wait_ge(g_step, 4)
                for e in range(E):
                    for m in range(2):
                        ins = pe.matmul(bank(psum, 2)[:, e * T:(e + 1) * T], gW2w[:, m, e, :], hsd[:, m, 0, :],
                                        start=(m == 0), stop=(m == 1))
                ins.then_inc(g_mm, 1)
                for m in range(2):
                    ins = pe.matmul(bank(psum, 3, E), hsd[:, m, :, :].rearrange("p d t -> p (d t)"), gW2[:, m, :],
                                    start=(m == 0), stop=(m == 1))
                ins.then_inc(g_mm, 1)
                for m in range(2):
                    ins = pe.matmul(psum[0:E, 4 * 512:4 * 512 + PAIR_TOK], gW2[:, m, :],
                                    hsd[:, m, :, :].rearrange("p d t -> p (d t)"), start=(m == 0), stop=(m == 1))
                ins.then_inc(g_mm, 1)
                pe.wait_ge(g_kept, 3)
                for f in range(FT):
                    ins = pe.matmul(bank(psum, 5)[:, f * T:(f + 1) * T], eb1[:, f * P:(f + 1) * P], G8[:, 0:T],
                                    start=True, stop=True)
                ins.then_inc(g_mm, 1)
                pe.matmul(bank(psum, 6, C), G8[:, :], eb2[:, :], start=True, stop=True).then_inc(g_mm, 1)

        Xg = sb("Xg", [P, E, CH])
        Xhi = sb("Xhi", [P, 2, E, CH], F16)
        Xlo = sb("Xlo", [P, 2, E, CH], F16)
        pre = [sb(f"pre{n}", [P, CH]) for n in range(2)]
        Hhi = sb("Hhi", [P, FT, CH], F16)
        Hlo = sb("Hlo", [P, FT, CH], F16)
        acc = [sb(f"acc{n}", [P, 2, C]) for n in range(2)]

        x_gated = sem("x_gated")
        x_hi = sem("x_hi")
        x_lo = sem("x_lo")
        h_done = sem("h_done")
        h_pre = sem("h_pre")
        h_hi = sem("h_hi")
        h_lo = sem("h_lo")
        u_done = sem("u_done")
        mixed = sem("mixed")
        stored = sem("stored")
        block = ctx.enter_context(nc.Block())
        UA = 8

        @block.tensor
        def _(pe):
            with pe.Fori(0, NCH) as i:
                for f in range(FT):
                    if f == 0:
                        pe.wait_ge(x_lo, i * 2 + 2)
                    pe.wait_ge(h_pre, i * 8 + (f - 1) + 2)
                    ps = bank(psum, f % 2, CH)
                    n = 0
                    for e in range(E):
                        for k in range(2):
                            cols = slice(k * DFF + f * P, k * DFF + (f + 1) * P)
                            for w, x in ((Whi, Xhi), (Whi, Xlo), (Wlo, Xhi)):
                                ins = pe.matmul(ps, w[:, e, cols], x[:, k, e, :], start=(n == 0), stop=(n == 6 * E - 1))
                                n += 1
                    ins.then_inc(h_done, 1)
                pe.wait_ge(h_lo, i * 8 + 8)
                for tt in range(2):
                    tok = slice(tt * P, (tt + 1) * P)
                    for ep in range(4):
                        pe.wait_ge(mixed, i * 16 + (8 * tt + 2 * ep + 2))
                        n = 0
                        for f in range(FT):
                            cols = slice(ep * 512, (ep + 1) * 512)
                            for h, w in ((Hhi, Whi), (Hhi, Wlo), (Hlo, Whi)):
                                ins = pe.matmul(bank(psum, 2 + ep), h[:, f, tok], w[:, E + f, cols],
                                                start=(n == 0), stop=(n == 3 * FT - 1))
                                n += 1
                        ins.then_inc(u_done, 1)

        @block.scalar
        def _(act):
            def split(v):
                for k in range(2):
                    act.wait_ge(x_gated, v(k + 1))
                    act.activation(Xhi[:, k, :, :], Xg[:, :, :], ACT.Copy).then_inc(x_hi, 1)

            split(lambda n: n)
            with act.Fori(0, NCH) as i:
                for f in range(FT):
                    act.wait_ge(h_pre, i * 8 + (f + 1) + 2)
                    act.activation(Hhi[:, f, :], pre[f % 2][:, :], ACT.Relu).then_inc(h_hi, 1)
                split(lambda n: i * 2 + (n + 2))

        @block.vector
        def _(dve):
            def gate_input(step, v):
                for k in range(2):
                    if isinstance(step, int):
                        src = xT[:, k, step * CH:(step + 1) * CH]
                    else:
                        src = xT[:, k, bass.ds(step * CH, CH)]
                    for q in range(NB):
                        ins = dve.tensor_tensor(Xg[:, :, q * T:(q + 1) * T], G[:, :, :],
                                                (xT[:, k, step * CH + q * T:step * CH + (q + 1) * T] if isinstance(step, int)
                                                 else xT[:, k, bass.ds(step * CH + q * T, T)])
                                                [:, None, :].to_broadcast([P, E, T]), ALU.mult)
                    ins.then_inc(x_gated, 1)
                    dve.wait_ge(x_hi, v(k + 1))
                    dve.tensor_tensor(Xlo[:, k, :, :], Xg[:, :, :], Xhi[:, k, :, :], ALU.subtract).then_inc(x_lo, 1)
                    dve.wait_ge(x_lo, v(k + 1))

            dve.sem_inc(h_pre, 2)
            dve.sem_inc(mixed, UA)
            gate_input(0, lambda n: n)
            with dve.Fori(0, NCH) as i:
                for f in range(FT):
                    dve.wait_ge(h_done, i * 8 + (f + 1))
                    dve.tensor_tensor(pre[f % 2][:, :].rearrange("p (b t) -> p b t", t=T),
                                      bank(psum, f % 2, CH).rearrange("p (b t) -> p b t", t=T),
                                      B1[:, f, :][:, None, :].to_broadcast([P, NB, T]), ALU.add).then_inc(h_pre, 1)
                    dve.wait_ge(h_hi, i * 8 + (f + 1))
                    dve.scalar_tensor_tensor(Hlo[:, f, :], pre[f % 2][:, :], 0.0, Hhi[:, f, :], ALU.max,
                                             ALU.subtract).then_inc(h_lo, 1)
                    dve.wait_ge(h_lo, i * 8 + (f + 1))
                gate_input(i + 1, lambda n: i * 2 + (n + 2))
                for tt in range(2):
                    for e in range(E):
                        if e % 2 == 0:
                            dve.wait_ge(u_done, i * 8 + (4 * tt + e // 2 + 1))
                        ps = bank(psum, 2 + e // 2)[:, (e % 2) * C:(e % 2 + 1) * C]
                        src = (X[:, bass.ds(i * 2 + tt, 1), :].rearrange("p a c -> p (a c)") if e == 0
                               else acc[(e - 1) % 2][:, tt, :])
                        if e == 0:
                            dve.wait_ge(stored, i * 16 + 16)
                        else:
                            dve.wait_ge(mixed, i * 16 + (8 * tt + e) + UA)
                        dve.scalar_tensor_tensor(acc[e % 2][:, tt, :], ps, Gt[:, e:e + 1], src, ALU.mult,
                                                 ALU.add).then_inc(mixed, 1)

        @block.sync
        def _(sp):
            sp.sem_inc(stored, 16)
            with sp.Fori(0, NCH) as i:
                sp.wait_ge(mixed, i * 16 + 16 + UA)
                sp.dma_start(out[bass.ds(i * CH, CH), :].rearrange("(n p) c -> p n c", p=P),
                             acc[(E - 1) % 2][:, :, :]).then_inc(stored, 16)
            sp.wait_ge(stored, 16 * (NCH + 1))


def kernel(**inputs):
    import concourse.bacc as bacc
    from concourse.bass_utils import run_bass_kernel_spmd

    given = {k.removeprefix("L0_"): np.asarray(v) for k, v in inputs.items()}
    Wkv, ctx = given["xattn_Wkv"], given["ctx_768"]
    HD = H * DK
    wk, wv = (w.T.reshape(HP, 2, DK, CTX) for w in (Wkv[:, :HD], Wkv[:, HD:]))
    WkS = np.zeros((2, DK, HP, 2, 2 * P), np.float32)
    WvS = np.zeros((2, DK, HP, 3, P), np.float32)
    for h2 in range(2):
        k, v = wk[:, h2].transpose(1, 0, 2), wv[:, h2].transpose(1, 0, 2)
        WkS[h2, :, :, h2, :CTX] = k
        WkS[h2, :, :, h2, CTX:] = k[:, :, P:]
        WvS[h2, :, :, h2] = v[:, :, :P]
        WvS[h2, :, :, 2, h2 * C1:(h2 + 1) * C1] = v[:, :, P:]
    WxT, side = given["attn_W_xproj"].T, P - DS
    WxW = np.zeros((DI, 3, P + side), np.float32)
    WxW[:, 0, side:P] = WxT[:, :DS]
    WxW[:, 1, side:P] = WxT[:, DS:2 * DS]
    WxW[:, 2, side:P] = WxT[:, 2 * DS:]
    eye = np.eye(8, dtype=np.float16)
    sel = np.broadcast_to(eye[:, None, :, None, None] * eye[None, :, None, :, None], (2, 8, 8, 8, 8, DS))
    sel = sel.reshape(P, 8, P)
    w1 = given["ffn_eW1"].reshape(E, DFF, 2, P).transpose(0, 3, 2, 1)
    w2 = given["ffn_eW2"].reshape(E, C, FT, P).transpose(2, 3, 0, 1)
    arrays = {
        "x": given["x"].reshape(B * T, C),
        "ident": np.eye(P, dtype=np.float32),
        "ctxT": ctx.transpose(0, 2, 1),
        "ctxN": ctx[:, :JT * P].reshape(B, JT, P, CTX).transpose(0, 2, 1, 3),
        "ctxR": ctx[:, JT * P:],
        "Wq": given["xattn_Wq"], "WkS": WkS.reshape(P, HP, 2, 2 * P), "WvS": WvS.reshape(P, HP, 3, P),
        "Wproj": given["xattn_Wproj"], "bproj": given["xattn_bproj"],
        "WinT": given["attn_W_in"].T, "convw": given["attn_conv_w"], "convb": given["attn_conv_b"],
        "WxW": WxW, "A_log8": np.tile(given["attn_A_log"], P // DS).reshape(P, 1), "Dp": given["attn_D_param"],
        "sel": sel, "m8": np.repeat(np.eye(P // DS, dtype=np.float32), DS, axis=0),
        "ident16": np.eye(P, dtype=np.float16),
        "WoutT": given["attn_W_out"].T,
        "gW1T": given["ffn_gW1"].T, "gb1": given["ffn_gb1"], "gW2T": given["ffn_gW2"].T, "gb2": given["ffn_gb2"],
        "eb1": given["ffn_eb1"], "eb2": given["ffn_eb2"],
        "WF": np.concatenate([w1.reshape(E, P, 2 * DFF), w2.reshape(FT, P, E * C)]),
    }
    arrays = {f"in_{k}": np.ascontiguousarray(v) for k, v in arrays.items()}
    nc = bacc.Bacc("TRN2", target_bir_lowering=False, num_devices=1)
    a = {k.removeprefix("in_"): nc.dram_tensor(k, v.shape, mybir.dt.from_np(v.dtype), kind="ExternalInput").ap() for k, v in arrays.items()}
    out = nc.dram_tensor("out_0", (B * T, C), F32, kind="ExternalOutput").ap()
    build(nc, a, out)
    r = run_bass_kernel_spmd(nc, [arrays], core_ids=[0])
    return r.results[0]["out_0"].reshape(B, T, C)
```

```python
from contextlib import ExitStack

import numpy as np
import concourse.bass as bass
from concourse import mybir

F32 = mybir.dt.float32
F16 = mybir.dt.float16
ALU = mybir.AluOpType
ACT = mybir.ActivationFunctionType
AX_X = mybir.AxisListType.X

P = 128
B, T, C = 32, 64, 256
J, CTX = 1601, 192
H, DK = 16, 64
HP = H // 2
PAIR_TOK = 2 * T
NPAIR = B // 2
JT = J // P
JR = J - JT * P
JN = JT + 1
C1 = CTX - P
SCALE = DK ** -0.5
EPS = 1e-5

DI, DS, DC = 512, 16, 4
KD = DI // P
XD = 2 * DS + 1
E, DFF = 8, 1024
FT = DFF // P


def bank(psum, i, n=512):
    return psum[:, 512 * i:512 * i + n]


class LayerNorm:

    def __init__(self, nc, ctx, tag, X, ident, psum, xT, nhalf, xn=None):
        def sb(name, shape):
            return ctx.enter_context(nc.sbuf_tensor(f"{tag}_{name}", shape, F32))

        def sem(name):
            return ctx.enter_context(nc.semaphore(f"{tag}_{name}"))

        self.X, self.ident, self.psum, self.xT, self.nhalf = X, ident, psum, xT, nhalf
        self.stats = sb("stats", [P, NPAIR, 6])
        self.diff = sb("diff", [P, NPAIR])
        self.var = sb("var", [P, NPAIR])
        self.mean = sb("mean", [P, NPAIR])
        self.rstd = sb("rstd", [P, NPAIR])
        self.xn = xn if xn is not None else sb("xn", [P, NPAIR, C])
        self.stats_done = sem("stats_done")
        self.var_done = sem("var_done")
        self.rstd_done = sem("rstd_done")
        self.wrapped = sem("wrapped")
        self.normed = sem("normed")
        self.turned = sem("turned")
        self.kept = sem("kept")

    def vector(self, dve):
        st = self.stats
        with dve.Fori(0, NPAIR // 8) as i:
            for u in range(8):
                n = i * 8 + u
                dve.bn_stats(st[:, bass.ds(n, 1), :].rearrange("p a s -> p (a s)"),
                             self.X[:, bass.ds(n, 1), :].rearrange("p a c -> p (a c)")).then_inc(self.stats_done, 1)
        dve.wait_ge(self.stats_done, NPAIR)
        dve.tensor_tensor(self.diff[:, :], st[:, :, 1], st[:, :, 4], ALU.subtract).then_inc(self.stats_done, 1)
        dve.tensor_tensor(self.mean[:, :], st[:, :, 1], st[:, :, 4], ALU.add).then_inc(self.stats_done, 1)
        dve.tensor_tensor(self.var[:, :], st[:, :, 2], st[:, :, 5], ALU.add).then_inc(self.stats_done, 1)
        dve.wait_ge(self.stats_done, NPAIR + 1)
        dve.scalar_tensor_tensor(self.rstd[:, :], self.diff[:, :], 0.25, self.diff[:, :], ALU.mult,
                                 ALU.mult).then_inc(self.stats_done, 1)
        dve.wait_ge(self.stats_done, NPAIR + 4)
        dve.tensor_scalar(self.mean[:, :], self.mean[:, :], 0.5, None, ALU.mult).then_inc(self.stats_done, 1)
        dve.scalar_tensor_tensor(self.diff[:, :], self.var[:, :], 1.0 / C, self.rstd[:, :], ALU.mult,
                                 ALU.add).then_inc(self.stats_done, 1)
        dve.wait_ge(self.stats_done, NPAIR + 6)
        dve.tensor_scalar(self.var[:, :], self.diff[:, :], EPS, None, ALU.add).then_inc(self.var_done, 1)
        dve.wait_ge(self.rstd_done, 1)
        for n in range(NPAIR):
            dve.tensor_scalar(self.xn[:, n, :], self.X[:, n, :], self.mean[:, n:n + 1], self.rstd[:, n:n + 1],
                              ALU.subtract, ALU.mult).then_inc(self.normed, 1)

    def gpsimd(self, pool):
        pool.wait_ge(self.var_done, 1)
        pool.tensor_tensor(self.rstd[:, :], self.var[:, :], self.nhalf[:, :], ALU.pow).then_inc(self.rstd_done, 1)

    def tensor(self, pe):
        for g in range(NPAIR // 2):
            pe.wait_ge(self.normed, 2 * g + 2)
            if g >= 4:
                pe.wait_ge(self.kept, g - 3)
            for n in range(2):
                for k in range(2):
                    ins = pe.transpose(bank(self.psum, 4 + g % 4)[:, (2 * n + k) * P:(2 * n + k + 1) * P],
                                       self.xn[:, 2 * g + n, k * P:(k + 1) * P], self.ident[:, :])
            ins.then_inc(self.turned, 1)

    def scalar(self, act):
        for g in range(NPAIR // 2):
            act.wait_ge(self.turned, g + 1)
            act.activation(self.xT[:, :, 2 * g * P:(2 * g + 2) * P].rearrange("p k (n t) -> p k n t", n=2),
                           bank(self.psum, 4 + g % 4).rearrange("p (n k t) -> p k n t", n=2, k=2),
                           ACT.Copy).then_inc(self.kept, 1)


def build(nc, a, out):
    with ExitStack() as top:
        def sem(name):
            return top.enter_context(nc.semaphore(name))

        def tensor_in(ctx):
            def sb(name, shape, dt=F32):
                return ctx.enter_context(nc.sbuf_tensor(name, shape, dt))
            return sb

        sb = tensor_in(top)
        psum = top.enter_context(nc.psum_tensor("psum", [P, 8 * 512], F32))
        X = sb("X", [P, NPAIR, C])
        ident = sb("ident", [P, P])
        nhalf = sb("nhalf", [P, NPAIR])
        xT = sb("xT", [P, 2, B * T + 2 * PAIR_TOK])

        attention(nc, a, sem, tensor_in, psum, X, ident, nhalf, xT)
        state_space(nc, a, sem, tensor_in, psum, X, ident, nhalf, xT)
        experts(nc, a, out, sem, tensor_in, psum, X, ident, nhalf, xT)


def attention(nc, a, sem, tensor_in, psum, X, ident, nhalf, xT):
    with ExitStack() as ctx:
        sb = tensor_in(ctx)
        Wq = sb("Wq", [P, 2, H * DK])
        WkS = sb("WkS", [P, 2, HP, 2, 2 * P], F16)
        Wvp = sb("Wvp", [P, 2, 3 * HP, C], F16)

        with ExitStack() as cs:
            sbs = tensor_in(cs)
            WvS = sbs("WvS", [P, HP, 3, P])
            Wpr = sbs("Wpr", [P, HP, C])
            Wk32 = sbs("Wk32", [P, HP, 2, 2 * P])
            wk_hi = sem("wk_hi")
            bpr = sbs("bpr", [P, C])
            x_in, w_in = sem("x_in"), sem("w_in")
            half_set, wvp_hi, wvp_done, wvp_kept, bias_in, wrap = (
                sem("half_set"), sem("wvp_hi"), sem("wvp_done"), sem("wvp_kept"), sem("bias_in"), sem("wrap"))
            ln = LayerNorm(nc, cs, "ln1", X, ident, psum, xT, nhalf)
            block = cs.enter_context(nc.Block())

            @block.sync
            def _(sp):
                sp.dma_start(X[:, :, :], a["x"].rearrange("(n p) c -> p n c", p=P)).then_inc(x_in, 16)
                sp.dma_start(ident[:, :], a["ident"]).then_inc(x_in, 16)
                sp.dma_start(bpr[:, :], a["bproj"].partition_broadcast(P)).then_inc(bias_in, 16)
                sp.dma_start(WvS[:, :, :, :], a["WvS"]).then_inc(w_in, 16)
                sp.dma_start(Wpr[:, :, :], a["Wproj"].rearrange("(g p) n -> p g n", p=P)).then_inc(w_in, 16)
                sp.dma_start(Wq[:, :, :], a["Wq"].rearrange("(k p) n -> p k n", p=P)).then_inc(w_in, 16)
                sp.dma_start(Wk32[:, :, :, :], a["WkS"]).then_inc(w_in, 16)
                sp.wait_ge(w_in, 64)

            @block.vector
            def _(dve):
                dve.memset(nhalf[:, :], -0.5).then_inc(half_set, 1)
                dve.wait_ge(x_in, 32)
                ln.vector(dve)
                dve.wait_ge(bias_in, 16)
                dve.wait_ge(ln.normed, NPAIR)
                dve.tensor_tensor(X[:, :, :], X[:, :, :], bpr[:, :][:, None, :].to_broadcast([P, NPAIR, C]), ALU.add)
                dve.wait_ge(w_in, 64)
                dve.wait_ge(wk_hi, 1)
                dve.tensor_tensor(WkS[:, 1, :, :, :], Wk32[:, :, :, :], WkS[:, 0, :, :, :], ALU.subtract)
                for g in range(HP):
                    for s in range(3):
                        n = 3 * g + s
                        k = 2 * g + s if s < 2 else H + g
                        dve.wait_ge(wvp_hi, n + 1)
                        dve.tensor_tensor(Wvp[:, 1, k, :], bank(psum, 2 + n % 2, C), Wvp[:, 0, k, :],
                                          ALU.subtract).then_inc(wvp_kept, 1)

            @block.gpsimd
            def _(pool):
                pool.wait_ge(half_set, 1)
                ln.gpsimd(pool)
                pool.wait_ge(ln.kept, 1)
                pool.tensor_copy(xT[:, :, B * T:B * T + PAIR_TOK], xT[:, :, 0:PAIR_TOK]).then_inc(wrap, 1)

            @block.tensor
            def _(pe):
                pe.wait_ge(x_in, 32)
                ln.tensor(pe)
                pe.wait_ge(w_in, 64)
                for g in range(HP):
                    for s in range(3):
                        n = 3 * g + s
                        if n >= 2:
                            pe.wait_ge(wvp_kept, n - 1)
                        pe.matmul(bank(psum, 2 + n % 2, C), WvS[:, g, s, :], Wpr[:, g, :],
                                  start=True, stop=True).then_inc(wvp_done, 1)

            @block.scalar
            def _(act):
                ln.scalar(act)
                act.wait_ge(w_in, 64)
                act.activation(WkS[:, 0, :, :, :], Wk32[:, :, :, :], ACT.Copy).then_inc(wk_hi, 1)
                for g in range(HP):
                    for s in range(3):
                        n = 3 * g + s
                        act.wait_ge(wvp_done, n + 1)
                        act.activation(Wvp[:, 0, 2 * g + s if s < 2 else H + g, :], bank(psum, 2 + n % 2, C),
                                       ACT.Copy).then_inc(wvp_hi, 1)

        qT = sb("qT", [P, 2, HP, PAIR_TOK], F16)
        Q = [sb(f"Q{i}", [P, 4, 2, H * T], F16) for i in range(2)]
        yN = [sb(f"yN{i}", [P, JN, 2 * CTX], F16) for i in range(2)]
        yT = [sb(f"yT{i}", [P, 3, J], F16) for i in range(2)]
        stage = [sb(f"stage{i}", [P, J]) for i in range(2)]
        prob = sb("prob", [P, J])
        pT = [sb(f"pT{i}", [P, JN, P], F16) for i in range(2)]
        On = sb("On", [P, 2 * P])
        Olo = sb("Olo", [P, CTX])
        OT = sb("OT", [P, 2, 3 * HP, PAIR_TOK], F16)
        mx = sb("mx", [P, 4])
        nb = sb("nb", [P, 2])
        den = sb("den", [P, 2])
        rden = sb("rden", [P, 2])
        psS = psum[:, 0:2048]
        psT = [bank(psum, 4), bank(psum, 5)]
        psO = bank(psum, 6)
        psM = bank(psum, 7)
        psP = psum[:, 1536:1536 + C]

        loaded = [sem("loaded0"), sem("loaded1")]
        stage_free = [sem("stage0_free"), sem("stage1_free")]
        hi_cut = sem("hi_cut")
        ctx_ready = sem("ctx_ready")
        scored = sem("scored")
        maxed = sem("maxed")
        biased = sem("biased")
        expd = sem("expd")
        recip = sem("recip")
        turned = sem("turned")
        hi_kept = sem("hi_kept")
        lo_kept = sem("lo_kept")
        summed = sem("summed")
        olo_kept = sem("olo_kept")
        normed = sem("normed")
        o_turned = sem("o_turned")
        o_hi = sem("o_hi")
        o_kept = sem("o_kept")
        q_done = sem("q_done")
        q_hi = sem("q_hi")
        q_kept = sem("q_kept")
        qk_done = sem("qk_done")
        qk_hi = sem("qk_hi")
        qk_lo = sem("qk_lo")
        projected = sem("projected")
        x_added = sem("x_added")
        AHEAD, LO_AHEAD, CTX_AHEAD = 16, 4, 2
        GROUPS = [(0, 4), (4, 8), (8, 12), (12, 13)]
        block = ctx.enter_context(nc.Block())

        def per_pair(i, u, n, k):
            return i * (2 * n) + (u * n + k)

        @block.sync
        def _(sp):
            with sp.Fori(0, NPAIR // 2) as i:
                for u in range(2):
                    for b in range(2):
                        be = i * 4 + (2 * u + b)
                        n = 2 * (2 * u + b)
                        yt = a["ctxT"][bass.ds(be, 1)].rearrange("a c j -> (a c) j")
                        yn = a["ctxN"][bass.ds(be, 1)].rearrange("a p m c -> (a p) m c")
                        yr = a["ctxR"][bass.ds(be, 1)].rearrange("a p c -> (a p) c")
                        half = 7 * CTX
                        sp.wait_ge(stage_free[0], i * 8 + (n + 1))
                        sp.dma_start(stage[0][:, :], yt[0:P, :]).then_inc(loaded[0], 16)
                        sp.wait_ge(ctx_ready, i * 8 + (n + CTX_AHEAD))
                        sp.dma_start(stage[1][0:C1, :], yt[P:CTX, :]).then_inc(loaded[1], 16)
                        sp.dma_start(stage[1][C1:P, :], yt[P:CTX, :]).then_inc(loaded[1], 16)
                        sp.wait_ge(stage_free[0], i * 8 + (n + 2))
                        sp.dma_start(stage[0][:, 0:half].rearrange("p (m c) -> p m c", c=CTX),
                                     yn[:, 0:7, :]).then_inc(loaded[0], 16)
                        sp.wait_ge(stage_free[1], i * 4 + (n // 2 + 1))
                        sp.dma_start(stage[1][:, 0:5 * CTX].rearrange("p (m c) -> p m c", c=CTX),
                                     yn[:, 7:12, :]).then_inc(loaded[1], 16)
                        sp.dma_start(stage[1][0:JR, 5 * CTX:6 * CTX], yr).then_inc(loaded[1], 16)

        @block.gpsimd
        def _(pool):
            pool.sem_inc(stage_free[0], 1)
            pool.sem_inc(ctx_ready, CTX_AHEAD)
            with pool.Fori(0, NPAIR // 2) as i:
                for u in range(2):
                    for b in range(2):
                        n = 2 * u + b
                        s0, s1, N_, T_ = stage[0], stage[1], yN[b], yT[b]
                        pool.wait_ge(normed, i * 32 + (AHEAD + (n - 1) * HP))
                        pool.wait_ge(loaded[0], i * 128 + (32 * n + 16))
                        pool.nop(nofuse=True)
                        pool.tensor_copy(T_[:, 0, :], s0[:, :]).then_inc(hi_cut, 1)
                        pool.wait_ge(hi_cut, i * 20 + (5 * n + 1))
                        pool.tensor_tensor(T_[:, 2, :], s0[:, :], T_[:, 0, :], ALU.subtract)\
                            .then_inc(stage_free[0], 1)
                        pool.wait_ge(loaded[1], i * 256 + (64 * n + 32))
                        pool.nop(nofuse=True)
                        pool.tensor_copy(T_[:, 1, :], s1[:, :]).then_inc(hi_cut, 1)
                        pool.wait_ge(hi_cut, i * 20 + (5 * n + 2))
                        pool.tensor_tensor(T_[0:C1, 1, :], s1[0:C1, :], T_[0:C1, 1, :], ALU.subtract)\
                            .then_inc(stage_free[1], 1)
                        v0 = s0[:, 0:7 * CTX].rearrange("p (m c) -> p m c", c=CTX)
                        pool.wait_ge(loaded[0], i * 128 + (32 * n + 32))
                        pool.nop(nofuse=True)
                        pool.tensor_copy(N_[:, 0:7, 0:CTX], v0).then_inc(hi_cut, 1)
                        pool.wait_ge(hi_cut, i * 20 + (5 * n + 3))
                        pool.tensor_tensor(N_[:, 0:7, CTX:], v0, N_[:, 0:7, 0:CTX], ALU.subtract)\
                            .then_inc(stage_free[0], 1)
                        v1 = s1[:, 0:5 * CTX].rearrange("p (m c) -> p m c", c=CTX)
                        vr = s1[0:JR, 5 * CTX:6 * CTX]
                        pool.wait_ge(loaded[1], i * 256 + (64 * n + 64))
                        pool.nop(nofuse=True)
                        pool.tensor_copy(N_[:, 7:12, 0:CTX], v1).then_inc(hi_cut, 1)
                        pool.tensor_copy(N_[0:JR, 12, 0:CTX], vr).then_inc(hi_cut, 1)
                        pool.wait_ge(hi_cut, i * 20 + (5 * n + 5))
                        pool.tensor_tensor(N_[:, 7:12, CTX:], v1, N_[:, 7:12, 0:CTX], ALU.subtract)\
                            .then_inc(ctx_ready, 1)
                        pool.tensor_tensor(N_[0:JR, 12, CTX:], vr, N_[0:JR, 12, 0:CTX], ALU.subtract)\
                            .then_inc(ctx_ready, 1)

        @block.tensor
        def _(pe):
            def q_half(pair, half, misc_free):
                misc_free()
                for g in range(4):
                    for k in range(2):
                        ins = pe.matmul(psM[:, g * P:(g + 1) * P],
                                        Wq[:, k, (4 * half + g) * P:(4 * half + g + 1) * P],
                                        xT[:, k, bass.ds(pair * PAIR_TOK, PAIR_TOK)]
                                        if not isinstance(pair, int) else
                                        xT[:, k, pair * PAIR_TOK:(pair + 1) * PAIR_TOK],
                                        start=(k == 0), stop=(k == 1))
                ins.then_inc(q_done, 1)

            def qk_group(g, misc_free):
                misc_free()
                for c in range(2):
                    for h2 in range(2):
                        for n, (w, q) in enumerate([(0, 0), (0, 1), (1, 0)]):
                            ins = pe.matmul(psM[:, (2 * c + h2) * P:(2 * c + h2 + 1) * P],
                                            WkS[:, w, g, h2, c * P:(c + 1) * P], qT[:, q, g, :],
                                            start=(n == 0), stop=(n == 2))
                ins.then_inc(qk_done, 1)

            def wait_for(s, v):
                return lambda: pe.wait_ge(s, v)

            q_half(0, 0, lambda: None)
            q_half(0, 1, wait_for(q_kept, 1))
            pe.wait_ge(q_kept, 2)
            for g in range(HP):
                qk_group(g, wait_for(qk_lo, g) if g else (lambda: None))

            with pe.Fori(0, NPAIR // 2) as i:
                for u in range(2):
                    nxt = i * 2 + (u + 1)

                    def at(n, k, u=u, i=i):
                        return per_pair(i, u, n, k)

                    def score(t, chunks, u=u, at=at):
                        b, tt = divmod(t, HP)
                        if 0 in chunks:
                            if tt == 0:
                                pe.wait_ge(ctx_ready, at(4, 2 * b + 2) + CTX_AHEAD)
                            if t == 0:
                                pe.wait_ge(qk_lo, at(8, 8))
                            if t > 0:
                                pe.wait_ge(expd, at(16, t))
                        for c in chunks:
                            lo, hi = 512 * c, min(J, 512 * (c + 1))
                            if t == 0 and c == 3:
                                pe.wait_ge(x_added, at(1, 1))
                            for n, (q, y) in enumerate([(0, 0), (1, 1), (0, 2), (2, 0), (3, 1)]):
                                ins = pe.matmul(psS[:, lo:hi], Q[u][:, q, b, tt * P:(tt + 1) * P],
                                                yT[b][:, y, lo:hi], start=(n == 0), stop=(n == 4))
                            if c in (1, 3):
                                ins.then_inc(scored, 1)

                    def turn(t, g, at=at):
                        if g == 0:
                            pe.wait_ge(expd, at(16, t + 1))
                        pe.wait_ge(lo_kept, at(64, 4 * t + g - 1) + LO_AHEAD)
                        lo, hi = GROUPS[g]
                        for n in range(lo, hi):
                            w = P if n < JT else JR
                            ins = pe.transpose(psT[g % 2][0:w, (n - lo) * P:(n - lo + 1) * P],
                                               prob[:, n * P:n * P + w], ident[:, :])
                        ins.then_inc(turned, 1)

                    def gather(t, at=at):
                        b = t // HP
                        pe.wait_ge(normed, at(16, t) + AHEAD)
                        for n in range(JN):
                            k = P if n < JT else JR
                            if n % 4 == 0:
                                pe.wait_ge(lo_kept, at(64, 4 * t + n // 4 + 1) + LO_AHEAD)
                            pe.matmul(psO[:, 0:2 * CTX], pT[0][0:k, n, :], yN[b][0:k, n, :],
                                      start=(n == 0), stop=False)
                            ins = pe.matmul(psO[:, 0:CTX], pT[1][0:k, n, :], yN[b][0:k, n, 0:CTX],
                                            start=False, stop=(n == JN - 1))
                        ins.then_inc(summed, 1)

                    def turn_o(t, misc_free, at=at):
                        pe.wait_ge(normed, at(16, t + 1) + AHEAD)
                        misc_free()
                        for k in range(2):
                            ins = pe.transpose(psM[:, k * P:(k + 1) * P], On[:, k * P:(k + 1) * P], ident[:, :])
                        ins.then_inc(o_turned, 1)

                    def project(chunks, first=False, last=False):
                        for n, k in enumerate(chunks):
                            for m, (o, w) in enumerate([(0, 0), (0, 1), (1, 0)]):
                                ins = pe.matmul(psP, OT[:, o, k, :], Wvp[:, w, k, :], start=(first and n == m == 0),
                                                stop=(last and n == len(chunks) - 1 and m == 2))
                        if last:
                            ins.then_inc(projected, 1)

                    def o_free(t, at=at):
                        return wait_for(o_kept, at(16, t) + AHEAD)

                    def qk_free(n, at=at):
                        return wait_for(qk_lo, at(8, n) + 8)

                    def q_free(n, at=at):
                        return wait_for(q_kept, at(2, n) + 2)

                    score(0, [0, 1])
                    q_half(nxt, 0, o_free(0))
                    score(0, [2, 3])
                    q_half(nxt, 1, q_free(1))
                    for t in range(1, 16):
                        turn(t - 1, 0)
                        turn(t - 1, 1)
                        score(t, [0])
                        turn(t - 1, 2)
                        score(t, [1])
                        turn(t - 1, 3)
                        score(t, [2, 3])
                        if t >= 2:
                            turn_o(t - 2, q_free(2) if t == 2 else qk_free(t - 2) if t <= 9 else o_free(t - 2))
                        gather(t - 1)
                        if 2 <= t <= 8:
                            qk_group(t - 2, o_free(t - 1))
                    turn(15, 0)
                    turn(15, 1)
                    pe.wait_ge(o_kept, at(16, 14) + AHEAD)
                    pe.wait_ge(expd, at(16, 16))
                    project(range(0, 6), first=True)
                    turn(15, 2)
                    turn(15, 3)
                    qk_group(7, o_free(14))
                    gather(15)
                    turn_o(14, qk_free(8))
                    project(range(6, 12))
                    pe.wait_ge(o_kept, at(16, 15) + AHEAD)
                    turn_o(15, lambda: None)
                    project([12, 13] + list(range(16, 23)))
                    pe.wait_ge(o_kept, at(16, 16) + AHEAD)
                    project([14, 15, 23], last=True)

        @block.scalar
        def _(act):
            def q_copy(half, v):
                act.wait_ge(q_done, v)
                act.activation(qT[:, 0, 4 * half:4 * half + 4, :], psM.rearrange("p (g t) -> p g t", g=4),
                               ACT.Copy).then_inc(q_hi, 1)

            def qk_high(g, dst, v):
                act.wait_ge(qk_done, v)
                for c in range(2):
                    ins = act.activation(dst[:, c, :, 2 * g * T:(2 * g + 2) * T].rearrange("p b (h t) -> p h b t", h=2),
                                         psM[:, 2 * c * P:(2 * c + 2) * P].rearrange("p (h b t) -> p h b t", h=2, b=2),
                                         ACT.Copy)
                ins.then_inc(qk_hi, 1)

            q_copy(0, 1)
            q_copy(1, 2)
            for g in range(HP):
                qk_high(g, Q[0], g + 1)

            with act.Fori(0, NPAIR // 2) as i:
                for u in range(2):
                    def at(n, k, u=u, i=i):
                        return per_pair(i, u, n, k)

                    def exponentials(t, at=at):
                        act.wait_ge(biased, at(16, t + 1))
                        act.activation(prob[:, :], psS[:, 0:J], ACT.Exp, bias=nb[:, t % 2:t % 2 + 1], scale=SCALE,
                                       accum_out=den[:, t % 2:t % 2 + 1]).then_inc(expd, 1)

                    def high(t, groups=range(4), at=at):
                        for g in groups:
                            lo, hi = GROUPS[g]
                            act.wait_ge(turned, at(64, 4 * t + g + 1))
                            w = P if g < 3 else JR
                            act.activation(pT[0][0:w, lo:hi, :],
                                           psT[g % 2][0:w, 0:(hi - lo) * P].rearrange("p (n h) -> p n h", h=P),
                                           ACT.Copy).then_inc(hi_kept, 1)

                    def sum_low(t, at=at):
                        act.wait_ge(summed, at(16, t + 1))
                        act.wait_ge(recip, at(16, t + 1))
                        act.activation(Olo[:, :], psO[:, CTX:2 * CTX], ACT.Copy,
                                       scale=rden[:, t % 2:t % 2 + 1]).then_inc(olo_kept, 1)

                    def o_copy(t, at=at):
                        b, tt = divmod(t, HP)
                        act.wait_ge(o_turned, at(16, t + 1))
                        if t == 0:
                            act.wait_ge(x_added, at(1, 1))
                        tok = slice(b * T, (b + 1) * T)
                        act.activation(OT[:, 0, 2 * tt:2 * tt + 2, tok], psM[:, 0:P].rearrange("p (h t) -> p h t", h=2),
                                       ACT.Copy)
                        act.activation(OT[0:C1, 0, H + tt, tok], psM[0:C1, P:P + T], ACT.Copy)
                        act.activation(OT[C1:P, 0, H + tt, tok], psM[C1:P, P + T:2 * P], ACT.Copy).then_inc(o_hi, 1)

                    q_copy(0, at(2, 1) + 2)
                    exponentials(0)
                    q_copy(1, at(2, 2) + 2)
                    for t in range(1, 16):
                        high(t - 1, (0, 1))
                        if 3 <= t <= 9:
                            qk_high(t - 3, Q[1 - u], at(8, t - 2) + 8)
                        high(t - 1, (2, 3))
                        if t >= 2:
                            o_copy(t - 2)
                        exponentials(t)
                        sum_low(t - 1)
                    high(15)
                    qk_high(7, Q[1 - u], at(8, 8) + 8)
                    sum_low(15)
                    o_copy(14)
                    o_copy(15)

        @block.vector
        def _(dve):
            dve.sem_inc(normed, AHEAD)
            dve.sem_inc(o_kept, AHEAD)
            dve.sem_inc(x_added, 1)
            dve.sem_inc(lo_kept, LO_AHEAD)

            def q_low(half, v):
                dve.wait_ge(q_hi, v)
                dve.tensor_tensor(qT[:, 1, 4 * half:4 * half + 4, :], psM.rearrange("p (g t) -> p g t", g=4),
                                  qT[:, 0, 4 * half:4 * half + 4, :], ALU.subtract).then_inc(q_kept, 1)

            def qk_low(g, dst, v):
                dve.wait_ge(qk_hi, v)
                for c in range(2):
                    hi, lo = (dst[:, s, :, 2 * g * T:(2 * g + 2) * T].rearrange("p b (h t) -> p h b t", h=2)
                              for s in (c, 2 + c))
                    ins = dve.tensor_tensor(lo, psM[:, 2 * c * P:(2 * c + 2) * P].rearrange("p (h b t) -> p h b t", h=2, b=2),
                                            hi, ALU.subtract)
                ins.then_inc(qk_lo, 1)

            q_low(0, 1)
            q_low(1, 2)
            for g in range(HP):
                qk_low(g, Q[0], g + 1)

            with dve.Fori(0, NPAIR // 2) as i:
                for u in range(2):
                    pair = i * 2 + u

                    def at(n, k, u=u, i=i):
                        return per_pair(i, u, n, k)

                    def maximum(t, at=at):
                        for n, (lo, hi) in enumerate([(0, 1024), (1024, J)]):
                            if t == 0 and n == 1:
                                q_low(0, at(2, 1) + 2)
                            dve.wait_ge(scored, at(32, 2 * t + n + 1))
                            dve.tensor_reduce(mx[:, 2 * (t % 2) + n:2 * (t % 2) + n + 1], psS[:, lo:hi], AX_X,
                                              ALU.max).then_inc(maxed, 1)
                        dve.wait_ge(maxed, at(32, 2 * t + 2))
                        m = 2 * (t % 2)
                        dve.tensor_scalar(nb[:, t % 2:t % 2 + 1], mx[:, m:m + 1], mx[:, m + 1:m + 2], -SCALE,
                                          ALU.max, ALU.mult).then_inc(biased, 1)

                    def low(t, groups=range(4), at=at):
                        for g in groups:
                            lo, hi = GROUPS[g]
                            dve.wait_ge(hi_kept, at(64, 4 * t + g + 1))
                            w = P if g < 3 else JR
                            dve.tensor_tensor(pT[1][0:w, lo:hi, :],
                                              psT[g % 2][0:w, 0:(hi - lo) * P].rearrange("p (n h) -> p n h", h=P),
                                              pT[0][0:w, lo:hi, :], ALU.subtract).then_inc(lo_kept, 1)

                    def o_low(t, at=at):
                        b, tt = divmod(t, HP)
                        dve.wait_ge(o_hi, at(16, t + 1))
                        tok = slice(b * T, (b + 1) * T)
                        dve.tensor_tensor(OT[:, 1, 2 * tt:2 * tt + 2, tok], psM[:, 0:P].rearrange("p (h t) -> p h t", h=2),
                                          OT[:, 0, 2 * tt:2 * tt + 2, tok], ALU.subtract)
                        dve.tensor_tensor(OT[0:C1, 1, H + tt, tok], psM[0:C1, P:P + T], OT[0:C1, 0, H + tt, tok],
                                          ALU.subtract)
                        dve.tensor_tensor(OT[C1:P, 1, H + tt, tok], psM[C1:P, P + T:2 * P], OT[C1:P, 0, H + tt, tok],
                                          ALU.subtract).then_inc(o_kept, 1)

                    def reciprocal(t, at=at):
                        dve.wait_ge(expd, at(16, t + 1))
                        dve.reciprocal(rden[:, t % 2:t % 2 + 1], den[:, t % 2:t % 2 + 1]).then_inc(recip, 1)

                    def normalise(t, at=at):
                        dve.wait_ge(olo_kept, at(16, t + 1))
                        if t == 15:
                            dve.wait_ge(o_turned, at(16, 15))
                        r = rden[:, t % 2:t % 2 + 1]
                        dve.scalar_tensor_tensor(On[:, 0:CTX], psO[:, 0:CTX], r, Olo[:, :], ALU.mult, ALU.add)
                        dve.scalar_tensor_tensor(On[:, CTX:2 * P], psO[:, P:CTX], r, Olo[:, P:CTX], ALU.mult,
                                                 ALU.add).then_inc(normed, 1)

                    maximum(0)
                    q_low(1, at(2, 2) + 2)
                    reciprocal(0)
                    for t in range(1, 16):
                        low(t - 1, (0, 1))
                        if 3 <= t <= 9:
                            qk_low(t - 3, Q[1 - u], at(8, t - 2) + 8)
                        low(t - 1, (2, 3))
                        maximum(t)
                        if t >= 2:
                            o_low(t - 2)
                        reciprocal(t)
                        normalise(t - 1)
                    low(15)
                    qk_low(7, Q[1 - u], at(8, 8) + 8)
                    normalise(15)
                    o_low(14)
                    o_low(15)
                    dve.wait_ge(projected, at(1, 1))
                    xp = X[:, bass.ds(pair, 1), :].rearrange("p a c -> p (a c)")
                    dve.tensor_tensor(xp, psP, xp, ALU.add).then_inc(x_added, 1)


def norm_phase(nc, tag, sem, tensor_in, psum, X, ident, nhalf, xT):
    with ExitStack() as ctx:
        ln = LayerNorm(nc, ctx, tag, X, ident, psum, xT, nhalf)
        block = ctx.enter_context(nc.Block())

        @block.vector
        def _(dve):
            ln.vector(dve)

        @block.gpsimd
        def _(pool):
            ln.gpsimd(pool)
            pool.wait_ge(ln.kept, 1)
            pool.tensor_copy(xT[:, :, B * T:], xT[:, :, 0:2 * PAIR_TOK]).then_inc(ln.wrapped, 1)

        @block.tensor
        def _(pe):
            ln.tensor(pe)

        @block.scalar
        def _(act):
            ln.scalar(act)


def state_space(nc, a, sem, tensor_in, psum, X, ident, nhalf, xT):
    norm_phase(nc, "ln2", sem, tensor_in, psum, X, ident, nhalf, xT)
    GB = P // DS
    NG = B // GB
    GT = GB * T
    TB = T // 8
    WIN = (2 * GB - 1) * DS
    XR = P
    with ExitStack() as ctx:
        sb = tensor_in(ctx)
        xD = sb("xD", [P, KD, B * T])
        zs = sb("zs", [P, KD, B * T])
        Xtm = sb("Xtm", [P, NG * TB, DI], F16)
        ABC = sb("ABC", [P, 3, NG, T])
        Dp = sb("Dp", [P, KD])
        eA = sb("eA", [P, 1])
        ss_in = sem("ss_in")
        ea_ready = sem("ea_ready")

        with ExitStack() as cs:
            sbs = tensor_in(cs)
            Win = sbs("Win", [P, 2, 2 * DI])
            Wx = sbs("Wx", [P, KD, XR])
            spread = sbs("spread", [XR, 3, WIN])
            xd = sbs("xd", [XR, NG, GB, T])
            cw = sbs("cw", [P, KD, DC])
            cb = sbs("cb", [P, KD])
            ident16 = sbs("ident16", [P, P], F16)
            xpad = sbs("xpad", [P, KD, GB, DC - 1 + T])
            xc = sbs("xc", [P, KD, GT])
            xs = [sbs(f"xs{n}", [P, KD, GT]) for n in range(2)]
            x16 = sbs("x16", [P, KD, TB, 2, 8 * GB], F16)
            in_done = sem("in_done")
            x_copied = sem("x_copied")
            taps = sem("taps")
            z_sig = sem("z_sig")
            x_sig = sem("x_sig")
            xs_done = sem("xs_done")
            zs_done = sem("zs_done")
            x_hi = sem("x16_hi")
            x_lo = sem("x16_lo")
            x_turned = sem("x_turned")
            xtm_kept = sem("xtm_kept")
            xd_done = sem("xd_done")
            xd_kept = sem("xd_kept")
            abc_done = sem("abc_done")
            pad_set = sem("pad_set")
            block = cs.enter_context(nc.Block())

            @block.sync
            def _(sp):
                sp.dma_start(Win[:, :, :], a["WinT"].rearrange("(k p) n -> p k n", p=P)).then_inc(ss_in, 16)
                with nc.allow_non_contiguous_dma(reason="small parameters"):
                    sp.dma_start(cw[:, :, :], a["convw"].rearrange("(k p) n -> p k n", p=P)).then_inc(ss_in, 16)
                    sp.dma_start(cb[:, :], a["convb"].rearrange("(k p) -> p k", p=P)).then_inc(ss_in, 16)
                    sp.dma_start(Dp[:, :], a["Dp"].rearrange("(k p) -> p k", p=P)).then_inc(ss_in, 16)
                sp.dma_start(Wx[:, :, :], a["Wx"].rearrange("(k p) n -> p k n", p=P)).then_inc(ss_in, 16)
                sp.dma_start(spread[:, :, :], a["spread"]).then_inc(ss_in, 16)
                sp.dma_start(eA[:, :], a["A_log8"]).then_inc(ss_in, 16)
                sp.dma_start(ident16[:, :], a["ident16"]).then_inc(ss_in, 16)

            def low(engine, g, tiles):
                engine.wait_ge(x_hi, g + 1)
                for k in tiles:
                    v = x16[:, k, :, :, :].rearrange("p c h (t b) -> p h b c t", b=GB)
                    ins = engine.tensor_tensor(v[:, 1], xs[g % 2][:, k, :].rearrange("p (b c t) -> p b c t", b=GB, c=TB),
                                               v[:, 0], ALU.subtract)
                ins.then_inc(x_lo, 1)

            @block.tensor
            def _(pe):
                def project(g, m):
                    if m == 0 and g:
                        pe.wait_ge(x_copied, g)
                    if m == 0 and g >= 2:
                        pe.wait_ge(xtm_kept, 4 * (g - 1))
                    if m == 1 and g:
                        pe.wait_ge(zs_done, g)
                    for k in (2, 3, 0, 1):
                        if m == 0 and g >= 2 and k == 0:
                            pe.wait_ge(xd_kept, g - 1)
                        for half in range(2):
                            ins = pe.matmul(bank(psum, 4 * m + k),
                                            Win[:, half, (4 * m + k) * P:(4 * m + k + 1) * P],
                                            xT[:, half, g * GT:(g + 1) * GT], start=(half == 0), stop=(half == 1))
                    ins.then_inc(in_done, 1)

                def turn(g, q):
                    half = bank(psum, 1 + q % 3).bitcast(F16)
                    if q == 0:
                        pe.wait_ge(x_lo, 2 * g + 2)
                    if q == 3:
                        pe.wait_ge(xtm_kept, 4 * g + 1)
                    for n in range(2):
                        for k in range(KD):
                            ins = pe.transpose(half[:, (4 * n + k) * P:(4 * n + k + 1) * P],
                                               x16[:, k, 2 * q + n, :, :].rearrange("p h n -> p (h n)"), ident16[:, :])
                    ins.then_inc(x_turned, 1)

                def dbl(g):
                    if g:
                        pe.wait_ge(xd_kept, g)
                    for k in range(KD):
                        ins = pe.matmul(psum[0:XR, 0:GT], Wx[:, k, :], xs[g % 2][:, k, :], start=(k == 0),
                                        stop=(k == KD - 1))
                    ins.then_inc(xd_done, 1)

                pe.wait_ge(ss_in, 128)
                project(0, 0)
                for g in range(NG + 1):
                    if g < NG:
                        project(g, 1)
                    if g:
                        pe.wait_ge(x_copied, min(g + 1, NG))
                        for q in range(3):
                            turn(g - 1, q)
                        dbl(g - 1)
                        turn(g - 1, 3)
                    if g + 1 < NG:
                        project(g + 1, 0)
                pe.wait_ge(xd_kept, NG)
                pe.wait_ge(zs_done, NG)
                for q in range(3):
                    for b in range(GB):
                        lo = (GB - 1 - b) * DS
                        ins = pe.matmul(psum[:, 2048 + q * NG * T:2048 + (q + 1) * NG * T], spread[:, q, lo:lo + P],
                                        xd[:, :, b, :], start=(b == 0), stop=(b == GB - 1))
                ins.then_inc(abc_done, 1)

            @block.scalar
            def _(act):
                act.wait_ge(ss_in, 128)
                act.activation(eA[:, :], eA[:, :], ACT.Exp).then_inc(ea_ready, 1)
                act.wait_ge(pad_set, 1)

                def copy_x(g):
                    act.wait_ge(in_done, 2 * g + 1)
                    if g:
                        act.wait_ge(taps, 16 * g)
                    act.activation(xpad[:, :, :, DC - 1:],
                                   psum[:, 0:2048].rearrange("p (k b t) -> p k b t", k=KD, b=GB),
                                   ACT.Copy).then_inc(x_copied, 1)

                copy_x(0)
                for g in range(NG + 1):
                    if g < NG:
                        act.wait_ge(in_done, 2 * g + 2)
                        act.activation(zs[:, :, g * GT:(g + 1) * GT], psum[:, 2048:].rearrange("p (k n) -> p k n", k=KD),
                                       ACT.Sigmoid).then_inc(z_sig, 1)
                    if g:
                        for q in range(4):
                            act.wait_ge(x_turned, 4 * (g - 1) + q + 1)
                            act.activation(Xtm[:, (g - 1) * TB + 2 * q:(g - 1) * TB + 2 * q + 2, :].rearrange("p a c -> p (a c)"),
                                           bank(psum, 1 + q % 3).bitcast(F16), ACT.Copy).then_inc(xtm_kept, 1)
                        act.wait_ge(xd_done, g)
                        act.activation(xd[:, g - 1, :, :].rearrange("p b t -> p (b t)"), psum[0:XR, 0:GT],
                                       ACT.Copy).then_inc(xd_kept, 1)
                    if g < NG:
                        act.wait_ge(taps, 16 * g + 16)
                        if g >= 2:
                            act.wait_ge(xd_done, g - 1)
                            act.wait_ge(x_lo, 2 * g - 2)
                        act.activation(xs[g % 2][:, :, :], xc[:, :, :], ACT.Sigmoid).then_inc(x_sig, 1)
                    if g + 1 < NG:
                        copy_x(g + 1)
                    if g < NG:
                        act.wait_ge(xs_done, g + 1)
                        for k in range(KD):
                            ins = act.activation(x16[:, k, :, 0, :].rearrange("p c (t b) -> p b c t", b=GB),
                                                 xs[g % 2][:, k, :].rearrange("p (b c t) -> p b c t", b=GB, c=TB), ACT.Copy)
                        ins.then_inc(x_hi, 1)
                        for k in range(KD):
                            act.activation(xD[:, k, g * GT:(g + 1) * GT], xs[g % 2][:, k, :], ACT.Copy, scale=Dp[:, k:k + 1])
                act.wait_ge(abc_done, 1)
                act.activation(ABC[:, :, :, :].rearrange("p q g t -> p (q g t)"), psum[:, 2048:2048 + 3 * NG * T],
                               ACT.Copy)

            @block.gpsimd
            def _(pool):
                pool.memset(xpad[:, :, :, 0:DC - 1], 0.0).then_inc(pad_set, 1)
                for g in range(NG):
                    low(pool, g, (0, 1))

            @block.vector
            def _(dve):
                dve.wait_ge(ss_in, 128)
                for g in range(NG):
                    dve.wait_ge(x_copied, g + 1)
                    if g:
                        dve.wait_ge(xs_done, g)
                    for k in range(KD):
                        dve.tensor_scalar(xc[:, k, :].rearrange("p (b t) -> p b t", b=GB), xpad[:, k, :, DC - 1:],
                                          cw[:, k, DC - 1:DC], cb[:, k:k + 1], ALU.mult, ALU.add).then_inc(taps, 1)
                    for j in range(DC - 1):
                        if j == 1 and g:
                            low(dve, g - 1, (2, 3))
                        for k in range(KD):
                            dve.wait_ge(taps, 16 * g + 4 * j + k + 1)
                            v = xc[:, k, :].rearrange("p (b t) -> p b t", b=GB)
                            dve.scalar_tensor_tensor(v, xpad[:, k, :, j:j + T], cw[:, k, j:j + 1], v, ALU.mult,
                                                     ALU.add).then_inc(taps, 1)
                    dve.wait_ge(z_sig, g + 1)
                    z = zs[:, :, g * GT:(g + 1) * GT]
                    dve.tensor_tensor(z, psum[:, 2048:].rearrange("p (k n) -> p k n", k=KD), z, ALU.mult)\
                       .then_inc(zs_done, 1)
                    dve.wait_ge(x_sig, g + 1)
                    dve.tensor_tensor(xs[g % 2][:, :, :], xc[:, :, :], xs[g % 2][:, :, :], ALU.mult).then_inc(xs_done, 1)
                low(dve, NG - 1, (2, 3))

        NS = 8 * NG
        Wout = sb("Wout", [P, KD, C])
        sel = sb("sel", [P, 8, P], F16)
        m8 = sb("m8", [P, GB])
        w = [sb(f"dtw{n}", [P, NG * T]) for n in range(6)]
        dec = sb("dec", [P, NG, T])
        Bb = sb("Bb", [P, NG, T])
        decb = sb("decb", [P, NG, 8])
        Bbb = sb("Bbb", [P, NG, 8])
        LC = sb("LC", [P, NG, 8 * 9 * GB])
        h1 = [sb(f"h1_{g}", [P, DI]) for g in range(NG)]
        h2 = [sb(f"h2_{g}", [P, DI]) for g in range(NG)]
        hs = [[sb(f"hs_{g}_{n}", [P, DI]) for n in range(2)] for g in range(NG)]
        BT = 8 * GB
        ysb = sb("ysb", [BT, NG, DI])
        yb = sb("yb", [P, NG, KD, 8, GB])
        psU = [bank(psum, n) for n in range(3)]
        psT = bank(psum, 3)
        psY = [psum[0:BT, (4 + g) * 512:(5 + g) * 512] for g in range(NG)]
        psW = [bank(psum, 6, C), bank(psum, 7, C)]

        sel_in = sem("sel_in")
        wout_in = sem("wout_in")
        dt_step = sem("dt_step")
        dt_exp = sem("dt_exp")
        scal_a = sem("scal_a")
        cleared = sem("cleared")
        lc_done = sem("lc_done")
        u_done = sem("ss_u_done")
        h1_done = sem("h1_done")
        h2_done = sem("h2_done")
        clipped = sem("clipped")
        y_done = sem("ss_y_done")
        ysb_kept = sem("ysb_kept")
        y_turned = sem("y_turned")
        yb_kept = sem("yb_kept")
        gated = sem("gated")
        y_ready = sem("y_ready")
        out_done = sem("ss_out_done")
        x2_added = sem("x2_added")
        block = ctx.enter_context(nc.Block())

        @block.sync
        def _(sp):
            sp.dma_start(sel[:, :, :], a["sel"]).then_inc(sel_in, 16)
            sp.dma_start(m8[:, :], a["m8"]).then_inc(sel_in, 16)
            sp.dma_start(Wout[:, :, :], a["WoutT"].rearrange("(k p) n -> p k n", p=P)).then_inc(wout_in, 16)

        @block.vector
        def _(dve):
            dve.sem_inc(h2_done, 4)
            n = [0]

            def step(ins):
                ins.then_inc(dt_step, 1)
                n[0] += 1

            def last():
                dve.wait_ge(dt_step, n[0])

            step(dve.tensor_scalar(w[0][:, :], ABC[:, 2, :, :].rearrange("p g t -> p (g t)"), 0.0, None, ALU.min))
            dve.memset(psum[0:BT, 4 * 512:8 * 512], 0.0).then_inc(cleared, 1)
            dve.wait_ge(dt_exp, 1)
            step(dve.tensor_scalar(w[2][:, :], w[1][:, :], 2.0, None, ALU.add))
            last()
            step(dve.reciprocal(w[3][:, :], w[2][:, :]))
            last()
            step(dve.tensor_tensor(w[4][:, :], w[1][:, :], w[3][:, :], ALU.mult))
            last()
            step(dve.tensor_tensor(w[5][:, :], w[4][:, :], w[4][:, :], ALU.mult))
            last()
            step(dve.tensor_scalar(w[2][:, :], w[5][:, :], 1.0 / 9, 1.0 / 7, ALU.mult, ALU.add))
            last()
            step(dve.tensor_tensor(w[3][:, :], w[2][:, :], w[5][:, :], ALU.mult))
            last()
            step(dve.scalar_tensor_tensor(w[2][:, :], w[3][:, :], 1.0 / 5, w[5][:, :], ALU.add, ALU.mult))
            last()
            step(dve.scalar_tensor_tensor(w[3][:, :], w[2][:, :], 1.0 / 3, w[5][:, :], ALU.add, ALU.mult))
            last()
            step(dve.scalar_tensor_tensor(w[2][:, :], w[3][:, :], 1.0, w[4][:, :], ALU.add, ALU.mult))
            last()
            step(dve.tensor_scalar(w[3][:, :], w[2][:, :], 2.0, 0.001, ALU.mult, ALU.max))
            last()
            step(dve.tensor_scalar(w[0][:, :], w[3][:, :], 0.1, None, ALU.min))
            last()
            step(dve.tensor_scalar(w[2][:, :], w[0][:, :], eA[:, 0:1], 20.0, ALU.mult, ALU.min))
            step(dve.tensor_tensor(w[3][:, :], w[0][:, :], ABC[:, 0, :, :].rearrange("p g t -> p (g t)"), ALU.mult))
            last()
            step(dve.tensor_scalar(w[4][:, :], w[2][:, :], 0.0, None, ALU.max))
            step(dve.tensor_scalar(Bb[:, :, :].rearrange("p g t -> p (g t)"), w[3][:, :], 10.0, -10.0, ALU.min, ALU.max))
            assert n[0] == 16
            dve.wait_ge(sel_in, 32)
            dve.wait_ge(cleared, 2)
            dve.wait_ge(clipped, 4)

            with dve.Fori(0, TB) as i:
                def clip(k, i=i):
                    t, g = divmod(k, NG)
                    dve.wait_ge(h2_done, i * NS + (k + 1 + 4))
                    dve.wait_ge(y_done, i * NS + (k + 1))
                    dve.tensor_scalar(hs[g][t % 2][:, :], h2[g][:, :], 100.0, -100.0, ALU.min,
                                      ALU.max).then_inc(clipped, 1)

                def own_c(half, i=i):
                    lc = LC[:, :, :].rearrange("p g (t r) -> p g t r", r=9 * GB)[:, :, 4 * half:4 * half + 4, 0:GB]
                    dve.tensor_tensor(lc, ABC[:, 1, :, bass.ds(i * 8 + 4 * half, 4)][:, :, :, None].to_broadcast([P, NG, 4, GB]),
                                      m8[:, :][:, None, None, :].to_broadcast([P, NG, 4, GB]),
                                      ALU.mult).then_inc(lc_done, 1)

                own_c(0)
                for k in range(NS):
                    t, g = divmod(k, NG)
                    if k == 8:
                        dve.wait_ge(y_done, i * NS + 8)
                        own_c(1)
                    if k % 16 == 0:
                        dve.wait_ge(scal_a, i * 2 + (k // 16 + 1))
                    dve.wait_ge(u_done, i * NS + (k + 1))
                    dve.wait_ge(h1_done, i * NS + (k + 1))
                    dve.scalar_tensor_tensor(h2[g][:, :], psU[k % 3], Bbb[:, g, t:t + 1], h1[g][:, :], ALU.mult,
                                             ALU.add).then_inc(h2_done, 1)
                    if k:
                        clip(k - 1)
                clip(NS - 1)

            for p in range(NPAIR):
                dve.wait_ge(out_done, p + 1)
                dve.tensor_tensor(X[:, p, :], psW[p % 2], X[:, p, :], ALU.add).then_inc(x2_added, 1)

        @block.scalar
        def _(act):
            act.sem_inc(yb_kept, 1)
            act.wait_ge(dt_step, 1)
            act.activation(w[1][:, :], w[0][:, :], ACT.Exp).then_inc(dt_exp, 1)
            act.wait_ge(dt_step, 16)
            act.activation(dec[:, :, :].rearrange("p g t -> p (g t)"), w[4][:, :], ACT.Exp, scale=-1.0)\
               .then_inc(dt_exp, 1)
            act.wait_ge(dt_exp, 2)
            act.wait_ge(cleared, 2)

            def copy_sums(g, i):
                act.wait_ge(y_done, i * NS + (g + 5))
                act.wait_ge(y_turned, i * 2 + (g // 2 + 1))
                act.activation(ysb[:, g, :], psY[g], ACT.Copy).then_inc(ysb_kept, 1)

            def copy_turned(h, i):
                act.wait_ge(y_turned, i * 2 + (h + 3))
                act.wait_ge(gated, i * 4 + (2 * h + 2))
                act.activation(yb[:, 2 * h:2 * h + 2, :, :, :].rearrange("p g k t b -> p (g k t b)"), psT,
                               ACT.Copy).then_inc(yb_kept, 1)

            with act.Fori(0, TB) as i:
                def scalars(half, i=i):
                    act.activation(decb[:, :, 4 * half:4 * half + 4], dec[:, :, bass.ds(i * 8 + 4 * half, 4)], ACT.Copy)
                    act.activation(Bbb[:, :, 4 * half:4 * half + 4], Bb[:, :, bass.ds(i * 8 + 4 * half, 4)],
                                   ACT.Copy).then_inc(scal_a, 1)

                scalars(0)
                for k in range(NS):
                    t, g = divmod(k, NG)
                    if k % 16 == 0:
                        act.wait_ge(scal_a, i * 2 + (k // 16 + 1))
                    act.wait_ge(clipped, i * NS + (k + 1))
                    act.activation(h1[g][:, :], hs[g][(t + 1) % 2][:, :], ACT.Copy,
                                   scale=decb[:, g, t:t + 1]).then_inc(h1_done, 1)
                    if k < 4:
                        copy_sums(k, i)
                    elif k in (6, 10):
                        copy_turned((k - 6) // 4, i)
                    elif k == 12:
                        scalars(1)
            for g in range(NG):
                copy_sums(g, TB)
                if g % 2:
                    copy_turned(g // 2, TB)

        @block.gpsimd
        def _(pool):
            pool.sem_inc(gated, 8)
            pool.memset(LC[:, :, :], 0.0).then_inc(cleared, 1)
            for g in range(NG):
                pool.memset(hs[g][1][:, :], 0.0).then_inc(clipped, 1)
            with pool.Fori(0, TB) as i:
                for g in range(NG):
                    def span(v, g=g, i=i):
                        return v[:, :, g * GT:(g + 1) * GT].rearrange("p k (b t) -> p k b t", b=GB)[:, :, :, bass.ds(i * 8, 8)]
                    z = span(zs)
                    pool.wait_ge(yb_kept, i * 2 + (g // 2 + 4))
                    pool.tensor_tensor(z, z, yb[:, g, :, :, :].rearrange("p k t b -> p k b t"), ALU.mult)\
                        .then_inc(gated, 1)
                for g in range(NG):
                    z, x = (v[:, :, g * GT:(g + 1) * GT].rearrange("p k (b t) -> p k b t", b=GB)[:, :, :, bass.ds(i * 8, 8)]
                            for v in (zs, xD))
                    pool.wait_ge(gated, i * 4 + (g + 9))
                    pool.tensor_tensor(z, z, x, ALU.add).then_inc(y_ready, 1)

        @block.tensor
        def _(pe):
            pe.sem_inc(y_done, 8)
            pe.sem_inc(y_turned, 2)
            pe.wait_ge(sel_in, 32)
            pe.wait_ge(cleared, 2)

            def turn_sums(h, i):
                pe.wait_ge(ysb_kept, i * 4 + (2 * h + 2))
                pe.wait_ge(yb_kept, i * 2 + (h + 1))
                pe.nop(nofuse=True)
                for g in range(2):
                    for n in range(KD):
                        ins = pe.transpose(psT[:, (g * KD + n) * BT:(g * KD + n + 1) * BT],
                                           ysb[:, 2 * h + g, n * P:(n + 1) * P], ident[0:BT, 0:BT])
                ins.then_inc(y_turned, 1)

            with pe.Fori(0, TB) as i:
                def sums(k, i=i):
                    t, g = divmod(k, NG)
                    if k % 16 == 0:
                        pe.wait_ge(lc_done, i * 2 + (k // 16 + 1))
                    if t == 0:
                        pe.wait_ge(ysb_kept, i * 4 + (g + 1))
                    pe.wait_ge(clipped, i * NS + (k + 1 + 4))
                    pe.matmul(psY[g], LC[:, g, t * BT:(t + 1) * BT], hs[g][t % 2][:, :],
                              start=(t == 0), stop=(t == 7)).then_inc(y_done, 1)

                for k in range(NS):
                    pe.wait_ge(h2_done, i * NS + ((3, 4, 4)[k] if k < 3 else k + 2))
                    t, g = divmod(k, NG)
                    pe.matmul(psU[k % 3], sel[:, t, :], Xtm[:, bass.ds(i + g * TB, 1), :].rearrange("p a c -> p (a c)"),
                              start=True, stop=True).then_inc(u_done, 1)
                    if k >= 4:
                        sums(k - 4)
                    if k in (6, 10):
                        turn_sums((k - 6) // 4, i)
                for k in range(NS - 4, NS):
                    sums(k)
            for h in range(2):
                turn_sums(h, TB)
            pe.wait_ge(y_ready, 4 * TB)
            pe.wait_ge(wout_in, 16)
            for p in range(NPAIR):
                if p >= 2:
                    pe.wait_ge(x2_added, p - 1)
                for k in range(KD):
                    ins = pe.matmul(psW[p % 2], zs[:, k, p * PAIR_TOK:(p + 1) * PAIR_TOK], Wout[:, k, :],
                                    start=(k == 0), stop=(k == KD - 1))
                ins.then_inc(out_done, 1)


def experts(nc, a, out, sem, tensor_in, psum, X, ident, nhalf, xT):
    with ExitStack() as ctx:
        sb = tensor_in(ctx)
        CH = 256
        NCH = B * T // CH
        NB = CH // T
        NPIECE = E + FT
        PW = 2 * DFF
        Whi = sb("Whi", [P, NPIECE, PW], F16)
        Wlo = sb("Wlo", [P, NPIECE, PW], F16)
        gW2 = sb("gW2", [P, 2, E])
        gb1 = sb("gb1", [P, 2])
        gb2b = sb("gb2b", [P, E])
        gb2c = sb("gb2c", [E, 1])
        hs = sb("hs", [P, 2, T])
        hsd = sb("hsd", [P, 2, 2, T])
        G = sb("G", [P, E, T])
        Gt = sb("Gt", [P, E])
        B1 = sb("B1", [P, FT, T])
    
        w_small = sem("ff_w_small")
        piece_in = [sem(f"piece_in{n}") for n in range(3)]
        piece_hi = sem("piece_hi")
        piece_lo = [sem(f"piece_lo{n}") for n in range(3)]
        gw_wide = sem("gw_wide")
        gate_used = sem("gate_used")
        gate_h = sem("gate_h")
        gate_relu = sem("gate_relu")
        g_step = sem("g_step")
        g_mm = sem("g_mm")
        g_kept = sem("g_kept")

        with ExitStack() as cs:
            sbs = tensor_in(cs)
            stage = [sbs(f"wstage{n}", [P, PW]) for n in range(3)]
            gW1 = sbs("gW1", [P, 2, C])
            eb1 = sbs("eb1", [E, DFF])
            eb2 = sbs("eb2", [E, C])
            G8 = sbs("G8", [E, PAIR_TOK])
            LATE = NPIECE - 4
            xn = Whi[:, LATE:, :].bitcast(F32).rearrange("p a n -> p (a n)").rearrange("p (n c) -> p n c", c=C)
            Hr = Wlo[:, LATE:LATE + 2, :].bitcast(F32).rearrange("p a n -> p (a n)").rearrange("p (n c) -> p n c", c=512)
            gW2w = Wlo[:, LATE + 2:, :].bitcast(F32).rearrange("p a n -> p (a n)").rearrange("p (m e q) -> p m e q", m=2, e=E)
            ln = LayerNorm(nc, cs, "ln3", X, ident, psum, xT, nhalf, xn)
            POOL_CUTS = (4, 8, 13)

            def low(engine, n):
                if n == 13:
                    engine.wait_ge(gate_used, 1)
                engine.wait_ge(piece_hi, n + 1)
                engine.tensor_tensor(Wlo[:, n, :], stage[n % 3][:, :], Whi[:, n, :], ALU.subtract)\
                      .then_inc(piece_lo[n % 3], 1)

            block = cs.enter_context(nc.Block())

            @block.sync
            def _(sp):
                for n in range(3):
                    sp.sem_inc(piece_lo[n], 1)
                sp.dma_start(gW1[:, :, :], a["gW1T"].rearrange("(k p) n -> p k n", p=P)).then_inc(w_small, 16)
                with nc.allow_non_contiguous_dma(reason="small parameters"):
                    sp.dma_start(gW2[:, :, :], a["gW2T"].rearrange("(k p) n -> p k n", p=P)).then_inc(w_small, 16)
                    sp.dma_start(gb1[:, :], a["gb1"].rearrange("(k p) -> p k", p=P)).then_inc(w_small, 16)
                    sp.dma_start(gb2c[:, :], a["gb2"].rearrange("(e o) -> e o", o=1)).then_inc(w_small, 16)
                sp.dma_start(gb2b[:, :], a["gb2"].partition_broadcast(P)).then_inc(w_small, 16)
                sp.dma_start(eb1[:, :], a["eb1"]).then_inc(w_small, 16)
                sp.dma_start(eb2[:, :], a["eb2"]).then_inc(w_small, 16)
                with sp.Fori(0, LATE // 3) as i:
                    for u in range(3):
                        sp.wait_ge(piece_lo[u], i + 1)
                        sp.dma_start(stage[u][:, :], a["WF"][bass.ds(i * 3 + u, 1)].rearrange("a p n -> (a p) n"))\
                            .then_inc(piece_in[u], 16)
                for n in range(LATE, NPIECE):
                    sp.wait_ge(piece_lo[n % 3], n // 3 + 1)
                    sp.dma_start(stage[n % 3][:, :], a["WF"][n]).then_inc(piece_in[n % 3], 16)

            @block.gpsimd
            def _(pool):
                ln.gpsimd(pool)
                pool.wait_ge(ln.kept, 1)
                pool.tensor_copy(xT[:, :, B * T:], xT[:, :, 0:2 * PAIR_TOK]).then_inc(ln.wrapped, 1)
                pool.wait_ge(w_small, 112)
                pool.tensor_copy(gW2w[:, :, :, :], gW2[:, :, :][:, :, :, None].to_broadcast([P, 2, E, P]))\
                    .then_inc(gw_wide, 1)
                for n in POOL_CUTS:
                    low(pool, n)

            @block.scalar
            def _(act):
                def high(n):
                    act.wait_ge(piece_in[n % 3], 16 * (n // 3 + 1))
                    act.activation(Whi[:, n, :], stage[n % 3][:, :], ACT.Copy).then_inc(piece_hi, 1)

                def relu(n):
                    m, c = divmod(n, 4)
                    act.wait_ge(gate_h, n + 1)
                    if n == 4:
                        act.wait_ge(g_step, 1)
                    act.activation(Hr[:, c, :], bank(psum, n % 2), ACT.Relu, bias=gb1[:, m:m + 1])\
                        .then_inc(gate_relu, 1)

                for n in range(3):
                    high(n)
                ln.scalar(act)
                act.wait_ge(w_small, 112)
                for n in range(4):
                    relu(n)
                for n in range(3, 6):
                    high(n)
                for n in range(4, 8):
                    relu(n)
                for n in range(6, NPIECE):
                    if n == LATE:
                        act.wait_ge(ln.turned, NPAIR // 2)
                    high(n)

            @block.vector
            def _(dve):
                ln.vector(dve)
                for n in range(3):
                    low(dve, n)
                dve.wait_ge(w_small, 112)
                for m in range(2):
                    dve.wait_ge(gate_relu, 4 * m + 4)
                    dve.tensor_reduce(hs[:, m, :], Hr[:, :, :].rearrange("p c (b t) -> p t (c b)", t=T), AX_X,
                                      ALU.add).then_inc(g_step, 1)
                    if m == 0:
                        for n in range(3, 6):
                            if n not in POOL_CUTS:
                                low(dve, n)
                dve.wait_ge(g_step, 2)
                dve.tensor_scalar(hsd[:, :, :, :].rearrange("p m d t -> p m d t"),
                                  hs[:, :, :][:, :, None, :].to_broadcast([P, 2, 2, T]), 1.0 / B, None,
                                  ALU.mult).then_inc(g_step, 1)
                for n in range(6, LATE - 2):
                    if n not in POOL_CUTS:
                        low(dve, n)
                dve.wait_ge(g_mm, 1)
                dve.tensor_tensor(G[:, :, :], bank(psum, 2).rearrange("p (e t) -> p e t", e=E),
                                  gb2b[:, :][:, :, None].to_broadcast([P, E, T]), ALU.add).then_inc(g_kept, 1)
                dve.wait_ge(g_mm, 2)
                dve.tensor_tensor(Gt[:, :], bank(psum, 3, E), gb2b[:, :], ALU.add).then_inc(g_kept, 1)
                dve.wait_ge(g_mm, 3)
                dve.tensor_scalar(G8[:, :], psum[0:E, 4 * 512:4 * 512 + PAIR_TOK], gb2c[:, :], None,
                                  ALU.add).then_inc(g_kept, 1)
                dve.sem_inc(gate_used, 1)
                low(dve, LATE - 2)
                dve.wait_ge(g_mm, 4)
                dve.tensor_copy(B1[:, :, :], bank(psum, 5).rearrange("p (f t) -> p f t", f=FT)).then_inc(g_kept, 1)
                dve.wait_ge(g_mm, 5)
                dve.tensor_tensor(X[:, :, :], X[:, :, :], bank(psum, 6, C)[:, None, :].to_broadcast([P, NPAIR, C]), ALU.add)
                for n in range(LATE - 1, NPIECE):
                    if n not in POOL_CUTS:
                        low(dve, n)

            @block.tensor
            def _(pe):
                ln.tensor(pe)
                pe.wait_ge(ln.kept, NPAIR // 2)
                pe.wait_ge(w_small, 112)
                for n in range(8):
                    m, c = divmod(n, 4)
                    if n >= 2:
                        pe.wait_ge(gate_relu, n - 1)
                    for k in range(2):
                        ins = pe.matmul(bank(psum, n % 2), gW1[:, k, m * P:(m + 1) * P], xT[:, k, c * 512:(c + 1) * 512],
                                        start=(k == 0), stop=(k == 1))
                    ins.then_inc(gate_h, 1)
                pe.wait_ge(g_step, 3)
                pe.wait_ge(gw_wide, 1)
                for e in range(E):
                    for m in range(2):
                        ins = pe.matmul(bank(psum, 2)[:, e * T:(e + 1) * T], gW2w[:, m, e, :], hsd[:, m, 0, :],
                                        start=(m == 0), stop=(m == 1))
                ins.then_inc(g_mm, 1)
                for m in range(2):
                    ins = pe.matmul(bank(psum, 3, E), hsd[:, m, :, :].rearrange("p d t -> p (d t)"), gW2[:, m, :],
                                    start=(m == 0), stop=(m == 1))
                ins.then_inc(g_mm, 1)
                for m in range(2):
                    ins = pe.matmul(psum[0:E, 4 * 512:4 * 512 + PAIR_TOK], gW2[:, m, :],
                                    hsd[:, m, :, :].rearrange("p d t -> p (d t)"), start=(m == 0), stop=(m == 1))
                ins.then_inc(g_mm, 1)
                pe.wait_ge(g_kept, 3)
                for f in range(FT):
                    ins = pe.matmul(bank(psum, 5)[:, f * T:(f + 1) * T], eb1[:, f * P:(f + 1) * P], G8[:, 0:T],
                                    start=True, stop=True)
                ins.then_inc(g_mm, 1)
                pe.matmul(bank(psum, 6, C), G8[:, :], eb2[:, :], start=True, stop=True).then_inc(g_mm, 1)

        Xg = sb("Xg", [P, E, CH])
        Xhi = sb("Xhi", [P, 2, E, CH], F16)
        Xlo = sb("Xlo", [P, 2, E, CH], F16)
        pre = [sb(f"pre{n}", [P, CH]) for n in range(2)]
        Hhi = sb("Hhi", [P, FT, CH], F16)
        Hlo = sb("Hlo", [P, FT, CH], F16)
        acc = [sb(f"acc{n}", [P, 2, C]) for n in range(2)]

        x_gated = sem("x_gated")
        x_hi = sem("x_hi")
        x_lo = sem("x_lo")
        h_done = sem("h_done")
        h_pre = sem("h_pre")
        h_hi = sem("h_hi")
        h_lo = sem("h_lo")
        u_done = sem("u_done")
        mixed = sem("mixed")
        stored = sem("stored")
        block = ctx.enter_context(nc.Block())
        UA = 8

        @block.tensor
        def _(pe):
            with pe.Fori(0, NCH) as i:
                for f in range(FT):
                    pe.wait_ge(h_pre, i * 8 + (f - 1) + 2)
                    ps = bank(psum, f % 2, CH)
                    n = 0
                    for k in range(2):
                        if f == 0:
                            pe.wait_ge(x_lo, i * 2 + (k + 1))
                        for e in range(E):
                            cols = slice(k * DFF + f * P, k * DFF + (f + 1) * P)
                            for w, x in ((Whi, Xhi), (Whi, Xlo), (Wlo, Xhi)):
                                ins = pe.matmul(ps, w[:, e, cols], x[:, k, e, :], start=(n == 0), stop=(n == 6 * E - 1))
                                n += 1
                    ins.then_inc(h_done, 1)
                for tt in range(2):
                    tok = slice(tt * P, (tt + 1) * P)
                    for ep in range(4):
                        pe.wait_ge(mixed, i * 16 + (8 * tt + 2 * ep + 2))
                        n = 0
                        for f in range(FT):
                            if tt == 0 and ep == 0:
                                pe.wait_ge(h_lo, i * 8 + (f + 1))
                            cols = slice(ep * 512, (ep + 1) * 512)
                            for h, w in ((Hhi, Whi), (Hhi, Wlo), (Hlo, Whi)):
                                ins = pe.matmul(bank(psum, 2 + ep), h[:, f, tok], w[:, E + f, cols],
                                                start=(n == 0), stop=(n == 3 * FT - 1))
                                n += 1
                        ins.then_inc(u_done, 1)

        @block.scalar
        def _(act):
            def split(v):
                for k in range(2):
                    act.wait_ge(x_gated, v(k + 1))
                    act.activation(Xhi[:, k, :, :], Xg[:, :, :], ACT.Copy).then_inc(x_hi, 1)

            split(lambda n: n)
            with act.Fori(0, NCH) as i:
                for f in range(FT):
                    act.wait_ge(h_pre, i * 8 + (f + 1) + 2)
                    act.activation(Hhi[:, f, :], pre[f % 2][:, :], ACT.Relu).then_inc(h_hi, 1)
                split(lambda n: i * 2 + (n + 2))

        @block.vector
        def _(dve):
            def gate_input(step, v):
                for k in range(2):
                    if isinstance(step, int):
                        src = xT[:, k, step * CH:(step + 1) * CH]
                    else:
                        src = xT[:, k, bass.ds(step * CH, CH)]
                    for q in range(NB):
                        ins = dve.tensor_tensor(Xg[:, :, q * T:(q + 1) * T], G[:, :, :],
                                                (xT[:, k, step * CH + q * T:step * CH + (q + 1) * T] if isinstance(step, int)
                                                 else xT[:, k, bass.ds(step * CH + q * T, T)])
                                                [:, None, :].to_broadcast([P, E, T]), ALU.mult)
                    ins.then_inc(x_gated, 1)
                    dve.wait_ge(x_hi, v(k + 1))
                    dve.tensor_tensor(Xlo[:, k, :, :], Xg[:, :, :], Xhi[:, k, :, :], ALU.subtract).then_inc(x_lo, 1)
                    dve.wait_ge(x_lo, v(k + 1))

            dve.sem_inc(h_pre, 2)
            dve.sem_inc(mixed, UA)
            gate_input(0, lambda n: n)
            with dve.Fori(0, NCH) as i:
                for f in range(FT):
                    dve.wait_ge(h_done, i * 8 + (f + 1))
                    dve.tensor_tensor(pre[f % 2][:, :].rearrange("p (b t) -> p b t", t=T),
                                      bank(psum, f % 2, CH).rearrange("p (b t) -> p b t", t=T),
                                      B1[:, f, :][:, None, :].to_broadcast([P, NB, T]), ALU.add).then_inc(h_pre, 1)
                    dve.wait_ge(h_hi, i * 8 + (f + 1))
                    dve.scalar_tensor_tensor(Hlo[:, f, :], pre[f % 2][:, :], 0.0, Hhi[:, f, :], ALU.max,
                                             ALU.subtract).then_inc(h_lo, 1)
                    dve.wait_ge(h_lo, i * 8 + (f + 1))
                gate_input(i + 1, lambda n: i * 2 + (n + 2))
                for tt in range(2):
                    for e in range(E):
                        if e % 2 == 0:
                            dve.wait_ge(u_done, i * 8 + (4 * tt + e // 2 + 1))
                        ps = bank(psum, 2 + e // 2)[:, (e % 2) * C:(e % 2 + 1) * C]
                        src = (X[:, bass.ds(i * 2 + tt, 1), :].rearrange("p a c -> p (a c)") if e == 0
                               else acc[(e - 1) % 2][:, tt, :])
                        if e == 0:
                            dve.wait_ge(stored, i * 16 + 16)
                        else:
                            dve.wait_ge(mixed, i * 16 + (8 * tt + e) + UA)
                        dve.scalar_tensor_tensor(acc[e % 2][:, tt, :], ps, Gt[:, e:e + 1], src, ALU.mult,
                                                 ALU.add).then_inc(mixed, 1)

        @block.sync
        def _(sp):
            sp.sem_inc(stored, 16)
            with sp.Fori(0, NCH) as i:
                sp.wait_ge(mixed, i * 16 + 16 + UA)
                sp.dma_start(out[bass.ds(i * CH, CH), :].rearrange("(n p) c -> p n c", p=P),
                             acc[(E - 1) % 2][:, :, :]).then_inc(stored, 16)
            sp.wait_ge(stored, 16 * (NCH + 1))


def kernel(**inputs):
    import concourse.bacc as bacc
    from concourse.bass_utils import run_bass_kernel_spmd

    given = {k.removeprefix("L0_"): np.asarray(v) for k, v in inputs.items()}
    Wkv, ctx = given["xattn_Wkv"], given["ctx_768"]
    HD = H * DK
    wk, wv = (w.T.reshape(HP, 2, DK, CTX) for w in (Wkv[:, :HD], Wkv[:, HD:]))
    WkS = np.zeros((2, DK, HP, 2, 2 * P), np.float32)
    WvS = np.zeros((2, DK, HP, 3, P), np.float32)
    for h2 in range(2):
        k, v = wk[:, h2].transpose(1, 0, 2), wv[:, h2].transpose(1, 0, 2)
        WkS[h2, :, :, h2, :CTX] = k
        WkS[h2, :, :, h2, CTX:] = k[:, :, P:]
        WvS[h2, :, :, h2] = v[:, :, :P]
        WvS[h2, :, :, 2, h2 * C1:(h2 + 1) * C1] = v[:, :, P:]
    WxT, side = given["attn_W_xproj"].T, P - DS
    Wx = np.concatenate([WxT[:, :2 * DS], np.repeat(WxT[:, 2 * DS:], P - 2 * DS, axis=1)], axis=1)
    spread = np.zeros((P, 3, P + side), np.float32)
    for q in range(3):
        spread[q * DS:(q + 1) * DS, q, side:P] = np.eye(DS, dtype=np.float32)
    eye = np.eye(8, dtype=np.float16)
    sel = np.broadcast_to(eye[:, None, :, None, None] * eye[None, :, None, :, None], (2, 8, 8, 8, 8, DS))
    sel = sel.reshape(P, 8, P)
    w1 = given["ffn_eW1"].reshape(E, DFF, 2, P).transpose(0, 3, 2, 1)
    w2 = given["ffn_eW2"].reshape(E, C, FT, P).transpose(2, 3, 0, 1)
    arrays = {
        "x": given["x"].reshape(B * T, C),
        "ident": np.eye(P, dtype=np.float32),
        "ctxT": ctx.transpose(0, 2, 1),
        "ctxN": ctx[:, :JT * P].reshape(B, JT, P, CTX).transpose(0, 2, 1, 3),
        "ctxR": ctx[:, JT * P:],
        "Wq": given["xattn_Wq"], "WkS": WkS.reshape(P, HP, 2, 2 * P), "WvS": WvS.reshape(P, HP, 3, P),
        "Wproj": given["xattn_Wproj"], "bproj": given["xattn_bproj"],
        "WinT": given["attn_W_in"].T, "convw": given["attn_conv_w"], "convb": given["attn_conv_b"],
        "Wx": Wx, "spread": spread, "A_log8": np.tile(given["attn_A_log"], P // DS).reshape(P, 1), "Dp": given["attn_D_param"],
        "sel": sel, "m8": np.repeat(np.eye(P // DS, dtype=np.float32), DS, axis=0),
        "ident16": np.eye(P, dtype=np.float16),
        "WoutT": given["attn_W_out"].T,
        "gW1T": given["ffn_gW1"].T, "gb1": given["ffn_gb1"], "gW2T": given["ffn_gW2"].T, "gb2": given["ffn_gb2"],
        "eb1": given["ffn_eb1"], "eb2": given["ffn_eb2"],
        "WF": np.concatenate([w1.reshape(E, P, 2 * DFF), w2.reshape(FT, P, E * C)]),
    }
    arrays = {f"in_{k}": np.ascontiguousarray(v) for k, v in arrays.items()}
    nc = bacc.Bacc("TRN2", target_bir_lowering=False, num_devices=1)
    a = {k.removeprefix("in_"): nc.dram_tensor(k, v.shape, mybir.dt.from_np(v.dtype), kind="ExternalInput").ap() for k, v in arrays.items()}
    out = nc.dram_tensor("out_0", (B * T, C), F32, kind="ExternalOutput").ap()
    build(nc, a, out)
    r = run_bass_kernel_spmd(nc, [arrays], core_ids=[0])
    return r.results[0]["out_0"].reshape(B, T, C)
```
